# Optimizing a Trainium2 kernel written in Bass

```python
import numpy as np
import jax
import jax.numpy as jnp

def _softmax(x, axis=-1):
    return jax.nn.softmax(x, axis=axis)

def _gelu(x):
    return jax.nn.gelu(x, approximate=True)

def _silu(x):
    return jax.nn.silu(x)

def _sigmoid(x):
    return jax.nn.sigmoid(x)

def _layernorm(x, axis=-1, eps=1e-05):
    m = jnp.mean(x, axis=axis, keepdims=True)
    v = jnp.var(x, axis=axis, keepdims=True)
    return (x - m) / jnp.sqrt(v + eps)

def _scatter_add(tgt, idx, src, axis=0):
    return tgt.at[idx].add(src)

def _segment_sum(src, seg, n):
    return jax.ops.segment_sum(src, seg, n)
kernel_name = 'mk_gps_d2_gnn_r32_6c6fb8'

def setup_inputs(seed: int=0):
    np.random.seed(seed)
    _w = jnp.asarray

    def _rec_inputs():
        import jax
        import jax.numpy as jnp
        _gk = jax.random.key(seed)
        x = -0.0003713 + 1 * jax.random.normal(jax.random.fold_in(_gk, 1), (3125, 256), jnp.float32)
        src = jax.random.randint(jax.random.fold_in(_gk, 2), (50000,), 0, 3125, jnp.int32)
        dst = jax.random.randint(jax.random.fold_in(_gk, 3), (50000,), 0, 3125, jnp.int32)
        _o = jnp.argsort(dst, stable=True)
        src = src[_o]
        dst = dst[_o]
        return (x, src, dst)
    x, src, dst = _rec_inputs()

    def _L0_gnn_setup():
        import jax, jax.numpy as jnp
        import numpy as np
        import math
        N_NODES = 50000
        N_EDGES = 50000
        C = 256
        H = 8
        HD = C // H

        def _layernorm(x, g, b, eps=1e-05):
            mu = jnp.mean(x, axis=-1, keepdims=True)
            var = jnp.mean(jnp.square(x - mu), axis=-1, keepdims=True)
            return (x - mu) * jax.lax.rsqrt(var + eps) * g + b
        key = jax.random.key(seed)
        ks = jax.random.split(key, 16)
        s = 0.02
        d = {'feat': jax.random.normal(ks[0], (N_NODES, C), jnp.float32), 'edge_src': jax.random.randint(ks[1], (N_EDGES,), 0, N_NODES), 'edge_dst': jax.random.randint(ks[2], (N_EDGES,), 0, N_NODES), 'Wq': jax.random.normal(ks[3], (C, C), jnp.float32) * s, 'bq': jnp.zeros((C,), jnp.float32), 'Wk': jax.random.normal(ks[4], (C, C), jnp.float32) * s, 'bk': jnp.zeros((C,), jnp.float32), 'Wv': jax.random.normal(ks[5], (C, C), jnp.float32) * s, 'bv': jnp.zeros((C,), jnp.float32), 'Wp': jax.random.normal(ks[6], (C, C), jnp.float32) * s, 'bp': jnp.zeros((C,), jnp.float32), 'ln_g': jnp.ones((C,), jnp.float32), 'ln_b': jnp.zeros((C,), jnp.float32), 'W1': jax.random.normal(ks[7], (4 * C, C), jnp.float32) * s, 'b1': jnp.zeros((4 * C,), jnp.float32), 'W2': jax.random.normal(ks[8], (C, 4 * C), jnp.float32) * s, 'b2': jnp.zeros((C,), jnp.float32)}
        return d
    _L0_gnn_all = _L0_gnn_setup()
    _L0_gnn_in = {k: v for k, v in _L0_gnn_all.items() if k in ('Wq', 'bq', 'Wk', 'bk', 'Wv', 'bv', 'Wp', 'bp', 'ln_g', 'ln_b', 'W1', 'b1', 'W2', 'b2')}
    del _L0_gnn_all

    def _L0_mix_setup():
        import jax, jax.numpy as jnp
        import numpy as np
        A, Bc, Cc = (0.5, 1.0, 1.0)
        H = 8
        EPS = 1e-12

        def _normalize(t):
            n = jnp.linalg.norm(t, axis=-1, keepdims=True)
            return t / jnp.maximum(n, EPS)
        key = jax.random.key(seed)
        ks = jax.random.split(key, 5)
        B, N, C = (8, 64, 256)
        D = C // H
        x = jax.random.normal(ks[0], (B, N, C), dtype=jnp.float32)
        Wqkv = jax.random.normal(ks[1], (3 * H * D, C), dtype=jnp.float32) * 0.02
        bqkv = jnp.zeros((3 * H * D,), dtype=jnp.float32)
        Wproj = jax.random.normal(ks[2], (C, H * D), dtype=jnp.float32) * 0.02
        bproj = jnp.zeros((C,), dtype=jnp.float32)
        temperature = jnp.ones((1, H, 1, 1), dtype=jnp.float32)
        return {'x': x, 'Wqkv': Wqkv, 'bqkv': bqkv, 'Wproj': Wproj, 'bproj': bproj, 'temperature': temperature}
    _L0_mix_all = _L0_mix_setup()
    _L0_mix_in = {k: v for k, v in _L0_mix_all.items() if k in ('Wqkv', 'bqkv', 'Wproj', 'bproj', 'temperature')}
    del _L0_mix_all

    def _L0_ffn_setup():
        import jax, jax.numpy as jnp
        import numpy as np
        BN_EPS = 0.001

        def _bn(h, g, b, m, v):
            return g * (h - m) * jax.lax.rsqrt(v + BN_EPS) + b
        key = jax.random.key(seed)
        ks = jax.random.split(key, 8)
        B, F, Df = (256, 64, 256)
        E, H, D = (8, 256, 256)
        s1 = 1.0 / np.sqrt(Df)
        s2 = 1.0 / np.sqrt(H)
        return {'x': jax.random.normal(ks[0], (B, F, Df), jnp.float32), 'Wr': jax.random.normal(ks[1], (Df, E), jnp.float32) * s1, 'br': jnp.zeros((E,), jnp.float32), 'W1': jax.random.normal(ks[2], (E, Df, H), jnp.float32) * s1, 'b1': jnp.zeros((E, H), jnp.float32), 'g1': jnp.ones((E, H), jnp.float32), 'be1': jnp.zeros((E, H), jnp.float32), 'm1': jnp.zeros((E, H), jnp.float32), 'v1': jnp.ones((E, H), jnp.float32), 'W2': jax.random.normal(ks[3], (E, H, H), jnp.float32) * s2, 'b2': jnp.zeros((E, H), jnp.float32), 'g2': jnp.ones((E, H), jnp.float32), 'be2': jnp.zeros((E, H), jnp.float32), 'm2': jnp.zeros((E, H), jnp.float32), 'v2': jnp.ones((E, H), jnp.float32), 'Wo': jax.random.normal(ks[4], (E, H, D), jnp.float32) * s2, 'bo': jnp.zeros((E, D), jnp.float32)}
    _L0_ffn_all = _L0_ffn_setup()
    _L0_ffn_in = {k: v for k, v in _L0_ffn_all.items() if k in ('Wr', 'br', 'W1', 'b1', 'g1', 'be1', 'm1', 'v1', 'W2', 'b2', 'g2', 'be2', 'm2', 'v2', 'Wo', 'bo')}
    del _L0_ffn_all

    def _L1_gnn_setup():
        import jax, jax.numpy as jnp
        import numpy as np
        N = 50000
        E_RAND = 25000
        IN_DIM = 256
        HID = 64
        HEADS = 4
        OUT_DIM = 256
        NEG_SLOPE = 0.01

        def _xavier(key, shape, fan_in, fan_out):
            gain = np.sqrt(2.0)
            std = gain * np.sqrt(2.0 / (fan_in + fan_out))
            return jax.random.normal(key, shape, dtype=jnp.float32) * std

        def _leaky(x):
            return jnp.where(x > 0, x, NEG_SLOPE * x)

        def _segment_softmax(e, dst, n):
            m = jax.ops.segment_max(e, dst, num_segments=n)
            m = jnp.where(jnp.isfinite(m), m, 0.0)
            ex = jnp.exp(e - m[dst])
            s = jax.ops.segment_sum(ex, dst, num_segments=n)
            return ex / s[dst]
        key = jax.random.key(seed)
        k = jax.random.split(key, 8)
        h = jax.random.normal(k[0], (N, IN_DIM), dtype=jnp.float32)
        src = jnp.concatenate([jax.random.randint(k[1], (E_RAND,), 0, N), jnp.arange(N)]).astype(jnp.int32)
        dst = jnp.concatenate([jax.random.randint(k[2], (E_RAND,), 0, N), jnp.arange(N)]).astype(jnp.int32)
        W1 = _xavier(k[3], (HEADS, HID, IN_DIM), IN_DIM, HID)
        a1 = _xavier(k[4], (HEADS, 2 * HID), 2 * HID, 1)
        W2 = _xavier(k[5], (OUT_DIM, HID * HEADS), HID * HEADS, OUT_DIM)
        a2 = _xavier(k[6], (2 * OUT_DIM,), 2 * OUT_DIM, 1)
        return {'h': h, 'W1': W1, 'a1': a1, 'W2': W2, 'a2': a2, 'src': src, 'dst': dst}
    _L1_gnn_all = _L1_gnn_setup()
    _L1_gnn_in = {k: v for k, v in _L1_gnn_all.items() if k in ('W1', 'a1', 'W2', 'a2')}
    del _L1_gnn_all

    def _L1_mix_setup():
        import jax, jax.numpy as jnp
        import numpy as np
        HEADS = 8
        DIM_HEAD = 64
        EPS = 1e-05

        def _inst_norm(t):
            mu = jnp.mean(t, axis=-1, keepdims=True)
            var = jnp.var(t, axis=-1, keepdims=True)
            return (t - mu) / jnp.sqrt(var + EPS)
        key = jax.random.key(seed)
        k1, k2, k3, k4 = jax.random.split(key, 4)
        b, n, dim = (4, 256, 256)
        inner = HEADS * DIM_HEAD
        x = jax.random.normal(k1, (b, n, dim), dtype=jnp.float32)
        w_qkv = jax.random.normal(k2, (dim, 3 * inner), dtype=jnp.float32) * (1.0 / DIM_HEAD)
        w_out = jax.random.normal(k3, (inner, dim), dtype=jnp.float32) * dim ** (-0.5)
        b_out = jax.random.normal(k4, (dim,), dtype=jnp.float32) * 0.01
        return {'x': x, 'w_qkv': w_qkv, 'w_out': w_out, 'b_out': b_out}
    _L1_mix_all = _L1_mix_setup()
    _L1_mix_in = {k: v for k, v in _L1_mix_all.items() if k in ('w_qkv', 'w_out', 'b_out')}
    del _L1_mix_all

    def _L1_ffn_setup():
        import jax, jax.numpy as jnp
        import numpy as np
        E = 8
        K = 2
        D = 256
        H = 512
        DOUT = 256
        EPS = 1e-05
        key = jax.random.key(seed)
        ks = jax.random.split(key, 9)
        s = 0.02
        return {'x': jax.random.normal(ks[0], (4, 256, D), jnp.float32), 'gamma': 1.0 + 0.05 * jax.random.normal(ks[1], (D,), jnp.float32), 'beta': 0.05 * jax.random.normal(ks[2], (D,), jnp.float32), 'Wr': 0.01 * jax.random.normal(ks[3], (D, E), jnp.float32), 'br': jnp.zeros((E,), jnp.float32), 'W1': s * jax.random.normal(ks[4], (E, D, H), jnp.float32), 'b1': s * jax.random.normal(ks[5], (E, H), jnp.float32), 'W2': s * jax.random.normal(ks[6], (E, H, DOUT), jnp.float32), 'b2': s * jax.random.normal(ks[7], (E, DOUT), jnp.float32)}
    _L1_ffn_all = _L1_ffn_setup()
    _L1_ffn_in = {k: v for k, v in _L1_ffn_all.items() if k in ('gamma', 'beta', 'Wr', 'br', 'W1', 'b1', 'W2', 'b2')}
    del _L1_ffn_all
    return {'x': x, 'src': src, 'dst': dst, 'L0_gnn_Wq': _L0_gnn_in['Wq'], 'L0_gnn_bq': _L0_gnn_in['bq'], 'L0_gnn_Wk': _L0_gnn_in['Wk'], 'L0_gnn_bk': _L0_gnn_in['bk'], 'L0_gnn_Wv': _L0_gnn_in['Wv'], 'L0_gnn_bv': _L0_gnn_in['bv'], 'L0_gnn_Wp': _L0_gnn_in['Wp'], 'L0_gnn_bp': _L0_gnn_in['bp'], 'L0_gnn_ln_g': _L0_gnn_in['ln_g'], 'L0_gnn_ln_b': _L0_gnn_in['ln_b'], 'L0_gnn_W1': _L0_gnn_in['W1'], 'L0_gnn_b1': _L0_gnn_in['b1'], 'L0_gnn_W2': _L0_gnn_in['W2'], 'L0_gnn_b2': _L0_gnn_in['b2'], 'L0_mix_Wqkv': _L0_mix_in['Wqkv'], 'L0_mix_bqkv': _L0_mix_in['bqkv'], 'L0_mix_Wproj': _L0_mix_in['Wproj'], 'L0_mix_bproj': _L0_mix_in['bproj'], 'L0_mix_temperature': _L0_mix_in['temperature'], 'L0_ffn_Wr': _L0_ffn_in['Wr'], 'L0_ffn_br': _L0_ffn_in['br'], 'L0_ffn_W1': _L0_ffn_in['W1'], 'L0_ffn_b1': _L0_ffn_in['b1'], 'L0_ffn_g1': _L0_ffn_in['g1'], 'L0_ffn_be1': _L0_ffn_in['be1'], 'L0_ffn_m1': _L0_ffn_in['m1'], 'L0_ffn_v1': _L0_ffn_in['v1'], 'L0_ffn_W2': _L0_ffn_in['W2'], 'L0_ffn_b2': _L0_ffn_in['b2'], 'L0_ffn_g2': _L0_ffn_in['g2'], 'L0_ffn_be2': _L0_ffn_in['be2'], 'L0_ffn_m2': _L0_ffn_in['m2'], 'L0_ffn_v2': _L0_ffn_in['v2'], 'L0_ffn_Wo': _L0_ffn_in['Wo'], 'L0_ffn_bo': _L0_ffn_in['bo'], 'L1_gnn_W1': _L1_gnn_in['W1'], 'L1_gnn_a1': _L1_gnn_in['a1'], 'L1_gnn_W2': _L1_gnn_in['W2'], 'L1_gnn_a2': _L1_gnn_in['a2'], 'L1_mix_w_qkv': _L1_mix_in['w_qkv'], 'L1_mix_w_out': _L1_mix_in['w_out'], 'L1_mix_b_out': _L1_mix_in['b_out'], 'L1_ffn_gamma': _L1_ffn_in['gamma'], 'L1_ffn_beta': _L1_ffn_in['beta'], 'L1_ffn_Wr': _L1_ffn_in['Wr'], 'L1_ffn_br': _L1_ffn_in['br'], 'L1_ffn_W1': _L1_ffn_in['W1'], 'L1_ffn_b1': _L1_ffn_in['b1'], 'L1_ffn_W2': _L1_ffn_in['W2'], 'L1_ffn_b2': _L1_ffn_in['b2']}

def reference(x, src, dst, L0_gnn_Wq, L0_gnn_bq, L0_gnn_Wk, L0_gnn_bk, L0_gnn_Wv, L0_gnn_bv, L0_gnn_Wp, L0_gnn_bp, L0_gnn_ln_g, L0_gnn_ln_b, L0_gnn_W1, L0_gnn_b1, L0_gnn_W2, L0_gnn_b2, L0_mix_Wqkv, L0_mix_bqkv, L0_mix_Wproj, L0_mix_bproj, L0_mix_temperature, L0_ffn_Wr, L0_ffn_br, L0_ffn_W1, L0_ffn_b1, L0_ffn_g1, L0_ffn_be1, L0_ffn_m1, L0_ffn_v1, L0_ffn_W2, L0_ffn_b2, L0_ffn_g2, L0_ffn_be2, L0_ffn_m2, L0_ffn_v2, L0_ffn_Wo, L0_ffn_bo, L1_gnn_W1, L1_gnn_a1, L1_gnn_W2, L1_gnn_a2, L1_mix_w_qkv, L1_mix_w_out, L1_mix_b_out, L1_ffn_gamma, L1_ffn_beta, L1_ffn_Wr, L1_ffn_br, L1_ffn_W1, L1_ffn_b1, L1_ffn_W2, L1_ffn_b2):
    import jax
    import jax.numpy as jnp

    def _L0_gnn_ref(feat, edge_src, edge_dst, Wq, bq, Wk, bk, Wv, bv, Wp, bp, ln_g, ln_b, W1, b1, W2, b2):
        import jax, jax.numpy as jnp
        import numpy as np
        import math
        N_NODES = 50000
        N_EDGES = 50000
        C = 256
        H = 8
        HD = C // H

        def _layernorm(x, g, b, eps=1e-05):
            mu = jnp.mean(x, axis=-1, keepdims=True)
            var = jnp.mean(jnp.square(x - mu), axis=-1, keepdims=True)
            return (x - mu) * jax.lax.rsqrt(var + eps) * g + b
        n = feat.shape[0]
        q = (feat @ Wq.T + bq).reshape(n, H, HD)
        k = (feat @ Wk.T + bk).reshape(n, H, HD)
        v = (feat @ Wv.T + bv).reshape(n, H, HD)
        score = jnp.einsum('ehd,ehd->eh', q[edge_dst], k[edge_src])
        score = jnp.clip(score / math.sqrt(HD), -10.0, 10.0)
        smax = jax.ops.segment_max(score, edge_dst, num_segments=n)
        smax = jnp.where(jnp.isfinite(smax), smax, 0.0)
        ex = jnp.exp(score - smax[edge_dst])
        den = jax.ops.segment_sum(ex, edge_dst, num_segments=n)
        alpha = ex / den[edge_dst]
        wv = jax.ops.segment_sum(alpha[:, :, None] * v[edge_src], edge_dst, num_segments=n).reshape(n, C)
        y = wv @ Wp.T + bp
        x = feat + y
        h = _layernorm(x, ln_g, ln_b)
        h = jax.nn.gelu(h @ W1.T + b1, approximate=False) @ W2.T + b2
        return x + h

    def _L0_mix_ref(x, Wqkv, bqkv, Wproj, bproj, temperature):
        import jax, jax.numpy as jnp
        import numpy as np
        A, Bc, Cc = (0.5, 1.0, 1.0)
        H = 8
        EPS = 1e-12

        def _normalize(t):
            n = jnp.linalg.norm(t, axis=-1, keepdims=True)
            return t / jnp.maximum(n, EPS)
        B, N, C = x.shape
        D = C // H
        scale = float(D) ** 0.25
        qkv = (x @ Wqkv.T + bqkv).reshape(B, N, 3, H, D)
        qkv = jnp.transpose(qkv, (2, 0, 3, 1, 4))
        q, k, v = (qkv[0], qkv[1], qkv[2])
        q = q * scale
        v1 = jnp.concatenate([jnp.ones((B, H, N, 1), dtype=v.dtype), v], axis=-1)
        qn = _normalize(q) * (scale * temperature)
        kn = _normalize(k) * scale
        vN = v1 / N
        kv_mod = jnp.einsum('bhni,bhnj,bhne->bhije', kn, kn, vN)
        kv = jnp.einsum('bhnd,bhne->bhde', kn, vN)
        vsum = jnp.sum(vN, axis=-2)[:, :, None, :]
        y = A * jnp.einsum('bhni,bhnj,bhije->bhne', qn, qn, kv_mod) + scale ** 2 * Bc * jnp.einsum('bhnd,bhde->bhne', qn, kv) + scale ** 4 * Cc * vsum
        y_norm, y = (y[..., :1], y[..., 1:])
        y = y / y_norm
        out = jnp.transpose(y, (0, 2, 1, 3)).reshape(B, N, H * D)
        return out @ Wproj.T + bproj

    def _L0_ffn_ref(x, Wr, br, W1, b1, g1, be1, m1, v1, W2, b2, g2, be2, m2, v2, Wo, bo):
        import jax, jax.numpy as jnp
        import numpy as np
        BN_EPS = 0.001

        def _bn(h, g, b, m, v):
            return g * (h - m) * jax.lax.rsqrt(v + BN_EPS) + b
        feat = jnp.mean(x, axis=0)
        w = jax.nn.softmax(feat @ Wr + br, axis=-1)
        h = jnp.einsum('bfd,edh->bfeh', x, W1) + b1
        h = jax.nn.relu(_bn(h, g1, be1, m1, v1))
        h = jnp.einsum('bfeh,ehk->bfek', h, W2) + b2
        h = jax.nn.relu(_bn(h, g2, be2, m2, v2))
        y = jnp.einsum('bfeh,ehd->bfed', h, Wo) + bo
        return jnp.einsum('bfed,fe->bfd', y, w)

    def _L1_gnn_ref(h, W1, a1, W2, a2, src, dst):
        import jax, jax.numpy as jnp
        import numpy as np
        N = 50000
        E_RAND = 25000
        IN_DIM = 256
        HID = 64
        HEADS = 4
        OUT_DIM = 256
        NEG_SLOPE = 0.01

        def _xavier(key, shape, fan_in, fan_out):
            gain = np.sqrt(2.0)
            std = gain * np.sqrt(2.0 / (fan_in + fan_out))
            return jax.random.normal(key, shape, dtype=jnp.float32) * std

        def _leaky(x):
            return jnp.where(x > 0, x, NEG_SLOPE * x)

        def _segment_softmax(e, dst, n):
            m = jax.ops.segment_max(e, dst, num_segments=n)
            m = jnp.where(jnp.isfinite(m), m, 0.0)
            ex = jnp.exp(e - m[dst])
            s = jax.ops.segment_sum(ex, dst, num_segments=n)
            return ex / s[dst]
        n = h.shape[0]
        z = jnp.einsum('ni,hoi->nho', h, W1)
        a_s, a_d = (a1[:, :HID], a1[:, HID:])
        es = jnp.einsum('nho,ho->nh', z, a_s)
        ed = jnp.einsum('nho,ho->nh', z, a_d)
        e = _leaky(es[src] + ed[dst])
        alpha = _segment_softmax(e, dst, n)
        m = jax.ops.segment_sum(alpha[:, :, None] * z[src], dst, num_segments=n)
        h1 = jax.nn.elu(m.reshape(n, HEADS * HID))
        z2 = h1 @ W2.T
        e2 = _leaky((z2 @ a2[:OUT_DIM])[src] + (z2 @ a2[OUT_DIM:])[dst])
        alpha2 = _segment_softmax(e2, dst, n)
        out = jax.ops.segment_sum(alpha2[:, None] * z2[src], dst, num_segments=n)
        return out

    def _L1_mix_ref(x, w_qkv, w_out, b_out):
        import jax, jax.numpy as jnp
        import numpy as np
        HEADS = 8
        DIM_HEAD = 64
        EPS = 1e-05

        def _inst_norm(t):
            mu = jnp.mean(t, axis=-1, keepdims=True)
            var = jnp.var(t, axis=-1, keepdims=True)
            return (t - mu) / jnp.sqrt(var + EPS)
        b, n, dim = x.shape
        qkv = x @ w_qkv
        q, k, v = jnp.split(qkv, 3, axis=-1)
        to_heads = lambda t: t.reshape(b, n, HEADS, DIM_HEAD).transpose(0, 2, 1, 3)
        q, k, v = (to_heads(q), to_heads(k), to_heads(v))
        k = _inst_norm(k)
        v = _inst_norm(v)
        dots = jnp.einsum('bhnd,bhne->bhde', k, v)
        out = jnp.einsum('bhnd,bhde->bhne', q, dots) * (1.0 / n)
        out = out.transpose(0, 2, 1, 3).reshape(b, n, HEADS * DIM_HEAD)
        return out @ w_out + b_out

    def _L1_ffn_ref(x, gamma, beta, Wr, br, W1, b1, W2, b2):
        import jax, jax.numpy as jnp
        import numpy as np
        E = 8
        K = 2
        D = 256
        H = 512
        DOUT = 256
        EPS = 1e-05
        mu = jnp.mean(x, axis=-1, keepdims=True)
        var = jnp.mean(jnp.square(x - mu), axis=-1, keepdims=True)
        xn = (x - mu) * jax.lax.rsqrt(var + EPS) * gamma + beta
        logits = jnp.einsum('bsd,de->bse', xn, Wr) + br
        top_vals, top_idx = jax.lax.top_k(logits, K)
        w = jax.nn.softmax(top_vals, axis=-1)
        w_full = jnp.einsum('bsk,bske->bse', w, jax.nn.one_hot(top_idx, E, dtype=w.dtype))
        y = jnp.zeros(x.shape[:-1] + (DOUT,), x.dtype)
        for e in range(E):
            h = jax.nn.gelu(jnp.einsum('bsd,dh->bsh', xn, W1[e]) + b1[e], approximate=False)
            y_e = jnp.einsum('bsh,hd->bsd', h, W2[e]) + b2[e]
            y = y + y_e * w_full[..., e, None]
        return y
    xn = _layernorm(x, axis=-1)
    x = x + _L0_gnn_ref(xn, src, dst, L0_gnn_Wq, L0_gnn_bq, L0_gnn_Wk, L0_gnn_bk, L0_gnn_Wv, L0_gnn_bv, L0_gnn_Wp, L0_gnn_bp, L0_gnn_ln_g, L0_gnn_ln_b, L0_gnn_W1, L0_gnn_b1, L0_gnn_W2, L0_gnn_b2) + _L0_mix_ref(xn[None], L0_mix_Wqkv, L0_mix_bqkv, L0_mix_Wproj, L0_mix_bproj, L0_mix_temperature)[0]
    x = x + _L0_ffn_ref(_layernorm(x, axis=-1)[None], L0_ffn_Wr, L0_ffn_br, L0_ffn_W1, L0_ffn_b1, L0_ffn_g1, L0_ffn_be1, L0_ffn_m1, L0_ffn_v1, L0_ffn_W2, L0_ffn_b2, L0_ffn_g2, L0_ffn_be2, L0_ffn_m2, L0_ffn_v2, L0_ffn_Wo, L0_ffn_bo)[0]
    xn = _layernorm(x, axis=-1)
    x = x + _L1_gnn_ref(xn, L1_gnn_W1, L1_gnn_a1, L1_gnn_W2, L1_gnn_a2, src, dst) + _L1_mix_ref(xn[None], L1_mix_w_qkv, L1_mix_w_out, L1_mix_b_out)[0]
    x = x + _L1_ffn_ref(_layernorm(x, axis=-1)[None], L1_ffn_gamma, L1_ffn_beta, L1_ffn_Wr, L1_ffn_br, L1_ffn_W1, L1_ffn_b1, L1_ffn_W2, L1_ffn_b2)[0]
    return x

_drawn_inputs = setup_inputs


def setup_inputs(seed=0):
    import zlib

    import numpy as np

    out = dict(_drawn_inputs(seed))
    spreads = {'L0_gnn_bq': (0.0, 0.8),
     'L0_gnn_bk': (0.0, 0.8),
     'L0_gnn_bv': (0.0, 0.369),
     'L0_gnn_bp': (0.0, 0.1),
     'L0_gnn_ln_g': (1.0, 0.6),
     'L0_gnn_ln_b': (0.0, 0.8),
     'L0_gnn_b1': (0.0, 0.378),
     'L0_gnn_b2': (0.0, 0.1),
     'L0_mix_bqkv': (0.0, 0.377),
     'L0_mix_bproj': (0.0, 0.1),
     'L0_mix_temperature': (1.0, 0.6),
     'L0_ffn_br': (0.0, 0.386),
     'L0_ffn_b1': (0.0, 0.539),
     'L0_ffn_g1': (1.0, 0.536),
     'L0_ffn_be1': (0.0, 0.556),
     'L0_ffn_m1': (0.0, 0.516),
     'L0_ffn_v1': (1.0, 0.6),
     'L0_ffn_b2': (0.0, 0.363),
     'L0_ffn_g2': (1.0, 0.2),
     'L0_ffn_be2': (0.0, 0.394),
     'L0_ffn_m2': (0.0, 0.37),
     'L0_ffn_v2': (1.0, 0.6),
     'L0_ffn_bo': (0.0, 0.1),
     'L1_ffn_br': (0.0, 0.419)}
    factors = {'L0_gnn_Wq': 8.0,
     'L0_gnn_Wk': 8.0,
     'L0_gnn_Wv': 3.756,
     'L0_mix_Wqkv': 8.0,
     'L0_mix_Wproj': 2.842,
     'L1_mix_b_out': 8.0,
     'L1_ffn_gamma': 8.0,
     'L1_ffn_beta': 8.0,
     'L1_ffn_b1': 27.617,
     'L1_ffn_b2': 8.0}
    for name, (base, spread) in spreads.items():
        noise = np.random.default_rng([zlib.crc32(name.encode()), seed]).standard_normal(out[name].shape)
        drawn = base * np.exp(spread * noise) if base else spread * noise
        out[name] = jnp.asarray(drawn.astype(out[name].dtype))
    for name, factor in factors.items():
        out[name] = (out[name] * factor).astype(out[name].dtype)
    return out
```

```python
from contextlib import ExitStack

import numpy as np

import concourse.bass as bass
from concourse import mybir

F32 = mybir.dt.float32
BF16 = mybir.dt.bfloat16
I32 = mybir.dt.int32
ALU = mybir.AluOpType
ACT = mybir.ActivationFunctionType
AX = mybir.AxisListType.X

P = 128
NODES = 3125
C = 256
KC = C // P
NT = -(-NODES // P)
ROWS = NT * P
FULL = NODES // P
LAST = NODES - FULL * P
GT = 5
NG = NT // GT
GN = GT * P
EDGES = 50000
ET = -(-EDGES // P)
EROWS = ET + 1
NP = 416
PB = NP // 4
BATCH = 4
NB = NP // BATCH
NPX = NP + BATCH
FAR = 8191
H0, D0 = 8, C // 8
H1, D1 = 4, C // 4
HM, DM = 8, 64
SW = C + H0
BIG = 2.0 ** 100
NE = 8


def after(eng, sem, value):
    if not isinstance(value, int) or value > 0:
        eng.wait_ge(sem, value)


def loop(eng, count, body):
    body(0)
    if count > 1:
        with eng.Fori(1, count) as i:
            body(i)


BEHIND = [1, 3, 2, 2, 2]
USES = [3, 2]


def uses(g, j):
    return g * USES[j % 2] + j // 2


def spread(ap, axis, n):
    shape = list(ap.shape)
    shape.insert(axis, n)
    return ap.unsqueeze(axis).broadcast_to(shape)


class Core:
    pass


def scope(nc, ctx, stage):
    def sb(name, shape, dt=F32):
        return ctx.enter_context(nc.sbuf_tensor(f"{stage}_{name}", shape, dt))

    def ps(name, shape, dt=F32):
        size = int(np.prod(shape[1:]))
        banks = -(-size // 512)
        whole = ctx.enter_context(nc.psum_tensor(f"{stage}_{name}", [P, banks * 512], dt))
        if len(shape) == 2:
            return whole[0:shape[0], 0:size]
        if len(shape) == 3:
            return whole[0:shape[0], 0:size].rearrange("p (a b) -> p a b", a=shape[1])
        return whole[0:shape[0], 0:size].rearrange("p (a b c) -> p a b c", a=shape[1], b=shape[2])

    sems = []

    def clear():
        if sems:
            nc.clear_and_free_semaphores(sems)
            nc.all_engine_barrier()
    ctx.callback(clear)

    def sem(name):
        sems.append(nc.alloc_semaphore(f"{stage}_{name}"))
        return sems[-1]

    return sb, ps, sem


def prepare(nc, k, a):
    with ExitStack() as ctx:
        sb, ps, sem = scope(nc, ctx, "prepare")
        tail = sb("tail", [1, 2, EROWS * P - EDGES], I32)
        first = sb("first", [1, EROWS], I32)
        firstw = sb("firstw", [1, EROWS], I32)
        start = sb("start", [1, EROWS])
        rowno = sb("rowno", [1, EROWS])
        ones_row = sb("ones_row", [1, P])
        pairno = sb("pairno", [PB, 4])
        hits = sb("hits", [PB, 4, EROWS])
        count = sb("count", [PB, 4])
        tile_f = sb("tile_f", [PB, 4])
        win_f = sb("win_f", [PB, 4])
        win_o = sb("win_o", [PB, 4])
        win_c = sb("win_c", [PB, 4])
        win_i = sb("win_i", [PB, 4], I32)
        srow = sb("srow", [PB, 4, P], I32)
        drow = sb("drow", [PB, 4, P], I32)
        sf = sb("sf", [PB, 4, P])
        df = sb("df", [PB, 4, P])
        dr = sb("dr", [PB, 4, P])
        pstart = ps("pstart", [P, EROWS])
        pT = ps("pT", [P, 2, 512])
        tails_set, padded, edges_in, x_in = sem("tails_set"), sem("padded"), sem("edges_in"), sem("x_in")
        firsts_in, zeroed, idf_set, consts = sem("firsts_in"), sem("zeroed"), sem("idf_set"), sem("consts")
        dve, bcast, tiles_ready = sem("dve"), sem("bcast"), sem("tiles_ready")
        rows_in, wins_out, wins_in, turned = sem("rows_in"), sem("wins_out"), sem("wins_in"), sem("turned")
        rel_ready, share_set = sem("rel_ready"), sem("share_set")

        with nc.Block() as block:
            @block.sync
            def _(sp):
                for name, pad in (("src", k.src_pad), ("dst", k.dst_pad)):
                    flat = pad.rearrange("a b -> (a b)")
                    sp.dma_start(flat[0:EDGES].rearrange("(a b) -> a b", a=80),
                                 a[name].rearrange("(a b) -> a b", a=80)).then_inc(edges_in, 16)
                sp.wait_ge(tails_set, 2)
                for n, pad in enumerate((k.src_pad, k.dst_pad)):
                    flat = pad.rearrange("(o a) b -> o (a b)", o=1)
                    sp.dma_start(flat[:, EDGES:EROWS * P], tail[:, n, :]).then_inc(edges_in, 16)
                sp.wait_ge(zeroed, 1)
                sp.dma_start(k.x[:, 0:FULL, :], a["x"][0:FULL * P, :].rearrange("(t p) c -> p t c", p=P)).then_inc(x_in, 16)
                sp.dma_start(k.x[0:LAST, FULL, :], a["x"][FULL * P:NODES, :]).then_inc(x_in, 16)
                sp.wait_ge(edges_in, 64)
                sp.dma_start(first[:, :], k.dst_pad[:, 0:1].rearrange("a b -> b a"),
                             allow_slow_non_contiguous=True).then_inc(firsts_in, 16)
                sp.wait_ge(dve, 8)
                sp.dma_start(k.win_dram.rearrange("b p -> p b"), win_i[:, :],
                             allow_slow_non_contiguous=True).then_inc(wins_out, 16)
                sp.wait_ge(wins_out, 16)
                sp.dma_start(k.win[:, 0:NP], k.win_dram.rearrange("(o b) p -> o (b p)", o=1)).then_inc(wins_in, 16)
                sp.wait_ge(wins_in, 16)
                sp.wait_ge(x_in, 32)

            @block.gpsimd
            def _(pool):
                pool.memset(k.x[:, FULL, :], 0.0).then_inc(zeroed, 1)
                pool.memset(k.share[:, :], 1.0 / NODES).then_inc(share_set, 1)
                pool.wait_ge(share_set, 1)
                pool.affine_select(out=k.share[:, :], in_=k.share[:, :], compare_op=ALU.is_gt, fill=0.0, base=NODES,
                                   pattern=[[-P, NT]], channel_multiplier=-1).then_inc(share_set, 1)
                pool.memset(k.ident[:, :], 0.0).then_inc(idf_set, 1)
                pool.wait_ge(idf_set, 1)
                pool.affine_select(out=k.ident[:, :], in_=k.ident[:, :], compare_op=ALU.not_equal, fill=1.0, base=0,
                                   pattern=[[-1, P]], channel_multiplier=1).then_inc(idf_set, 1)
                pool.iota(k.lane[:, :], [[1, P]], base=0, channel_multiplier=0,
                          allow_small_or_imprecise_dtypes=True).then_inc(consts, 1)
                pool.iota(rowno[:, :], [[1, EROWS]], base=0, channel_multiplier=0,
                          allow_small_or_imprecise_dtypes=True).then_inc(consts, 1)
                pool.iota(pairno[:, :], [[PB, 4]], base=0, channel_multiplier=1,
                          allow_small_or_imprecise_dtypes=True).then_inc(consts, 1)
                pool.memset(ones_row[:, :], 1.0).then_inc(consts, 1)
                pool.memset(k.power[:, :], -0.5).then_inc(consts, 1)
                pool.memset(k.win[:, NP:NPX], 0).then_inc(consts, 1)
                pool.memset(k.rel[:, NP:NPX], -1.0).then_inc(consts, 1)
                pool.memset(k.src[:, NP:NPX], 0).then_inc(consts, 1)
                pool.wait_ge(tiles_ready, 1)
                for b in range(4):
                    for table, rows in ((k.src_pad, srow), (k.dst_pad, drow)):
                        pool.indirect_dma_start(rows[:, b, :], None, table,
                                                bass.IndirectOffsetOnAxis(ap=k.tile_i[:, b:b + 1], axis=0)).then_inc(rows_in, 16)

            @block.vector
            def _(dv):
                dv.memset(tail[:, 0, :], 0).then_inc(tails_set, 1)
                dv.memset(tail[:, 1, :], FAR).then_inc(tails_set, 1)
                dv.memset(k.ones[:, :], 1.0).then_inc(dve, 1)
                dv.wait_ge(firsts_in, 16)
                dv.tensor_scalar(firstw[:, :], first[:, :], 7, None, ALU.arith_shift_right).then_inc(dve, 1)
                dv.wait_ge(consts, 8)
                dv.wait_ge(dve, 2)
                dv.tensor_tensor(start[:, :], firstw[:, :], rowno[:, :], ALU.add).then_inc(dve, 1)
                dv.wait_ge(dve, 3)
                dv.memset(start[:, 0:1], 0.0).then_inc(dve, 1)
                dv.wait_ge(bcast, 1)
                for b in range(4):
                    ins = dv.tensor_scalar(hits[:, b, :], pstart[0:PB, :], pairno[:, b:b + 1], None, ALU.is_le, ALU.add,
                                           accum_out=count[:, b:b + 1])
                ins.then_inc(dve, 1)
                dv.wait_ge(dve, 5)
                dv.tensor_scalar(k.tile_i[:, :], count[:, :], -1.0, None, ALU.add).then_inc(tiles_ready, 1)
                dv.tensor_tensor(win_f[:, :], pairno[:, :], count[:, :], ALU.subtract).then_inc(dve, 1)
                dv.wait_ge(dve, 6)
                dv.tensor_scalar(win_o[:, :], win_f[:, :], 1.0, float(P), ALU.add, ALU.mult).then_inc(dve, 1)
                dv.tensor_scalar(win_i[:, :], win_f[:, :], 1.0, float(NT - 1), ALU.add, ALU.min).then_inc(dve, 1)
                dv.wait_ge(dve, 8)
                dv.wait_ge(rows_in, 128)
                dv.tensor_tensor(dr[:, :, :], drow[:, :, :], spread(win_o[:, :], 2, P), ALU.subtract).then_inc(rel_ready, 1)
                dv.tensor_copy(sf[:, :, :], srow[:, :, :]).then_inc(rel_ready, 1)
                dv.wait_ge(turned, 8)
                for b in range(4):
                    dv.tensor_copy(k.rel[:, b * PB:(b + 1) * PB], pT[:, 0, b * P:b * P + PB]).then_inc(dve, 1)
                    dv.tensor_copy(k.src[:, b * PB:(b + 1) * PB], pT[:, 1, b * P:b * P + PB]).then_inc(dve, 1)

            @block.tensor
            def _(pe):
                pe.wait_ge(dve, 4)
                pe.wait_ge(consts, 8)
                pe.matmul(pstart[:, :], ones_row[:, :], start[:, :], start=True, stop=True).then_inc(bcast, 1)
                pe.wait_ge(idf_set, 2)
                pe.wait_ge(rel_ready, 2)
                for n, rows in enumerate((dr, sf)):
                    for b in range(4):
                        pe.transpose(pT[:, n, b * P:b * P + PB], rows[:, b, :], k.ident[0:PB, 0:PB]).then_inc(turned, 1)


def normalise(dv, g, source, s, t):
    for j in range(GT):
        dv.bn_stats(t.stats[:, j, :], source(g, j)).then_inc(s.stats_ready, 1)
    dv.wait_ge(s.stats_ready, g * GT + GT)
    dv.sem_inc(s.stats_fence, 1)
    for j in range(GT):
        dv.bn_aggr(t.moments[:, j, :], t.stats[:, j, :]).then_inc(s.moments_ready, 1)
    dv.wait_ge(s.moments_ready, g * GT + GT)
    dv.tensor_scalar(t.vareps[:, :], t.moments[:, :, 1], 1e-5, None, ALU.add).then_inc(s.vareps_ready, 1)
    dv.wait_ge(s.rstd_ready, g + 1)
    for j in range(GT):
        dv.tensor_scalar(t.normed[:, j, :], source(g, j), t.moments[:, j, 0:1], t.rstd[:, j:j + 1],
                         ALU.subtract, ALU.mult).then_inc(s.normed_ready, 1)


def deviations(pool, g, k, s, t):
    pool.wait_ge(s.vareps_ready, g + 1)
    pool.tensor_tensor(t.rstd[:, :], t.vareps[:, :], k.power[:, 0:GT], ALU.pow).then_inc(s.rstd_ready, 1)


class Chain:

    def __init__(self, eng, sem, per):
        self.eng, self.sem, self.per = eng, sem, per

    def turn(self, i):
        self.count = i * self.per
        self.left = self.per

    def __call__(self, instruction):
        self.left -= 1
        instruction.then_inc(self.sem, 1)
        self.eng.wait_ge(self.sem, self.count + self.per - self.left)


def norm_tensors(sb, sem, tag=""):
    t, s = Core(), Core()
    t.stats = sb(f"stats{tag}", [P, GT, 6])
    t.moments = sb(f"moments{tag}", [P, GT, 2])
    t.vareps = sb(f"vareps{tag}", [P, GT])
    t.rstd = sb(f"rstd{tag}", [P, GT])
    t.normed = sb(f"normed{tag}", [P, GT, C])
    s.stats_ready = sem("stats_ready" + tag)
    s.stats_fence = sem("stats_fence" + tag)
    s.moments_ready = sem("moments_ready" + tag)
    s.vareps_ready = sem("vareps_ready" + tag)
    s.rstd_ready = sem("rstd_ready" + tag)
    s.normed_ready = sem("normed_ready" + tag)
    return t, s


def project_first(nc, k, a):
    with ExitStack() as ctx:
        sb, ps, sem = scope(nc, ctx, "project_first")
        t, s = norm_tensors(sb, sem)
        W = 1536
        CH = W // 512
        w = sb("w", [P, KC, W])
        bias = sb("bias", [P, W])
        xT = sb("xT", [P, 2, KC, P])
        outs = sb("outs", [P, 2, W])
        pT = [ps(f"pT{i}", [P, 512]) for i in range(2)]
        pM = [[ps(f"pM{i}{c}", [P, 512]) for c in range(CH)] for i in range(2)]
        loaded, kept, xT_psum, xT_ready = sem("loaded"), sem("kept"), sem("xT_psum"), sem("xT_ready")
        projected, outs_ready, xn_kept = sem("projected"), sem("outs_ready"), sem("xn_kept")
        stored = [sem("stored0"), sem("stored1")]
        sums_clear = sem("sums_clear")

        with nc.Block() as block:
            @block.sync
            def _(sp):
                for n in range(KC):
                    sp.dma_start(w[:, n, :], a["w_first"][n * P:(n + 1) * P, :]).then_inc(loaded, 16)
                sp.dma_start(bias[:, :], a["b_first"].partition_broadcast(P)).then_inc(loaded, 16)

                def group(g):
                    for j in range(GT):
                        n, u = g * GT + j, j % 2
                        sp.wait_ge(outs_ready, CH * n + CH)
                        sp.dma_start(k.kv_table[bass.ds(n * P, P), :], outs[:, u, 0:512]).then_inc(stored[u], 16)
                        sp.dma_start(k.mix_qkv[bass.ds(n * P, P), :], outs[:, u, 768:1536]).then_inc(stored[u], 16)
                loop(sp, NG, group)
                for u in range(2):
                    sp.wait_ge(stored[u], 32 * USES[u] * NG)

            @block.gpsimd
            def _(pool):
                pool.memset(k.sums[:, :, :], 0.0).then_inc(sums_clear, 1)
                loop(pool, NG, lambda g: deviations(pool, g, k, s, t))

            @block.vector
            def _(dv):
                dv.wait_ge(loaded, 48)

                def group(g):
                    after(dv, xT_psum, GT * g)
                    after(dv, xn_kept, g)
                    normalise(dv, g, lambda g, j: k.x[:, bass.ds(g * GT + j, 1), :], s, t)
                    for j in range(GT):
                        n, u = g * GT + j, j % 2
                        after(dv, stored[u], 32 * uses(g, j))
                        after(dv, kept, n - BEHIND[j] + 1)
                        for c in range(CH):
                            dv.wait_ge(projected, CH * n + c + 1)
                            dv.tensor_tensor(outs[:, u, c * 512:(c + 1) * 512], pM[u][c][:, :],
                                             bias[:, c * 512:(c + 1) * 512], ALU.add).then_inc(outs_ready, 1)
                loop(dv, NG, group)

            @block.scalar
            def _(ac):
                def group(g):
                    for j in range(GT):
                        n, u = g * GT + j, j % 2
                        ac.wait_ge(xT_psum, n + 1)
                        after(ac, projected, CH * (n - BEHIND[j] + 1))
                        ac.copy(xT[:, u, :, :], pT[u][:, 0:C].rearrange("p (k n) -> p k n", k=KC)).then_inc(xT_ready, 1)
                        if j >= 1:
                            ac.wait_ge(outs_ready, CH * (n - 1) + 2)
                            ac.copy(k.node[:, bass.ds(n - 1, 1), :], outs[:, 1 - u:2 - u, 512:768]).then_inc(kept, 1)
                    ac.wait_ge(outs_ready, CH * n + 2)
                    ac.copy(k.node[:, bass.ds(n, 1), :], outs[:, 0:1, 512:768]).then_inc(kept, 1)
                    ac.copy(k.xn[:, bass.ds(g * GT, GT), :], t.normed[:, :, :]).then_inc(xn_kept, 1)
                loop(ac, NG, group)

            @block.tensor
            def _(pe):
                pe.wait_ge(loaded, 48)

                def group(g):
                    for j in range(GT):
                        n, u = g * GT + j, j % 2
                        pe.wait_ge(s.normed_ready, n + 1)
                        after(pe, xT_ready, n - BEHIND[j] + 1)
                        for c in range(KC):
                            ins = pe.transpose(pT[u][:, c * P:(c + 1) * P], t.normed[:, j, c * P:(c + 1) * P], k.ident[:, :])
                        ins.then_inc(xT_psum, 1)
                        pe.wait_ge(xT_ready, n + 1)
                        after(pe, outs_ready, CH * (n - BEHIND[j] + 1))
                        for c in range(CH):
                            for q in range(KC):
                                ins = pe.matmul(pM[u][c][:, :], xT[:, u, q, :], w[:, q, c * 512:(c + 1) * 512],
                                                start=q == 0, stop=q == KC - 1)
                            ins.then_inc(projected, 1)
                loop(pe, NG, group)


def edge_tensors(sb, ps, sem, width, look):
    t, s = Core(), Core()
    t.index = sb("index", [P, 2, BATCH], I32)
    t.rows = sb("rows", [P, 2, BATCH, width])
    t.hot = sb("hot", [P, 2, BATCH, P])
    t.hotT = sb("hotT", [P, 2, BATCH, P])
    t.score = sb("score", [P, 2, BATCH, H0])
    t.weighted = sb("weighted", [P, 2, BATCH, SW])
    t.p_hotT = ps("p_hotT", [P, BATCH, P])
    t.p_look = ps("p_look", [P, BATCH, look])
    t.p_sum = ps("p_sum", [P, BATCH, 512])
    s.fence = sem("fence")
    s.index_ready = sem("index_ready")
    s.hot_ready = sem("hot_ready")
    s.hotT_psum = sem("hotT_psum")
    s.hotT_ready = sem("hotT_ready")
    s.looked_up = sem("looked_up")
    s.products_ready = sem("products_ready")
    s.scores_ready = sem("scores_ready")
    s.clipped = sem("clipped")
    s.exp_ready = sem("exp_ready")
    s.weighted_ready = sem("weighted_ready")
    s.summed = sem("summed")
    s.added = sem("added")
    s.rows_in = [sem("rows_in0"), sem("rows_in1")]
    return t, s


def edge_gather(pool, i, k, t, s, table, rows_free):
    for u in range(2):
        b = 2 * i + u
        after(pool, rows_free, b - 1)
        pool.sem_inc(s.fence, 1)
        pool.tensor_copy(t.index[:, u, :], k.src[:, bass.ds(b * BATCH, BATCH)]).then_inc(s.index_ready, 1)
        pool.wait_ge(s.index_ready, b + 1)
        pool.sem_inc(s.fence, 1)
        for m in range(BATCH):
            pool.indirect_dma_start(t.rows[:, u, m, :], None, table,
                                    bass.IndirectOffsetOnAxis(ap=t.index[:, u, m:m + 1], axis=0)).then_inc(s.rows_in[u], 16)


def edge_hot(dv, b, u, k, t, s):
    after(dv, s.summed, b - 1)
    for m in range(BATCH):
        ins = dv.tensor_scalar(t.hot[:, u, m, :], k.lane[:, :], k.rel[:, bass.ds(b * BATCH + m, 1)], None, ALU.is_equal)
    ins.then_inc(s.hot_ready, 1)


def edge_turn(pe, b, u, k, t, s):
    pe.wait_ge(s.hot_ready, b + 1)
    after(pe, s.hotT_ready, b)
    for m in range(BATCH):
        ins = pe.transpose(t.p_hotT[:, m, :], t.hot[:, u, m, :], k.ident[:, :])
    ins.then_inc(s.hotT_psum, 1)


def edge_keep(ac, b, u, t, s):
    ac.wait_ge(s.hotT_psum, b + 1)
    after(ac, s.looked_up, b - 1)
    ac.copy(t.hotT[:, u, :, :], t.p_hotT[:, :, :]).then_inc(s.hotT_ready, 1)


def edge_look(pe, b, u, k, t, s, windows, node, look_free):
    pe.wait_ge(s.hotT_ready, b + 1)
    after(pe, look_free, b)
    for m in range(BATCH):
        ins = pe.matmul(t.p_look[:, m, :], t.hotT[:, u, m, :], node[:, bass.ds(windows[m], 1), :], start=True, stop=True)
    ins.then_inc(s.looked_up, 1)


def edge_sum(pe, b, u, t, s, width):
    pe.wait_ge(s.weighted_ready, b + 1)
    after(pe, s.added, b * BATCH)
    for m in range(BATCH):
        ins = pe.matmul(t.p_sum[:, m, 0:width], t.hot[:, u, m, :], t.weighted[:, u, m, 0:width], start=True, stop=True)
    ins.then_inc(s.summed, 1)


def edge_add(dv, b, k, t, s, width):
    dv.wait_ge(s.summed, b + 1)
    for m in range(BATCH):
        window = dv.value_load(k.win[0:1, bass.ds(b * BATCH + m, 1)], min_val=0, max_val=NT - 1)
        into = k.sums[:, bass.ds(window, 1), 0:width]
        after(dv, s.added, b * BATCH + m)
        dv.tensor_tensor(into, into, t.p_sum[:, m:m + 1, 0:width], ALU.add).then_inc(s.added, 1)


def windows_of(pe, k, b):
    return [pe.value_load(k.win[0:1, bass.ds(b * BATCH + m, 1)], min_val=0, max_val=NT - 1) for m in range(BATCH)]


def edge_tensor_engine(pe, k, t, s, node, look_free, width):
    edge_turn(pe, 0, 0, k, t, s)
    edge_look(pe, 0, 0, k, t, s, windows_of(pe, k, 0), node, look_free)

    def steps(i):
        for u in range(2):
            b = 2 * i + u
            edge_turn(pe, b + 1, 1 - u, k, t, s)
            edge_look(pe, b + 1, 1 - u, k, t, s, windows_of(pe, k, b + 1), node, look_free)
            edge_sum(pe, b, u, t, s, width)
    loop(pe, NB // 2, steps)


def attend_first(nc, k):
    with ExitStack() as ctx:
        sb, ps, sem = scope(nc, ctx, "attend_first")
        t, s = edge_tensors(sb, ps, sem, 2 * C, C)
        product = sb("product", [P, BATCH, C])
        root = D0 ** 0.5
        with nc.Block() as block:
            @block.gpsimd
            def _(pool):
                loop(pool, NB // 2, lambda i: edge_gather(pool, i, k, t, s, k.kv_table, s.weighted_ready))
                for u in range(2):
                    pool.wait_ge(s.rows_in[u], 16 * BATCH * NB // 2)

            @block.tensor
            def _(pe):
                edge_tensor_engine(pe, k, t, s, k.node, s.products_ready, SW)

            @block.scalar
            def _(ac):
                edge_keep(ac, 0, 0, t, s)

                def steps(i):
                    for u in range(2):
                        b = 2 * i + u
                        edge_keep(ac, b + 1, 1 - u, t, s)
                        ac.wait_ge(s.clipped, b + 1)
                        after(ac, s.summed, b - 1)
                        ac.activation(t.weighted[:, u, :, C:SW], t.score[:, u, :, :], ACT.Exp,
                                      scale=1.0 / root).then_inc(s.exp_ready, 1)
                loop(ac, NB // 2, steps)

            @block.vector
            def _(dv):
                edge_hot(dv, 0, 0, k, t, s)

                def steps(i):
                    for u in range(2):
                        b = 2 * i + u
                        edge_hot(dv, b + 1, 1 - u, k, t, s)
                        dv.wait_ge(s.looked_up, b + 1)
                        dv.wait_ge(s.rows_in[u], (i + 1) * 16 * BATCH)
                        dv.tensor_tensor(product[:, :, :], t.p_look[:, :, :], t.rows[:, u, :, 0:C], ALU.mult).then_inc(s.products_ready, 1)
                        dv.wait_ge(s.products_ready, b + 1)
                        dv.tensor_reduce(t.score[:, u, :, :], product[:, :, :].rearrange("p m (h d) -> p m h d", h=H0),
                                         AX, ALU.add).then_inc(s.scores_ready, 1)
                        dv.wait_ge(s.scores_ready, b + 1)
                        dv.tensor_scalar(t.score[:, u, :, :], t.score[:, u, :, :], -10.0 * root, 10.0 * root, ALU.max,
                                         ALU.min).then_inc(s.clipped, 1)
                        if u or not isinstance(i, int):
                            edge_add(dv, b - 1, k, t, s, SW)
                        dv.wait_ge(s.exp_ready, b + 1)
                        dv.tensor_tensor(t.weighted[:, u, :, 0:C].rearrange("p m (h d) -> p m h d", h=H0),
                                         t.rows[:, u, :, C:2 * C].rearrange("p m (h d) -> p m h d", h=H0),
                                         spread(t.weighted[:, u, :, C:SW], 3, D0), ALU.mult).then_inc(s.weighted_ready, 1)
                loop(dv, NB // 2, steps)
                edge_add(dv, NB - 1, k, t, s, SW)


SHIFTS = D0 // 2 + 1
FEAT = SHIFTS * D0 + D0 + 1
FCH = -(-FEAT // P)
FLAST = FEAT - (FCH - 1) * P
ROOT4 = float(D0) ** 0.25
VW = D0 + 1


def features(dv, double, phi, ready):
    ap = double[:, :, :]
    steps = [list(x) for x in ap.ap]
    onward = bass.AP(tensor=ap.tensor, offset=ap.offset, ap=[steps[0], steps[1], [1, SHIFTS], [1, D0]])
    dv.tensor_tensor(phi[:, :, 0:SHIFTS * D0].rearrange("p h (s d) -> p h s d", s=SHIFTS),
                     spread(double[:, :, 0:D0], 2, SHIFTS), onward, ALU.mult).then_inc(ready, 1)


def mix_keys(nc, k, a):
    with ExitStack() as ctx:
        sb, ps, sem = scope(nc, ctx, "mix_keys")
        kv = sb("kv", [P, 2, 2 * C])
        square = sb("square", [P, C])
        norm2 = sb("norm2", [P, H0])
        factor = sb("factor", [P, H0])
        double = sb("double", [P, H0, 2 * D0])
        phi = sb("phi", [P, 2, H0, FEAT])
        vals = sb("vals", [P, 2, H0, VW])
        zeros = sb("zeros", [P, SW])
        acc = [ps(f"acc{c}", [P, 512]) for c in range(FCH)]
        kv_in = [sem("kv_in0"), sem("kv_in1")]
        squared, norm2_ready, clamped, factor_ready = sem("squared"), sem("norm2_ready"), sem("clamped"), sem("factor_ready")
        half, doubled, phi_ready, vals_ready, summed = sem("half"), sem("doubled"), sem("phi_ready"), sem("vals_ready"), sem("summed")
        zeroed, consts, cleared, kept, lin = sem("zeroed"), sem("consts"), sem("cleared"), sem("kept"), sem("lin")

        with nc.Block() as block:
            @block.sync
            def _(sp):
                def group(g):
                    for j in range(GT):
                        n, u = g * GT + j, j % 2
                        after(sp, vals_ready, n - BEHIND[j] + 1)
                        sp.dma_start(kv[:, u, :], k.mix_qkv[bass.ds(n * P, P), 0:2 * C]).then_inc(kv_in[u], 16)
                loop(sp, NG, group)

            @block.gpsimd
            def _(pool):
                pool.memset(phi[:, 0, :, FEAT - 1:FEAT], 1.0).then_inc(consts, 1)
                pool.memset(phi[:, 1, :, FEAT - 1:FEAT], 1.0).then_inc(consts, 1)
                pool.memset(zeros[:, :], 0.0).then_inc(zeroed, 1)

                def group(g):
                    for j in range(GT):
                        n = g * GT + j
                        pool.wait_ge(clamped, n + 1)
                        pool.tensor_tensor(factor[:, :], norm2[:, :], k.power[:, 0:H0], ALU.pow).then_inc(factor_ready, 1)
                loop(pool, NG, group)

            @block.vector
            def _(dv):
                dv.wait_ge(consts, 2)

                def group(g):
                    for j in range(GT):
                        n, u = g * GT + j, j % 2
                        keys = kv[:, u, 0:C].rearrange("p (h d) -> p h d", h=H0)
                        dv.wait_ge(kv_in[u], 16 * (uses(g, j) + 1))
                        dv.tensor_tensor(square[:, :], kv[:, u, 0:C], kv[:, u, 0:C], ALU.mult).then_inc(squared, 1)
                        dv.wait_ge(squared, n + 1)
                        dv.tensor_reduce(norm2[:, :], square[:, :].rearrange("p (h d) -> p h d", h=H0), AX, ALU.add).then_inc(norm2_ready, 1)
                        dv.wait_ge(norm2_ready, n + 1)
                        dv.tensor_scalar(norm2[:, :], norm2[:, :], 1e-24, ROOT4 ** -2, ALU.max, ALU.mult).then_inc(clamped, 1)
                        after(dv, summed, n - BEHIND[j] + 1)
                        dv.tensor_scalar(vals[:, u, :, 0:1], spread(k.share[:, bass.ds(n, 1)], 1, H0), 1.0, None, ALU.mult)
                        dv.tensor_scalar(vals[:, u, :, 1:VW], kv[:, u, C:2 * C].rearrange("p (h d) -> p h d", h=H0),
                                         k.share[:, bass.ds(n, 1)], None, ALU.mult)
                        dv.wait_ge(factor_ready, n + 1)
                        dv.tensor_tensor(double[:, :, 0:D0], keys, spread(factor[:, :], 2, D0), ALU.mult).then_inc(half, 1)
                        dv.wait_ge(half, n + 1)
                        dv.tensor_copy(double[:, :, D0:2 * D0], double[:, :, 0:D0]).then_inc(doubled, 1)
                        dv.tensor_copy(phi[:, u, :, SHIFTS * D0:FEAT - 1], double[:, :, 0:D0]).then_inc(vals_ready, 1)
                        dv.wait_ge(doubled, n + 1)
                        features(dv, double, phi[:, u], phi_ready)
                loop(dv, NG, group)
                dv.wait_ge(summed, NT)
                for c in range(FCH):
                    m = P if c < FCH - 1 else FLAST
                    if c == 0:
                        parts = [(0, D0, 0.5), (D0, 2 * D0, 1.0), (2 * D0, P, 1.0)]
                    elif c < FCH - 1:
                        parts = [(0, P, 1.0)]
                    else:
                        parts = [(0, D0, 0.5), (D0, 2 * D0, ROOT4 ** 2), (2 * D0, m, ROOT4 ** 4)]
                    for lo, hi, weight in parts:
                        dv.tensor_scalar(k.mixed[lo:hi, c, :], acc[c][lo:hi, 0:SW], weight, None, ALU.mult).then_inc(kept, 1)

            @block.tensor
            def _(pe):
                pe.wait_ge(zeroed, 1)
                for c in range(FCH):
                    ins = pe.matmul(acc[c][:, 0:SW], zeros[:, 0:P], zeros[:, 0:SW], start=True, stop=False, skip_group_check=True)

                def group(g):
                    for j in range(GT):
                        n, u = g * GT + j, j % 2
                        pe.wait_ge(phi_ready, n + 1)
                        for h in range(H0):
                            for c in range(FCH):
                                m = P if c < FCH - 1 else FLAST
                                ins = pe.matmul(acc[c][0:m, h * VW:(h + 1) * VW], phi[:, u, h, c * P:c * P + m],
                                                vals[:, u, h, :], start=False, stop=False, skip_group_check=True)
                        ins.then_inc(summed, 1)
                loop(pe, NG, group)


def mix_queries(nc, k, a):
    with ExitStack() as ctx:
        sb, ps, sem = scope(nc, ctx, "mix_queries")
        q = sb("q", [P, 2, C])
        square = sb("square", [P, C])
        norm2 = sb("norm2", [P, H0])
        factor = sb("factor", [P, H0])
        scaled = sb("scaled", [P, H0])
        temper = sb("temper", [P, H0])
        double = sb("double", [P, H0, 2 * D0])
        phi = sb("phi", [P, 2, H0, FEAT])
        headT = sb("headT", [P, 2, 4, P])
        restT = sb("restT", [P, H0, P])
        recip = sb("recip", [P, H0])
        y = sb("y", [P, 2, C])
        yT = sb("yT", [P, KC, P])
        w = sb("w", [P, KC, C])
        bias = sb("bias", [P, C])
        part = sb("part", [P, 2, C])
        pT = [ps(f"pT{i}", [P, 4, P]) for i in range(2)]
        pY = [ps(f"pY{i}", [P, H0, VW]) for i in range(2)]
        pYT = ps("pYT", [P, KC, P])
        pO = [ps(f"pO{i}", [P, C]) for i in range(2)]
        loaded, q_in = sem("loaded"), [sem("q_in0"), sem("q_in1")]
        squared, norm2_ready, clamped, factor_ready = sem("squared"), sem("norm2_ready"), sem("clamped"), sem("factor_ready")
        tempered, half, doubled, phi_ready = sem("tempered"), sem("half"), sem("doubled"), sem("phi_ready")
        turned, kept, head_done, recip_ready = sem("turned"), sem("kept"), sem("head_done"), sem("recip_ready")
        y_ready, yT_psum, yT_ready, projected = sem("y_ready"), sem("yT_psum"), sem("yT_ready"), sem("projected")
        part_ready, consts, done = sem("part_ready"), sem("consts"), sem("done")
        QUADS = H0 + 2

        def buf(j):
            return j % GT % 2

        with nc.Block() as block:
            @block.sync
            def _(sp):
                for n in range(KC):
                    sp.dma_start(w[:, n, :], a["w_mixproj"][n * P:(n + 1) * P, :]).then_inc(loaded, 16)
                sp.dma_start(bias[:, :], a["b_mixproj"].partition_broadcast(P)).then_inc(loaded, 16)
                sp.dma_start(temper[:, :], a["temperature"].partition_broadcast(P)).then_inc(loaded, 16)

                def group(g):
                    for j in range(GT):
                        n, u = g * GT + j, buf(j)
                        after(sp, half, n - BEHIND[j] + 1)
                        sp.dma_start(q[:, u, :], k.mix_qkv[bass.ds(n * P, P), 2 * C:3 * C]).then_inc(q_in[u], 16)
                loop(sp, NG, group)

            @block.gpsimd
            def _(pool):
                for u in range(2):
                    pool.memset(phi[:, u, :, FEAT - 1:FEAT], 1.0).then_inc(consts, 1)

                def group(g):
                    for j in range(GT):
                        pool.wait_ge(clamped, g * GT + j + 1)
                        pool.tensor_tensor(factor[:, :], norm2[:, :], k.power[:, 0:H0], ALU.pow).then_inc(factor_ready, 1)
                loop(pool, NG, group)

            @block.vector
            def _(dv):
                dv.wait_ge(consts, 2)
                dv.wait_ge(loaded, 64)

                def divide(n, u, j):
                    after(dv, yT_psum, n - BEHIND[j % GT] + 1)
                    dv.wait_ge(head_done, n * H0 + H0)
                    dv.reciprocal(recip[:, :], pY[u][:, :, 0]).then_inc(recip_ready, 1)
                    dv.wait_ge(recip_ready, n + 1)
                    dv.tensor_tensor(y[:, u, :].rearrange("p (h d) -> p h d", h=H0), pY[u][:, :, 1:VW],
                                     spread(recip[:, :], 2, D0), ALU.mult).then_inc(y_ready, 1)

                def add(n, u):
                    dv.wait_ge(projected, n + 1)
                    dv.tensor_tensor(part[:, u, :], pO[u][:, :], bias[:, :], ALU.add).then_inc(part_ready, 1)
                    dv.wait_ge(part_ready, n + 1)
                    nodes = k.x[:, bass.ds(n, 1), :]
                    dv.tensor_tensor(nodes, nodes, part[:, u:u + 1, :], ALU.add).then_inc(done, 1)

                def group(g):
                    for j in range(GT):
                        n, u = g * GT + j, buf(j)
                        dv.wait_ge(q_in[u], 16 * (uses(g, j) + 1))
                        dv.tensor_tensor(square[:, :], q[:, u, :], q[:, u, :], ALU.mult).then_inc(squared, 1)
                        dv.wait_ge(squared, n + 1)
                        dv.tensor_reduce(norm2[:, :], square[:, :].rearrange("p (h d) -> p h d", h=H0), AX, ALU.add).then_inc(norm2_ready, 1)
                        dv.wait_ge(norm2_ready, n + 1)
                        dv.tensor_scalar(norm2[:, :], norm2[:, :], ROOT4 ** 2, 1e-24, ALU.mult, ALU.max).then_inc(clamped, 1)
                        dv.wait_ge(factor_ready, n + 1)
                        dv.scalar_tensor_tensor(out=scaled[:, :], in0=factor[:, :], scalar=ROOT4 ** 2, in1=temper[:, :],
                                                op0=ALU.mult, op1=ALU.mult).then_inc(tempered, 1)
                        dv.wait_ge(tempered, n + 1)
                        dv.tensor_tensor(double[:, :, 0:D0], q[:, u, :].rearrange("p (h d) -> p h d", h=H0),
                                         spread(scaled[:, :], 2, D0), ALU.mult).then_inc(half, 1)
                        dv.wait_ge(half, n + 1)
                        dv.tensor_copy(double[:, :, D0:2 * D0], double[:, :, 0:D0]).then_inc(doubled, 1)
                        after(dv, turned, QUADS * (n - BEHIND[j] + 1))
                        dv.tensor_copy(phi[:, u, :, SHIFTS * D0:FEAT - 1], double[:, :, 0:D0])
                        dv.wait_ge(doubled, n + 1)
                        features(dv, double, phi[:, u], phi_ready)
                        if j >= 1 or not isinstance(g, int):
                            divide(n - 1, buf(j + GT - 1), j + GT - 1)
                        if j >= 2 or not isinstance(g, int):
                            add(n - 2, buf(j + GT - 2))
                loop(dv, NG, group)
                divide(NT - 1, buf(GT - 1), GT - 1)
                add(NT - 2, buf(GT - 2))
                add(NT - 1, buf(GT - 1))

            @block.scalar
            def _(ac):
                def keep(n, j):
                    ac.wait_ge(yT_psum, n + 1)
                    after(ac, projected, n)
                    ac.copy(yT[:, :, :], pYT[:, :, :]).then_inc(yT_ready, 1)

                def group(g):
                    for j in range(GT):
                        n = g * GT + j
                        for c in range(QUADS):
                            ac.wait_ge(turned, n * QUADS + c + 1)
                            if c < 2:
                                after(ac, head_done, n * H0)
                                ac.copy(restT[0:FLAST, 4 * c:4 * c + 4, :], pT[c % 2][0:FLAST, :, :]).then_inc(kept, 1)
                            else:
                                after(ac, head_done, n * H0 + c - 3)
                                ac.copy(headT[:, c % 2, :, :], pT[c % 2][:, :, :]).then_inc(kept, 1)
                        if j or not isinstance(g, int):
                            keep(n - 1, j)
                loop(ac, NG, group)
                keep(NT - 1, 0)

            @block.tensor
            def _(pe):
                pe.wait_ge(loaded, 64)

                def project(n, u):
                    pe.wait_ge(y_ready, n + 1)
                    after(pe, yT_ready, n)
                    for c in range(KC):
                        ins = pe.transpose(pYT[:, c, :], y[:, u, c * P:(c + 1) * P], k.ident[:, :])
                    ins.then_inc(yT_psum, 1)

                def product(n, u, j):
                    pe.wait_ge(yT_ready, n + 1)
                    after(pe, part_ready, n - BEHIND[j % GT] + 1)
                    for c in range(KC):
                        ins = pe.matmul(pO[u][:, :], yT[:, c, :], w[:, c, :], start=c == 0, stop=c == KC - 1)
                    ins.then_inc(projected, 1)

                def group(g):
                    for j in range(GT):
                        n, u = g * GT + j, buf(j)
                        pe.wait_ge(phi_ready, n + 1)
                        for c in range(QUADS + 1):
                            if c < QUADS:
                                after(pe, kept, n * QUADS + c - 1)
                                for m in range(4):
                                    if c < 2:
                                        ins = pe.transpose(pT[c % 2][0:FLAST, m, :], phi[:, u, 4 * c + m, (FCH - 1) * P:FEAT],
                                                           k.ident[:, :])
                                    else:
                                        ins = pe.transpose(pT[c % 2][:, m, :], phi[:, u, c - 2, m * P:(m + 1) * P], k.ident[:, :])
                                ins.then_inc(turned, 1)
                            if c >= 3:
                                h = c - 3
                                pe.wait_ge(kept, n * QUADS + c)
                                if h == 0:
                                    after(pe, y_ready, n - BEHIND[j] + 1)
                                pe.matmul(pY[u][:, h, :], restT[0:FLAST, h, :], k.mixed[0:FLAST, FCH - 1, h * VW:(h + 1) * VW],
                                          start=True, stop=False)
                                for m in range(4):
                                    ins = pe.matmul(pY[u][:, h, :], headT[:, (h + 2) % 2, m, :], k.mixed[:, m, h * VW:(h + 1) * VW],
                                                    start=False, stop=m == 3)
                                ins.then_inc(head_done, 1)
                        if j or not isinstance(g, int):
                            project(n - 1, buf(j + GT - 1))
                            product(n - 1, buf(j + GT - 1), j + GT - 1)
                loop(pe, NG, group)
                project(NT - 1, buf(GT - 1))
                product(NT - 1, buf(GT - 1), GT - 1)


def layer_first(nc, k, a):
    HID = 4 * C
    HC = HID // P
    HALF = GN // 2
    with ExitStack() as ctx:
        sb, ps, sem = scope(nc, ctx, "layer_first")
        t, s = norm_tensors(sb, sem)
        wp = sb("wp", [P, KC, C])
        w1 = sb("w1", [P, KC, HID])
        w2 = sb("w2", [P, HC, C])
        b1 = sb("b1", [P, HC])
        bp = sb("bp", [P, C])
        b2 = sb("b2", [P, C])
        gain = sb("gain", [P, KC])
        shift = sb("shift", [P, KC])
        den = sb("den", [P, GT, H0])
        rec = sb("rec", [P, GT, H0])
        mean = sb("mean", [P, GT, C])
        meanT = sb("meanT", [P, 2, KC, P])
        based = sb("based", [P, GT, C])
        mid = sb("mid", [P, GT, C])
        result = sb("result", [P, GT, C])
        hT = sb("hT", [P, KC, GN])
        hid = sb("hid", [P, HC, GN])
        pT = [ps(f"pT{i}", [P, KC, P]) for i in range(2)]
        pS = [ps(f"pS{i}", [P, C]) for i in range(2)]
        pW = [ps(f"pW{i}", [P, 2, 512]) for i in range(2)]
        loaded, den_ready, rec_ready, mean_ready = sem("loaded"), sem("den_ready"), sem("rec_ready"), sem("mean_ready")
        turned, kept, multiplied, taken = sem("turned"), sem("kept"), sem("multiplied"), sem("taken")
        wide_ready, gelu_ready, based_ready, result_base = sem("wide_ready"), sem("gelu_ready"), sem("based_ready"), sem("result_base")
        fence, done = sem("fence"), sem("done")

        with nc.Block() as block:
            @block.sync
            def _(sp):
                for n in range(KC):
                    sp.dma_start(wp[:, n, :], a["w_p"][n * P:(n + 1) * P, :]).then_inc(loaded, 16)
                    sp.dma_start(w1[:, n, :], a["w_1"][n * P:(n + 1) * P, :]).then_inc(loaded, 16)
                sp.dma_start(w2[:, :, :], a["w_2"].rearrange("(c p) n -> p c n", p=P)).then_inc(loaded, 16)
                for to, name in ((b1, "b_1"), (gain, "ln_g"), (shift, "ln_b")):
                    sp.dma_start(to[:, :], a[name]).then_inc(loaded, 16)
                sp.dma_start(bp[:, :], a["b_p"].partition_broadcast(P)).then_inc(loaded, 16)
                sp.dma_start(b2[:, :], a["b_2"].partition_broadcast(P)).then_inc(loaded, 16)
                sp.wait_ge(loaded, 160)

            @block.gpsimd
            def _(pool):
                pool.wait_ge(loaded, 160)

                def group(g):
                    after(pool, taken, 10 * g - 5)
                    pool.sem_inc(fence, 1)
                    pool.tensor_tensor(based[:, :, :], k.xn[:, bass.ds(g * GT, GT), :], spread(bp[:, :], 1, GT),
                                       ALU.add).then_inc(based_ready, 1)
                    deviations(pool, g, k, s, t)
                    after(pool, done, g * GT)
                    pool.wait_ge(taken, 10 * g + 5)
                    pool.tensor_tensor(result[:, :, :], mid[:, :, :], spread(b2[:, :], 1, GT), ALU.add).then_inc(result_base, 1)
                loop(pool, NG, group)

            @block.vector
            def _(dv):
                def group(g):
                    sums = k.sums[:, bass.ds(g * GT, GT), :]
                    dv.tensor_scalar(den[:, :, :], sums[:, :, C:SW], 1e-30, None, ALU.max).then_inc(den_ready, 1)
                    dv.wait_ge(den_ready, g + 1)
                    dv.reciprocal(rec[:, :, :], den[:, :, :]).then_inc(rec_ready, 1)
                    dv.wait_ge(rec_ready, g + 1)
                    after(dv, turned, 10 * g - 5)
                    dv.tensor_tensor(mean[:, :, :].rearrange("p t (h d) -> p t h d", h=H0),
                                     sums[:, :, 0:C].rearrange("p t (h d) -> p t h d", h=H0),
                                     spread(rec[:, :, :], 3, D0), ALU.mult).then_inc(mean_ready, 1)
                    dv.wait_ge(based_ready, g + 1)
                    after(dv, result_base, g)
                    for j in range(GT):
                        dv.wait_ge(multiplied, 10 * g + j + 1)
                        dv.tensor_tensor(mid[:, j, :], pS[j % 2][:, :], based[:, j, :], ALU.add).then_inc(taken, 1)
                    dv.wait_ge(taken, 10 * g + 5)
                    after(dv, turned, 10 * g)
                    normalise(dv, g, lambda g, j: mid[:, j, :], s, t)
                    dv.wait_ge(result_base, g + 1)
                    for j in range(GT):
                        dv.wait_ge(multiplied, 10 * g + 5 + j + 1)
                        dv.tensor_tensor(result[:, j, :], pS[(5 + j) % 2][:, :], result[:, j, :], ALU.add).then_inc(taken, 1)
                        dv.wait_ge(taken, 10 * g + 5 + j + 1)
                        nodes = k.x[:, bass.ds(g * GT + j, 1), :]
                        dv.tensor_tensor(nodes, nodes, result[:, j:j + 1, :], ALU.add).then_inc(done, 1)
                loop(dv, NG, group)

            @block.scalar
            def _(ac):
                ac.wait_ge(loaded, 160)

                def group(g):
                    for j in range(GT):
                        ac.wait_ge(turned, 10 * g + j + 1)
                        after(ac, multiplied, 10 * g + j - 1 if j >= 2 else 10 * g - GT)
                        ac.copy(meanT[:, j % 2, :, :], pT[j % 2][:, :, :]).then_inc(kept, 1)
                    for j in range(GT):
                        ac.wait_ge(turned, 10 * g + GT + j + 1)
                        after(ac, wide_ready, HC * g)
                        for c in range(KC):
                            ins = ac.activation(hT[:, c, j * P:(j + 1) * P], pT[(GT + j) % 2][:, c, :], ACT.Identity,
                                                bias=shift[:, c:c + 1], scale=gain[:, c:c + 1])
                        ins.then_inc(kept, 1)
                    after(ac, multiplied, 10 * g)
                    for m in range(HC):
                        ac.wait_ge(wide_ready, HC * g + m + 1)
                        ac.activation(hid[:, m, :].rearrange("p (a b) -> p a b", a=2), pW[m % 2][:, :, 0:HALF], ACT.Gelu,
                                      bias=b1[:, m:m + 1]).then_inc(gelu_ready, 1)
                loop(ac, NG, group)

            @block.tensor
            def _(pe):
                pe.wait_ge(loaded, 160)

                def turn(g, n, source, j):
                    after(pe, kept, 10 * g + n - 1)
                    for c in range(KC):
                        ins = pe.transpose(pT[n % 2][:, c, :], source[:, j, c * P:(c + 1) * P], k.ident[:, :])
                    ins.then_inc(turned, 1)

                def group(g):
                    pe.wait_ge(mean_ready, g + 1)
                    for j in range(GT + 1):
                        if j < GT:
                            turn(g, j, mean, j)
                        if j > 0:
                            m = j - 1
                            pe.wait_ge(kept, 10 * g + m + 1)
                            after(pe, taken, 10 * g + m - 1)
                            for c in range(KC):
                                ins = pe.matmul(pS[m % 2][:, :], meanT[:, m % 2, c, :], wp[:, c, :], start=c == 0, stop=c == KC - 1)
                            ins.then_inc(multiplied, 1)
                    for j in range(GT):
                        pe.wait_ge(s.normed_ready, g * GT + j + 1)
                        turn(g, GT + j, t.normed, j)
                    pe.wait_ge(kept, 10 * g + 10)
                    for m in range(HC):
                        after(pe, gelu_ready, HC * g + m - 1)
                        for half in range(2):
                            for c in range(KC):
                                ins = pe.matmul(pW[m % 2][:, half, 0:HALF], w1[:, c, m * P:(m + 1) * P],
                                                hT[:, c, half * HALF:(half + 1) * HALF], start=c == 0, stop=c == KC - 1)
                        ins.then_inc(wide_ready, 1)
                    for j in range(GT):
                        pe.wait_ge(gelu_ready, HC * g + HC)
                        after(pe, taken, 10 * g + GT + j - 1)
                        for m in range(HC):
                            ins = pe.matmul(pS[(GT + j) % 2][:, :], hid[:, m, j * P:(j + 1) * P], w2[:, m, :],
                                            start=m == 0, stop=m == HC - 1)
                        ins.then_inc(multiplied, 1)
                loop(pe, NG, group)


def experts(nc, k, a, second):
    wide = 2 * C if second else C
    MC = wide // P
    layers = 1 if second else 2
    HALF = GN // 2
    stage = "experts2" if second else "experts1"
    TURNS = GT + 3
    SMALL = 1 + GT + GT * NE
    WIDE = NE * layers * MC
    plan = []
    if second:
        plan = [("hidden", 0, 0), ("gates", 0, 0)]
        for e in range(NE):
            plan += [("hidden", 0, e + 1)] * (e + 1 < NE) + [("out", 0, e)]
    else:
        plan = [("hidden", 0, 0), ("hidden", 0, 1), ("hidden", 1, 0), ("gates", 0, 0)]
        for e in range(NE):
            plan += [("hidden", 0, e + 2)] * (e + 2 < NE) + [("hidden", 1, e + 1)] * (e + 1 < NE) + [("out", 0, e)]
    wides = [(layer, e, m) for what, layer, e in plan if what == "hidden" for m in range(MC)]
    nth = {w: i for i, w in enumerate(wides)}
    with ExitStack() as ctx:
        sb, ps, sem = scope(nc, ctx, stage)
        t, s = norm_tensors(sb, sem)
        if second:
            t2, s2 = norm_tensors(sb, sem, "_again")
            gain, shift = sb("gain", [P, KC]), sb("shift", [P, KC])
        else:
            t2, s2 = t, s
        w1 = sb("w1", [P, NE, KC, wide])
        w2 = sb("w2", [P, NE, KC, C]) if not second else None
        wo = sb("wo", [P, NE, MC, C])
        wr = sb("wr", [P, KC, NE])
        bo = sb("bo", [NE, C])
        br = sb("br", [P, NE])
        bn = sb("bn", [P, 2, 5, MC * NE]) if not second else None
        bn_eps = sb("bn_eps", [P, 2, MC * NE]) if not second else None
        scale = sb("scale", [P, 2, MC * NE]) if not second else None
        offset = sb("offset", [P, 2, MC * NE])
        hT = sb("hT", [P, KC, GN])
        act = [sb(f"act{n}", [P, 2, MC, GN]) for n in range(layers)]
        y = sb("y", [P, GT, C])
        logits = sb("logits", [P, GT, NE])
        shifted = sb("shifted", [P, GT, NE])
        odds = sb("odds", [P, GT, NE])
        gate = sb("gate", [P, GT, NE])
        gateT = sb("gateT", [NE, GN])
        top = sb("top", [P, GT])
        total = sb("total", [P, GT])
        if second:
            place = sb("place", [P, NE])
            found = sb("found", [P, GT, NE])
            one = [sb(f"one{n}", [P, GT, NE]) for n in range(2)]
            best = sb("best", [P, 2, GT])
            where = sb("where", [P, GT])
        pT = [ps(f"pT{i}", [P, KC, P]) for i in range(2)]
        pS = [ps(f"pS{i}", [P, 512]) for i in range(2)]
        pW = [ps(f"pW{i}", [P, 2, 512]) for i in range(2)]
        loaded, bn_ready, bn_power, offset_ready = sem("loaded"), sem("bn_ready"), sem("bn_power"), sem("offset_ready")
        turned, kept, wide_ready, act_ready = sem("turned"), sem("kept"), sem("wide_ready"), sem("act_ready")
        multiplied, taken, small, shifted_ready = sem("multiplied"), sem("taken"), sem("small"), sem("shifted_ready")
        odds_ready, gate_ready, done, placed = sem("odds_ready"), sem("gate_ready"), sem("done"), sem("placed")
        fold = sem("fold")
        LOADS = (2 * NE + 6) if second else (3 * NE + 4)

        with nc.Block() as block:
            @block.sync
            def _(sp):
                sp.dma_start(wr[:, :, :], a["w_r" + stage[-1]].rearrange("(c p) n -> p c n", p=P)).then_inc(loaded, 16)
                sp.dma_start(bo[:, :], a["b_o" + stage[-1]]).then_inc(loaded, 16)
                sp.dma_start(br[:, :], a["b_r" + stage[-1]].partition_broadcast(P)).then_inc(loaded, 16)
                if second:
                    sp.dma_start(offset[:, 0, :], a["b_hidden"]).then_inc(loaded, 16)
                    sp.dma_start(gain[:, :], a["gamma"]).then_inc(loaded, 16)
                    sp.dma_start(shift[:, :], a["beta"]).then_inc(loaded, 16)
                else:
                    sp.dma_start(bn[:, :, :, :], a["bn"]).then_inc(loaded, 16)
                for e in range(NE):
                    sp.dma_start(w1[:, e, :, :], a["w_hidden" + stage[-1]][e].rearrange("(c p) n -> p c n", p=P)).then_inc(loaded, 16)
                    if not second:
                        sp.dma_start(w2[:, e, :, :], a["w_deep"][e].rearrange("(c p) n -> p c n", p=P)).then_inc(loaded, 16)
                    sp.dma_start(wo[:, e, :, :], a["w_out" + stage[-1]][e].rearrange("(c p) n -> p c n", p=P)).then_inc(loaded, 16)
                sp.wait_ge(loaded, 16 * LOADS)

            @block.gpsimd
            def _(pool):
                if second:
                    pool.iota(place[:, :], [[1, NE]], base=0, channel_multiplier=0,
                              allow_small_or_imprecise_dtypes=True).then_inc(placed, 1)
                else:
                    pool.wait_ge(bn_ready, 1)
                    pool.tensor_tensor(scale[:, :, :].rearrange("p l n -> p (l n)"), bn_eps[:, :, :].rearrange("p l n -> p (l n)"),
                                       k.power[:, 0:2 * MC * NE], ALU.pow).then_inc(bn_power, 1)

                def group(g):
                    deviations(pool, g, k, s, t)
                    if second:
                        deviations(pool, g, k, s2, t2)
                loop(pool, NG, group)

            @block.vector
            def _(dv):
                dv.wait_ge(loaded, 16 * LOADS)
                if not second:
                    dv.tensor_scalar(bn_eps[:, :, :], bn[:, :, 3, :], 1e-3, None, ALU.add).then_inc(bn_ready, 1)
                    dv.wait_ge(bn_power, 1)
                    chain = Chain(dv, fold, 4)
                    chain.turn(0)
                    chain(dv.tensor_tensor(scale[:, :, :], scale[:, :, :], bn[:, :, 0, :], ALU.mult))
                    chain(dv.tensor_tensor(offset[:, :, :], bn[:, :, 4, :], bn[:, :, 2, :], ALU.subtract))
                    chain(dv.tensor_tensor(offset[:, :, :], offset[:, :, :], scale[:, :, :], ALU.mult))
                    chain(dv.tensor_tensor(offset[:, :, :], offset[:, :, :], bn[:, :, 1, :], ALU.add))
                else:
                    dv.wait_ge(placed, 1)
                chain = Chain(dv, small, 17 if second else 4)

                def softmax(g):
                    chain(dv.tensor_reduce(top[:, :], logits[:, :, :], AX, ALU.max))
                    dv.tensor_tensor(shifted[:, :, :], logits[:, :, :], spread(top[:, :], 2, NE), ALU.subtract).then_inc(shifted_ready, 1)
                    dv.wait_ge(odds_ready, g + 1)
                    chain(dv.tensor_reduce(total[:, :], odds[:, :, :], AX, ALU.add))
                    chain(dv.reciprocal(total[:, :], total[:, :]))
                    dv.tensor_tensor(gate[:, :, :], odds[:, :, :], spread(total[:, :], 2, NE), ALU.mult).then_inc(gate_ready, 1)

                def two_best(g):
                    places = spread(place[:, :], 1, GT)
                    for n in range(2):
                        chain(dv.tensor_reduce(best[:, n, :], logits[:, :, :], AX, ALU.max))
                        chain(dv.tensor_tensor(found[:, :, :], logits[:, :, :], spread(best[:, n, :], 2, NE), ALU.is_lt))
                        chain(dv.tensor_scalar(found[:, :, :], found[:, :, :], float(NE), None, ALU.mult))
                        chain(dv.tensor_tensor(found[:, :, :], found[:, :, :], places, ALU.add))
                        chain(dv.tensor_reduce(where[:, :], found[:, :, :], AX, ALU.min))
                        chain(dv.tensor_tensor(one[n][:, :, :], places, spread(where[:, :], 2, NE), ALU.is_equal))
                        if n == 0:
                            chain(dv.scalar_tensor_tensor(out=logits[:, :, :], in0=one[0][:, :, :], scalar=-BIG, in1=logits[:, :, :],
                                                          op0=ALU.mult, op1=ALU.add))
                    dv.tensor_tensor(shifted[:, :, 0], best[:, 1, :], best[:, 0, :], ALU.subtract).then_inc(shifted_ready, 1)
                    dv.wait_ge(odds_ready, g + 1)
                    chain(dv.tensor_scalar(total[:, :], odds[:, :, 0], 1.0, None, ALU.add))
                    chain(dv.reciprocal(total[:, :], total[:, :]))
                    chain(dv.tensor_tensor(top[:, :], odds[:, :, 0], total[:, :], ALU.mult))
                    dv.tensor_tensor(one[0][:, :, :], one[0][:, :, :], spread(total[:, :], 2, NE), ALU.mult)
                    dv.tensor_tensor(one[1][:, :, :], one[1][:, :, :], spread(top[:, :], 2, NE), ALU.mult).then_inc(small, 1)
                    chain.left -= 1
                    dv.wait_ge(small, chain.count + chain.per - chain.left)
                    dv.tensor_tensor(gate[:, :, :], one[0][:, :, :], one[1][:, :, :], ALU.add).then_inc(gate_ready, 1)

                def group(g):
                    chain.turn(g)
                    after(dv, turned, TURNS * g)
                    nodes = lambda g, j: k.x[:, bass.ds(g * GT + j, 1), :]
                    normalise(dv, g, nodes, s, t)
                    if second:
                        dv.wait_ge(s.normed_ready, g * GT + GT)
                        normalise(dv, g, lambda g, j: t.normed[:, j, :], s2, t2)
                    dv.wait_ge(multiplied, SMALL * g + 1)
                    dv.tensor_tensor(logits[:, :, :], pS[0][:, 0:GT * NE].rearrange("p (t e) -> p t e", t=GT),
                                     spread(br[:, :], 1, GT), ALU.add).then_inc(taken, 1)
                    dv.wait_ge(taken, SMALL * g + 1)
                    (two_best if second else softmax)(g)
                    if not second:
                        chain.left -= 1
                        dv.tensor_copy(top[:, :], total[:, :]).then_inc(small, 1)
                    assert chain.left == 0, chain.left
                    for j in range(GT):
                        dv.wait_ge(multiplied, SMALL * g + 2 + j)
                        dv.tensor_copy(y[:, j, :], pS[(1 + j) % 2][:, 0:C]).then_inc(taken, 1)
                    for e in range(NE):
                        for j in range(GT):
                            n = 1 + GT + e * GT + j
                            dv.wait_ge(multiplied, SMALL * g + n + 1)
                            dv.wait_ge(taken, SMALL * g + n - GT + 1)
                            dv.scalar_tensor_tensor(out=y[:, j, :], in0=pS[n % 2][:, 0:C], scalar=gate[:, j, e:e + 1], in1=y[:, j, :],
                                                    op0=ALU.mult, op1=ALU.add).then_inc(taken, 1)
                    dv.wait_ge(taken, SMALL * g + SMALL)
                    nodes = k.x[:, bass.ds(g * GT, GT), :]
                    dv.tensor_tensor(nodes, nodes, y[:, :, :], ALU.add).then_inc(done, 1)
                loop(dv, NG, group)

            @block.scalar
            def _(ac):
                ac.wait_ge(loaded, 16 * LOADS)
                if not second:
                    ac.wait_ge(fold, 4)

                def group(g):
                    for j in range(GT):
                        ac.wait_ge(turned, TURNS * g + j + 1)
                        after(ac, wide_ready, WIDE * g)
                        for c in range(KC):
                            if second:
                                ins = ac.activation(hT[:, c, j * P:(j + 1) * P], pT[j % 2][:, c, :], ACT.Identity,
                                                    bias=shift[:, c:c + 1], scale=gain[:, c:c + 1])
                            else:
                                ins = ac.copy(hT[:, c, j * P:(j + 1) * P], pT[j % 2][:, c, :])
                        ins.then_inc(kept, 1)
                    for what, layer, e in plan:
                        if what == "hidden":
                            for m in range(MC):
                                n = nth[layer, e, m]
                                ac.wait_ge(wide_ready, WIDE * g + n + 1)
                                if layer < layers - 1:
                                    after(ac, wide_ready, WIDE * g + nth[layer + 1, e - 2, MC - 1] + 1 if e >= 2
                                          else WIDE * (g - 1) + nth[layer + 1, NE - 2 + e, MC - 1] + 1)
                                else:
                                    after(ac, multiplied, SMALL * g + 1 + GT + (e - 1) * GT if e >= 2
                                          else SMALL * (g - 1) + 1 + GT + (NE - 1 + e) * GT)
                                to = act[layer][:, e % 2, m, :].rearrange("p (a b) -> p a b", a=2)
                                if second:
                                    ac.activation(to, pW[n % 2][:, :, 0:HALF], ACT.Gelu,
                                                  bias=offset[:, 0, m * NE + e:m * NE + e + 1]).then_inc(act_ready, 1)
                                else:
                                    ac.activation(to, pW[n % 2][:, :, 0:HALF], ACT.Relu,
                                                  bias=offset[:, layer, m * NE + e:m * NE + e + 1],
                                                  scale=scale[:, layer, m * NE + e:m * NE + e + 1]).then_inc(act_ready, 1)
                        elif what == "gates":
                            ac.wait_ge(shifted_ready, g + 1)
                            n = 1 if second else NE
                            ac.activation(odds[:, :, 0:n], shifted[:, :, 0:n], ACT.Exp).then_inc(odds_ready, 1)
                            for q in range(3):
                                i = GT + q
                                tiles = 2 if q < 2 else 1
                                ac.wait_ge(turned, TURNS * g + i + 1)
                                after(ac, multiplied, SMALL * g - GT * NE)
                                ac.copy(gateT[:, q * 2 * P:(q * 2 + tiles) * P].rearrange("e (t n) -> e t n", n=P),
                                        pT[i % 2][0:NE, 0:tiles, :]).then_inc(kept, 1)
                loop(ac, NG, group)

            @block.tensor
            def _(pe):
                pe.wait_ge(loaded, 16 * LOADS)

                def group(g):
                    for j in range(GT):
                        pe.wait_ge(s2.normed_ready, g * GT + j + 1)
                        after(pe, kept, TURNS * g + j - 1)
                        for c in range(KC):
                            ins = pe.transpose(pT[j % 2][:, c, :], t2.normed[:, j, c * P:(c + 1) * P], k.ident[:, :])
                        ins.then_inc(turned, 1)
                    pe.wait_ge(kept, TURNS * g + GT)
                    after(pe, taken, SMALL * g - 1)
                    for j in range(GT):
                        for c in range(KC):
                            ins = pe.matmul(pS[0][:, j * NE:(j + 1) * NE], hT[:, c, j * P:(j + 1) * P], wr[:, c, :],
                                            start=c == 0, stop=c == KC - 1)
                    ins.then_inc(multiplied, 1)
                    for what, layer, e in plan:
                        if what == "hidden":
                            if layer:
                                pe.wait_ge(act_ready, WIDE * g + nth[layer - 1, e, MC - 1] + 1)
                            weights = w2 if layer else w1
                            for m in range(MC):
                                n = nth[layer, e, m]
                                after(pe, act_ready, WIDE * g + n - 1)
                                for half in range(2):
                                    span = slice(half * HALF, (half + 1) * HALF)
                                    for c in range(KC):
                                        moving = act[0][:, e % 2, c, span] if layer else hT[:, c, span]
                                        ins = pe.matmul(pW[n % 2][:, half, 0:HALF], weights[:, e, c, m * P:(m + 1) * P], moving,
                                                        start=c == 0, stop=c == KC - 1)
                                ins.then_inc(wide_ready, 1)
                        elif what == "gates":
                            pe.wait_ge(gate_ready, g + 1)
                            for q in range(3):
                                i = GT + q
                                after(pe, kept, TURNS * g + i - 1)
                                for j in range(2 * q, min(2 * q + 2, GT)):
                                    ins = pe.transpose(pT[i % 2][0:NE, j % 2, :], gate[:, j, :], k.ident[:, :])
                                ins.then_inc(turned, 1)
                            pe.wait_ge(kept, TURNS * g + TURNS)
                            for j in range(GT):
                                n = 1 + j
                                after(pe, taken, SMALL * g + n - 1)
                                pe.matmul(pS[n % 2][:, 0:C], gateT[:, j * P:(j + 1) * P], bo[:, :], start=True,
                                          stop=True).then_inc(multiplied, 1)
                        else:
                            pe.wait_ge(act_ready, WIDE * g + nth[layers - 1, e, MC - 1] + 1)
                            for j in range(GT):
                                n = 1 + GT + e * GT + j
                                after(pe, taken, SMALL * g + n - 1)
                                for m in range(MC):
                                    ins = pe.matmul(pS[n % 2][:, 0:C], act[layers - 1][:, e % 2, m, j * P:(j + 1) * P], wo[:, e, m, :],
                                                    start=m == 0, stop=m == MC - 1)
                                ins.then_inc(multiplied, 1)
                loop(pe, NG, group)


EP = 125
EJ = EDGES // EP
GB = 8


def project_second(nc, k, a):
    HK = 2 * HM
    ZW = C + 2 * H1
    W = ZW + HK * DM
    PAIRS = HM * DM // P
    with ExitStack() as ctx:
        sb, ps, sem = scope(nc, ctx, "project_second")
        t, s = norm_tensors(sb, sem)
        w = sb("w", [P, KC, W])
        natural = sb("natural", [P, KC, C])
        vectors = sb("vectors", [P, KC, 2 * H1])
        xT = sb("xT", [P, 2, KC, P])
        outs = sb("outs", [P, 2, ZW])
        total = sb("total", [P, HK])
        mean = sb("mean", [P, HK])
        centred = sb("centred", [P, 2, HK, DM])
        square = sb("square", [P, HK, DM])
        var = sb("var", [P, HK])
        vareps = sb("vareps2", [P, HK])
        rstd = sb("rstd2", [P, HK])
        factor = sb("factor", [P, 2, HK])
        kv = sb("kv", [P, 2, HK * DM])
        zeros = sb("zeros", [P, 512])
        pT = ps("pT", [P, KC, P])
        pM = [ps(f"pM{i}", [P, 3, 512]) for i in range(2)]
        pD = ps("pD", [P, PAIRS, P])
        loaded, folded, fold_kept, zeroed = sem("loaded"), sem("folded"), sem("fold_kept"), sem("zeroed")
        xT_psum, xT_ready, xT_kept, projected = sem("xT_psum"), sem("xT_ready"), sem("xT_kept"), sem("projected")
        z_ready, summed, mean_ready, centred_ready = sem("z_ready"), sem("summed"), sem("mean_ready"), sem("centred_ready")
        squared, var_ready, vareps_ready, rstd_ready = sem("squared"), sem("var_ready"), sem("vareps2_ready"), sem("rstd2_ready")
        factor_ready, kv_ready, dots_done, cleared = sem("factor_ready"), sem("kv_ready"), sem("dots_done"), sem("cleared")
        kept = sem("kept")
        stored = [sem("stored0"), sem("stored1")]

        def running(g, j, back):
            return j >= back or not isinstance(g, int)

        with nc.Block() as block:
            @block.sync
            def _(sp):
                for n in range(KC):
                    rows = slice(n * P, (n + 1) * P)
                    sp.dma_start(w[:, n, 0:C], a["w_z1"][rows, :]).then_inc(loaded, 16)
                    sp.dma_start(w[:, n, ZW:W], a["w_mixkv"][rows, :]).then_inc(loaded, 16)
                    sp.dma_start(natural[:, n, :], a["w_natural1"][rows, :]).then_inc(loaded, 16)
                    sp.dma_start(vectors[:, n, :], a["vectors1"][rows, :]).then_inc(loaded, 16)

                def group(g):
                    for j in range(GT):
                        n, u = g * GT + j, j % 2
                        sp.wait_ge(z_ready, n + 1)
                        rows = bass.ds(n * P, P)
                        sp.dma_start(k.z_table[rows, :], outs[:, u, 0:C]).then_inc(stored[u], 16)
                        sp.dma_start(k.es_table1[rows, :], outs[:, u, C:C + H1]).then_inc(stored[u], 16)
                        sp.dma_start(k.ed_table1[rows, :], outs[:, u, C + H1:ZW]).then_inc(stored[u], 16)
                loop(sp, NG, group)
                for u in range(2):
                    sp.wait_ge(stored[u], 48 * USES[u] * NG)

            @block.gpsimd
            def _(pool):
                pool.memset(zeros[:, :], 0.0).then_inc(zeroed, 1)

                def scale(n, u, j):
                    pool.wait_ge(vareps_ready, n + 1)
                    pool.tensor_tensor(rstd[:, :], vareps[:, :], k.power[:, 0:HK], ALU.pow).then_inc(rstd_ready, 1)
                    pool.wait_ge(factor_ready, n + 1)
                    after(pool, dots_done, n - BEHIND[j] + 1)
                    pool.tensor_tensor(kv[:, u, :].rearrange("p (h d) -> p h d", h=HK), centred[:, u, :, :],
                                       spread(factor[:, u, :], 2, DM), ALU.mult).then_inc(kv_ready, 1)

                def group(g):
                    deviations(pool, g, k, s, t)
                    for j in range(GT):
                        if running(g, j, 1):
                            i = (j - 1) % GT
                            scale(g * GT + j - 1, i % 2, i)
                loop(pool, NG, group)
                scale(NT - 1, (GT - 1) % 2, GT - 1)

            @block.vector
            def _(dv):
                dv.memset(k.dots[:, :, :], 0.0).then_inc(cleared, 1)
                dv.wait_ge(folded, 1)
                dv.tensor_copy(w[:, :, C:ZW], pT[:, :, 0:2 * H1]).then_inc(fold_kept, 1)

                def centre(n, u, j):
                    heads = pM[u][:, 1:3, :].rearrange("p b (h d) -> p (b h) d", d=DM)
                    dv.wait_ge(projected, 2 * n + 2)
                    dv.tensor_reduce(total[:, :], heads, AX, ALU.add).then_inc(summed, 1)
                    dv.wait_ge(summed, n + 1)
                    dv.tensor_scalar(mean[:, :], total[:, :], 1.0 / DM, None, ALU.mult).then_inc(mean_ready, 1)
                    dv.wait_ge(mean_ready, n + 1)
                    after(dv, kv_ready, n - BEHIND[j] + 1)
                    dv.tensor_tensor(centred[:, u, :, :], heads, spread(mean[:, :], 2, DM), ALU.subtract).then_inc(centred_ready, 1)

                def deviate(n, u):
                    dv.wait_ge(squared, n + 1)
                    dv.tensor_reduce(var[:, :], square[:, :, :], AX, ALU.add).then_inc(var_ready, 1)
                    dv.wait_ge(var_ready, n + 1)
                    dv.tensor_scalar(vareps[:, :], var[:, :], 1.0 / DM, 1e-5, ALU.mult, ALU.add).then_inc(vareps_ready, 1)
                    dv.wait_ge(rstd_ready, n + 1)
                    dv.tensor_copy(factor[:, u, 0:HM], rstd[:, 0:HM])
                    dv.tensor_scalar(factor[:, u, HM:HK], rstd[:, HM:HK], k.share[:, bass.ds(n, 1)], None,
                                     ALU.mult).then_inc(factor_ready, 1)

                def group(g):
                    after(dv, xT_psum, GT * g)
                    normalise(dv, g, lambda g, j: k.x[:, bass.ds(g * GT + j, 1), :], s, t)
                    for j in range(GT):
                        n = g * GT + j
                        if running(g, j, 1) and j == 0:
                            deviate(n - 1, (GT - 1) % 2)
                        centre(n, j % 2, j)
                        if j > 0:
                            deviate(n - 1, (j - 1) % 2)
                loop(dv, NG, group)
                deviate(NT - 1, (GT - 1) % 2)
                dv.wait_ge(dots_done, NT)
                dv.wait_ge(cleared, 1)
                for lo in (0, DM):
                    dv.tensor_copy(k.dots[lo:lo + DM, :, lo:lo + DM], pD[lo:lo + DM, :, lo:lo + DM]).then_inc(kept, 1)

            @block.scalar
            def _(ac):
                ac.wait_ge(fold_kept, 1)

                def keep(n, j):
                    u = j % 2
                    ac.wait_ge(xT_psum, n + 1)
                    after(ac, projected, 2 * (n - BEHIND[j] + 1))
                    ac.copy(xT[:, u, :, :], pT[:, :, :]).then_inc(xT_ready, 1)
                    ac.wait_ge(xT_ready, n + 1)
                    ac.copy(k.xn[:, bass.ds(n, 1), :], xT[:, u:u + 1, :, :].rearrange("p a c n -> p a (c n)")).then_inc(xT_kept, 1)

                def squares(n, u):
                    ac.wait_ge(centred_ready, n + 1)
                    after(ac, var_ready, n)
                    ac.activation(square[:, :, :], centred[:, u, :, :], ACT.Square).then_inc(squared, 1)

                def group(g):
                    keep(g * GT, 0)
                    for j in range(GT):
                        n, u = g * GT + j, j % 2
                        if j + 1 < GT:
                            keep(n + 1, j + 1)
                        if running(g, j, 1):
                            squares(n - 1, (j - 1) % GT % 2)
                        ac.wait_ge(projected, 2 * n + 1)
                        after(ac, stored[u], 48 * uses(g, j))
                        ac.copy(outs[:, u, :], pM[u][:, 0, 0:ZW]).then_inc(z_ready, 1)
                loop(ac, NG, group)
                squares(NT - 1, (GT - 1) % 2)

            @block.tensor
            def _(pe):
                pe.wait_ge(loaded, 128)
                for m in range(KC):
                    for c in range(KC):
                        ins = pe.matmul(pT[:, m, 0:2 * H1], natural[:, c, m * P:(m + 1) * P], vectors[:, c, :],
                                        start=c == 0, stop=c == KC - 1)
                ins.then_inc(folded, 1)
                pe.wait_ge(zeroed, 1)
                pe.matmul(pD[:, :, :], zeros[:, 0:P], zeros[:, :], start=True, stop=False, skip_group_check=True)
                pe.wait_ge(fold_kept, 1)

                def turn(n, j):
                    pe.wait_ge(s.normed_ready, n + 1)
                    after(pe, xT_ready, n)
                    for c in range(KC):
                        ins = pe.transpose(pT[:, c, :], t.normed[:, j, c * P:(c + 1) * P], k.ident[:, :])
                    ins.then_inc(xT_psum, 1)

                def dots(n, u):
                    pe.wait_ge(kv_ready, n + 1)
                    for m in range(PAIRS):
                        ins = pe.matmul(pD[:, m, :], kv[:, u, HM * DM + m * P:HM * DM + (m + 1) * P], kv[:, u, m * P:(m + 1) * P],
                                        start=False, stop=False, skip_group_check=True)
                    ins.then_inc(dots_done, 1)

                def group(g):
                    turn(g * GT, 0)
                    for j in range(GT):
                        n, u = g * GT + j, j % 2
                        if j + 1 < GT:
                            turn(n + 1, j + 1)
                        pe.wait_ge(xT_ready, n + 1)
                        for b, (lo, hi) in enumerate(((0, ZW), (ZW, ZW + 512), (ZW + 512, W))):
                            if b < 2:
                                after(pe, (z_ready, centred_ready)[b], n - BEHIND[j] + 1)
                            for q in range(KC):
                                ins = pe.matmul(pM[u][:, b, 0:hi - lo], xT[:, u, q, :], w[:, q, lo:hi], start=q == 0, stop=q == KC - 1)
                            if b != 1:
                                ins.then_inc(projected, 1)
                        if running(g, j, 2):
                            dots(n - 2, (j - 2) % GT % 2)
                loop(pe, NG, group)
                dots(NT - 2, (GT - 2) % 2)
                dots(NT - 1, (GT - 1) % 2)


def mix_second(nc, k, a):
    PAIRS = HM * DM // P
    with ExitStack() as ctx:
        sb, ps, sem = scope(nc, ctx, "mix_second")
        wq = sb("wq", [P, PAIRS, C])
        wo = sb("wo", [P, PAIRS, C])
        bias = sb("bias", [1, C])
        inner = sb("inner", [P, PAIRS, C])
        whole = sb("whole", [P, KC, C])
        xT = sb("xT", [P, 2, KC, P])
        pG = ps("pG", [P, PAIRS, C])
        pW = ps("pW", [P, KC, C])
        pO = [ps(f"pO{i}", [P, C]) for i in range(2)]
        loaded, inner_psum, inner_ready, whole_psum = sem("loaded"), sem("inner_psum"), sem("inner_ready"), sem("whole_psum")
        whole_ready, xT_ready, projected, done = sem("whole_ready"), sem("xT_ready"), sem("projected"), sem("done")

        with nc.Block() as block:
            @block.sync
            def _(sp):
                sp.dma_start(wq[:, :, :], a["w_mixq"].rearrange("(c p) n -> p c n", p=P)).then_inc(loaded, 16)
                sp.dma_start(wo[:, :, :], a["w_mixout"].rearrange("(c p) n -> p c n", p=P)).then_inc(loaded, 16)
                sp.dma_start(bias[:, :], a["b_mixout"]).then_inc(loaded, 16)

            @block.vector
            def _(dv):
                def group(g):
                    for j in range(GT):
                        n, u = g * GT + j, j % 2
                        dv.wait_ge(projected, n + 1)
                        nodes = k.x[:, bass.ds(n, 1), :]
                        dv.tensor_tensor(nodes, nodes, pO[u].rearrange("p (a c) -> p a c", a=1), ALU.add).then_inc(done, 1)
                loop(dv, NG, group)

            @block.scalar
            def _(ac):
                ac.wait_ge(inner_psum, 1)
                ac.copy(inner[:, :, :], pG[:, :, :]).then_inc(inner_ready, 1)
                ac.wait_ge(whole_psum, 1)
                ac.copy(whole[:, :, :], pW[:, :, :]).then_inc(whole_ready, 1)

                def group(g):
                    for j in range(GT):
                        n, u = g * GT + j, j % 2
                        after(ac, projected, n - BEHIND[j] + 1)
                        ac.copy(xT[:, u:u + 1, :, :].rearrange("p a c n -> p a (c n)"), k.xn[:, bass.ds(n, 1), :]).then_inc(xT_ready, 1)
                loop(ac, NG, group)

            @block.tensor
            def _(pe):
                pe.wait_ge(loaded, 48)
                for m in range(PAIRS):
                    ins = pe.matmul(pG[:, m, :], k.dots[:, m, :], wo[:, m, :], start=True, stop=True)
                ins.then_inc(inner_psum, 1)
                pe.wait_ge(inner_ready, 1)
                for m in range(KC):
                    for c in range(PAIRS):
                        ins = pe.matmul(pW[:, m, :], wq[:, c, m * P:(m + 1) * P], inner[:, c, :], start=c == 0, stop=c == PAIRS - 1)
                ins.then_inc(whole_psum, 1)
                pe.wait_ge(whole_ready, 1)

                def group(g):
                    for j in range(GT):
                        n, u = g * GT + j, j % 2
                        pe.wait_ge(xT_ready, n + 1)
                        after(pe, done, n - BEHIND[j] + 1)
                        pe.matmul(pO[u][:, :], k.ones[0:1, :], bias[:, :], start=True, stop=False)
                        for c in range(KC):
                            ins = pe.matmul(pO[u][:, :], xT[:, u, c, :], whole[:, c, :], start=False, stop=c == KC - 1)
                        ins.then_inc(projected, 1)
                loop(pe, NG, group)


def edge_odds(nc, k, a, H, es_table, ed_table, ex_table):
    stage = f"odds{H}"
    NBG = EJ // GB
    with ExitStack() as ctx:
        sb, ps, sem = scope(nc, ctx, stage)
        src = sb("src", [EP, EJ], I32)
        dst = sb("dst", [EP, EJ], I32)
        index = sb("index", [EP, 2, 2, GB], I32)
        got = sb("got", [EP, 2, 2, GB, H])
        e = sb("e", [EP, EJ, H])
        le = sb("le", [EP, EJ, H])
        forth = sb("forth", [EP, EJ, H])
        back = sb("back", [EP, EJ, H])
        seg = sb("seg", [EP, EJ])
        enter = sb("enter", [EP, EJ])
        leave = sb("leave", [EP, EJ])
        other = sb("other", [EP, 2, EJ])
        NCOL = 2 + 2 * H
        diag = sb("diag", [EP, NCOL, P])
        lines = sb("lines", [EP, NCOL, P])
        barred = sb("barred", [EP, 2, 2, P])
        parts = sb("parts", [EP, 2, 2, H, P])
        ends = sb("ends", [EP, 2, 2, H])
        end = sb("end", [EP, 2, H])
        odds = sb("odds", [EP, EJ, H])
        rows = sb("rows", [PB, 4, P * H])
        rest = sb("rest", [1, (EROWS * P - EDGES) * H])
        pL = ps("pL", [P, NCOL, P])
        pR = [ps(f"pR{i}", [P, 4, P]) for i in range(2)]
        edges_in, fence, index_ready, taken = sem("edges_in"), sem("fence"), sem("index_ready"), sem("taken")
        rows_in = [sem("rows_in0"), sem("rows_in1")]
        step, diag_ready, lines_psum, scores_less = sem("step"), sem("diag_ready"), sem("lines_psum"), sem("scores_less")
        odds_ready, stored, rest_set, pair_rows = sem("odds_ready"), sem("stored"), sem("rest_set"), sem("pair_rows")
        turned, kept, cleared, lines_ready = sem("turned"), sem("kept"), sem("cleared"), sem("lines_ready")

        with nc.Block() as block:
            @block.sync
            def _(sp):
                sp.dma_start(src[:, :], a["src"].rearrange("(p j) -> p j", p=EP)).then_inc(edges_in, 16)
                sp.dma_start(dst[:, :], a["dst"].rearrange("(p j) -> p j", p=EP)).then_inc(edges_in, 16)
                flat = ex_table.rearrange("a b -> (a b)")
                sp.wait_ge(odds_ready, 1)
                sp.dma_start(flat[0:EDGES * H].rearrange("(p j) -> p j", p=EP), odds.rearrange("p j h -> p (j h)")).then_inc(stored, 16)
                sp.wait_ge(rest_set, 1)
                sp.dma_start(flat[EDGES * H:EROWS * P * H].rearrange("(p j) -> p j", p=1), rest[:, :]).then_inc(stored, 16)
                sp.wait_ge(stored, 32)

            @block.gpsimd
            def _(pool):
                pool.memset(rest[:, :], 0.0).then_inc(rest_set, 1)
                pool.memset(k.odds[:, :, :], 0.0).then_inc(cleared, 1)
                pool.memset(k.sums[:, :, :], 0.0).then_inc(cleared, 1)
                pool.wait_ge(edges_in, 32)

                def steps(i):
                    for u in range(2):
                        b = 2 * i + u
                        after(pool, taken, b - 1)
                        pool.sem_inc(fence, 1)
                        pool.tensor_copy(index[:, u, 0, :], src[:, bass.ds(b * GB, GB)])
                        pool.tensor_copy(index[:, u, 1, :], dst[:, bass.ds(b * GB, GB)]).then_inc(index_ready, 1)
                        pool.wait_ge(index_ready, b + 1)
                        pool.sem_inc(fence, 1)
                        for n, table in enumerate((es_table, ed_table)):
                            for m in range(GB):
                                pool.indirect_dma_start(got[:, u, n, m, :], None, table,
                                                        bass.IndirectOffsetOnAxis(ap=index[:, u, n, m:m + 1], axis=0)).then_inc(rows_in[u], 16)
                loop(pool, NBG // 2, steps)
                pool.wait_ge(stored, 32)
                for b in range(4):
                    pool.indirect_dma_start(rows[:, b, :], None, ex_table,
                                            bass.IndirectOffsetOnAxis(ap=k.tile_i[:, b:b + 1], axis=0)).then_inc(pair_rows, 16)

            @block.vector
            def _(dv):
                chain = Chain(dv, step, 22)
                chain.turn(0)
                dv.wait_ge(edges_in, 32)
                chain(dv.tensor_copy(seg[:, :], dst[:, :]))
                chain(dv.tensor_tensor(leave[:, 0:EJ - 1], seg[:, 0:EJ - 1], seg[:, 1:EJ], ALU.is_equal))
                chain(dv.tensor_scalar(leave[:, 0:EJ - 1], leave[:, 0:EJ - 1], 1.0, BIG, ALU.subtract, ALU.mult))
                chain(dv.memset(leave[:, EJ - 1:EJ], -BIG))
                chain(dv.tensor_copy(enter[:, 1:EJ], leave[:, 0:EJ - 1]))
                chain(dv.memset(enter[:, 0:1], -BIG))
                for end_of in range(2):
                    at = (EJ - 1) * end_of
                    chain(dv.tensor_scalar(other[:, end_of, :], seg[:, :], seg[:, at:at + 1], 1.0, ALU.is_equal, ALU.subtract))
                chain(dv.tensor_scalar(other[:, :, :], other[:, :, :], BIG, None, ALU.mult))

                def steps(i):
                    for u in range(2):
                        b = 2 * i + u
                        dv.wait_ge(rows_in[u], 16 * 2 * GB * (i + 1))
                        dv.tensor_tensor(e[:, bass.ds(b * GB, GB), :], got[:, u, 0, :, :], got[:, u, 1, :, :], ALU.add).then_inc(taken, 1)
                loop(dv, NBG // 2, steps)
                dv.wait_ge(taken, NBG)
                chain(dv.scalar_tensor_tensor(out=le[:, :, :], in0=e[:, :, :], scalar=0.01, in1=e[:, :, :], op0=ALU.mult, op1=ALU.max))
                for h in range(H):
                    dv.tensor_tensor_scan(forth[:, :, h], enter[:, :], le[:, :, h], -BIG, ALU.add, ALU.max)
                    ins = dv.tensor_tensor_scan(backwards(back[:, :, h]), backwards(leave[:, :]), backwards(le[:, :, h]), -BIG,
                                                ALU.add, ALU.max)
                chain(ins)
                columns = [seg[:, 0:1], seg[:, EJ - 1:EJ]] + [back[:, 0, h:h + 1] for h in range(H)] + \
                    [forth[:, EJ - 1, h:h + 1] for h in range(H)]
                for n, column in enumerate(columns):
                    ins = dv.tensor_scalar(diag[:, n, :], k.ident[0:EP, :], column, None, ALU.mult)
                ins.then_inc(diag_ready, 1)
                dv.wait_ge(lines_psum, 1)
                chain(dv.tensor_tensor(forth[:, :, :], forth[:, :, :], back[:, :, :], ALU.max))
                chain(dv.tensor_copy(lines[:, :, :], pL[0:EP, :, :]))
                for end_of in range(2):
                    at = (EJ - 1) * end_of
                    ins = dv.tensor_scalar(barred[:, end_of, :, 0:EP], lines[:, 0:2, 0:EP], seg[:, at:at + 1], 1.0, ALU.is_equal, ALU.subtract)
                chain(ins)
                chain(dv.tensor_scalar(barred[:, :, :, 0:EP], barred[:, :, :, 0:EP], BIG, None, ALU.mult))
                for end_of in range(2):
                    ins = dv.tensor_tensor(parts[:, end_of, :, :, 0:EP], spread(barred[:, end_of, :, 0:EP], 2, H),
                                           lines[:, 2:NCOL, 0:EP].rearrange("p (w h) n -> p w h n", w=2), ALU.add)
                chain(ins)
                for end_of in range(2):
                    ins = dv.tensor_reduce(ends[:, end_of, :, :], parts[:, end_of, :, :, 0:EP], AX, ALU.max)
                chain(ins)
                chain(dv.tensor_tensor(end[:, :, :], ends[:, :, 0, :], ends[:, :, 1, :], ALU.max))
                for end_of in range(2):
                    chain(dv.tensor_tensor(back[:, :, :], spread(other[:, end_of, :], 2, H), spread(end[:, end_of, :], 1, EJ), ALU.add))
                    chain(dv.tensor_tensor(forth[:, :, :], forth[:, :, :], back[:, :, :], ALU.max))
                dv.tensor_tensor(le[:, :, :], le[:, :, :], forth[:, :, :], ALU.subtract).then_inc(scores_less, 1)
                dv.wait_ge(cleared, 2)
                for n in range(H):
                    dv.wait_ge(turned, n + 1)
                    dv.tensor_copy(k.odds[:, 0:NP, n].rearrange("p (b n) -> p b n", b=4), pR[n % 2][:, :, 0:PB]).then_inc(kept, 1)

            @block.scalar
            def _(ac):
                ac.wait_ge(scores_less, 1)
                ac.activation(odds[:, :, :], le[:, :, :], ACT.Exp).then_inc(odds_ready, 1)

            @block.tensor
            def _(pe):
                pe.wait_ge(diag_ready, 1)
                for n in range(NCOL):
                    ins = pe.matmul(pL[:, n, :], k.ones[0:EP, :], diag[:, n, :], start=True, stop=True)
                ins.then_inc(lines_psum, 1)
                pe.wait_ge(pair_rows, 64)
                for h in range(H):
                    after(pe, kept, h - 1)
                    for b in range(4):
                        ins = pe.transpose(pR[h % 2][:, b, 0:PB], rows[:, b, :].rearrange("p (n h) -> p n h", h=H)[:, :, h],
                                           k.ident[0:PB, 0:PB])
                    ins.then_inc(turned, 1)


def backwards(ap):
    (partitions, lanes), (stride, n) = [list(x) for x in ap.ap]
    return bass.AP(tensor=ap.tensor, offset=ap.offset + (n - 1) * stride, ap=[[partitions, lanes], [-stride, n]])


def edge_sums(nc, k, H, table):
    W = C + H
    with ExitStack() as ctx:
        sb, ps, sem = scope(nc, ctx, f"sums{H}")
        t, s = Core(), Core()
        t.index = sb("index", [P, 2, BATCH], I32)
        t.rows = sb("rows", [P, 2, BATCH, C])
        t.hot = sb("hot", [P, 2, BATCH, P])
        t.weighted = sb("weighted", [P, 2, BATCH, SW])
        t.p_sum = ps("p_sum", [P, BATCH, 512])
        s.fence, s.index_ready, s.hot_ready, s.weights_ready = sem("fence"), sem("index_ready"), sem("hot_ready"), sem("weights_ready")
        s.weighted_ready, s.summed, s.added = sem("weighted_ready"), sem("summed"), sem("added")
        s.rows_in = [sem("rows_in0"), sem("rows_in1")]

        with nc.Block() as block:
            @block.gpsimd
            def _(pool):
                loop(pool, NB // 2, lambda i: edge_gather(pool, i, k, t, s, table, s.weighted_ready))
                for u in range(2):
                    pool.wait_ge(s.rows_in[u], 16 * BATCH * NB // 2)

            @block.tensor
            def _(pe):
                def steps(i):
                    for u in range(2):
                        pe.wait_ge(s.hot_ready, 2 * i + u + 1)
                        pe.wait_ge(s.weights_ready, 2 * i + u + 1)
                        edge_sum(pe, 2 * i + u, u, t, s, W)
                loop(pe, NB // 2, steps)

            @block.scalar
            def _(ac):
                def steps(i):
                    for u in range(2):
                        b = 2 * i + u
                        after(ac, s.summed, b - 1)
                        ac.copy(t.weighted[:, u, :, C:W], k.odds[:, bass.ds(b * BATCH, BATCH), 0:H]).then_inc(s.weights_ready, 1)
                loop(ac, NB // 2, steps)

            @block.vector
            def _(dv):
                def steps(i):
                    for u in range(2):
                        b = 2 * i + u
                        edge_hot(dv, b, u, k, t, s)
                        dv.wait_ge(s.rows_in[u], (i + 1) * 16 * BATCH)
                        dv.tensor_tensor(t.weighted[:, u, :, 0:C].rearrange("p m (h d) -> p m h d", h=H),
                                         t.rows[:, u, :, :].rearrange("p m (h d) -> p m h d", h=H),
                                         spread(k.odds[:, bass.ds(b * BATCH, BATCH), 0:H], 3, C // H), ALU.mult).then_inc(s.weighted_ready, 1)
                        if u or not isinstance(i, int):
                            edge_add(dv, b - 1, k, t, s, W)
                loop(dv, NB // 2, steps)
                edge_add(dv, NB - 1, k, t, s, W)


def between_second(nc, k, a):
    ZW = C + 2
    with ExitStack() as ctx:
        sb, ps, sem = scope(nc, ctx, "between")
        w = sb("w", [P, KC, ZW])
        natural = sb("natural", [P, KC, C])
        vectors = sb("vectors", [P, KC, 2])
        den = sb("den", [P, GT, H1])
        mean = sb("mean", [P, GT, C])
        below = sb("below", [P, GT, C])
        grown = sb("grown", [P, GT, C])
        hidden = sb("hidden", [P, GT, C])
        hT = sb("hT", [P, 2, KC, P])
        outs = sb("outs", [P, 2, ZW])
        pT = [ps(f"pT{i}", [P, KC, P]) for i in range(2)]
        pM = [ps(f"pM{i}", [P, ZW]) for i in range(2)]
        loaded, folded, fold_kept, small = sem("loaded"), sem("folded"), sem("fold_kept"), sem("small")
        mean_ready, below_ready, grown_ready, above_ready = sem("mean_ready"), sem("below_ready"), sem("grown_ready"), sem("above_ready")
        hidden_ready, turned, kept, projected, z_ready = sem("hidden_ready"), sem("turned"), sem("kept"), sem("projected"), sem("z_ready")
        stored = [sem("stored0"), sem("stored1")]

        with nc.Block() as block:
            @block.sync
            def _(sp):
                for n in range(KC):
                    rows = slice(n * P, (n + 1) * P)
                    sp.dma_start(w[:, n, 0:C], a["w_z2"][rows, :]).then_inc(loaded, 16)
                    sp.dma_start(natural[:, n, :], a["w_natural2"][rows, :]).then_inc(loaded, 16)
                    sp.dma_start(vectors[:, n, :], a["vectors2"][rows, :], allow_slow_non_contiguous=True).then_inc(loaded, 16)

                def group(g):
                    for j in range(GT):
                        n, u = g * GT + j, j % 2
                        sp.wait_ge(z_ready, n + 1)
                        rows = bass.ds(n * P, P)
                        sp.dma_start(k.z_table[rows, :], outs[:, u, 0:C]).then_inc(stored[u], 16)
                        sp.dma_start(k.es_table2[rows, :], outs[:, u, C:C + 1]).then_inc(stored[u], 16)
                        sp.dma_start(k.ed_table2[rows, :], outs[:, u, C + 1:ZW]).then_inc(stored[u], 16)
                loop(sp, NG, group)
                for u in range(2):
                    sp.wait_ge(stored[u], 48 * USES[u] * NG)

            @block.vector
            def _(dv):
                dv.wait_ge(folded, 1)
                dv.tensor_copy(w[:, :, C:ZW], pT[0][:, :, 0:2]).then_inc(fold_kept, 1)

                def group(g):
                    sums = k.sums[:, bass.ds(g * GT, GT), :]
                    dv.tensor_scalar(den[:, :, :], sums[:, :, C:C + H1], 1e-30, None, ALU.max).then_inc(small, 1)
                    dv.wait_ge(small, 2 * g + 1)
                    dv.reciprocal(den[:, :, :], den[:, :, :]).then_inc(small, 1)
                    dv.wait_ge(small, 2 * g + 2)
                    dv.tensor_tensor(mean[:, :, :].rearrange("p t (h d) -> p t h d", h=H1),
                                     sums[:, :, 0:C].rearrange("p t (h d) -> p t h d", h=H1),
                                     spread(den[:, :, :], 3, D1), ALU.mult).then_inc(mean_ready, 1)
                    dv.wait_ge(mean_ready, g + 1)
                    dv.tensor_scalar(below[:, :, :], mean[:, :, :], 0.0, None, ALU.min).then_inc(below_ready, 1)
                    dv.tensor_scalar(mean[:, :, :], mean[:, :, :], 0.0, None, ALU.max).then_inc(above_ready, 1)
                    dv.wait_ge(above_ready, g + 1)
                    dv.wait_ge(grown_ready, g + 1)
                    after(dv, turned, GT * g)
                    dv.scalar_tensor_tensor(out=hidden[:, :, :], in0=grown[:, :, :], scalar=-1.0, in1=mean[:, :, :],
                                            op0=ALU.add, op1=ALU.add).then_inc(hidden_ready, 1)
                    for j in range(GT):
                        n, u = g * GT + j, j % 2
                        dv.wait_ge(projected, n + 1)
                        after(dv, stored[u], 48 * uses(g, j))
                        dv.tensor_copy(outs[:, u, :], pM[u][:, :]).then_inc(z_ready, 1)
                loop(dv, NG, group)

            @block.scalar
            def _(ac):
                ac.wait_ge(fold_kept, 1)

                def group(g):
                    ac.wait_ge(below_ready, g + 1)
                    after(ac, hidden_ready, g)
                    ac.activation(grown[:, :, :], below[:, :, :], ACT.Exp).then_inc(grown_ready, 1)
                    for j in range(GT):
                        n, u = g * GT + j, j % 2
                        ac.wait_ge(turned, n + 1)
                        after(ac, projected, n - BEHIND[j] + 1)
                        ac.copy(hT[:, u, :, :], pT[u][:, :, :]).then_inc(kept, 1)
                loop(ac, NG, group)

            @block.tensor
            def _(pe):
                pe.wait_ge(loaded, 96)
                for m in range(KC):
                    for c in range(KC):
                        ins = pe.matmul(pT[0][:, m, 0:2], natural[:, c, m * P:(m + 1) * P], vectors[:, c, :],
                                        start=c == 0, stop=c == KC - 1)
                ins.then_inc(folded, 1)
                pe.wait_ge(fold_kept, 1)

                def group(g):
                    pe.wait_ge(hidden_ready, g + 1)
                    for j in range(GT):
                        n, u = g * GT + j, j % 2
                        after(pe, kept, n - BEHIND[j] + 1)
                        for c in range(KC):
                            ins = pe.transpose(pT[u][:, c, :], hidden[:, j, c * P:(c + 1) * P], k.ident[:, :])
                        ins.then_inc(turned, 1)
                        pe.wait_ge(kept, n + 1)
                        after(pe, z_ready, n - BEHIND[j] + 1)
                        for c in range(KC):
                            ins = pe.matmul(pM[u][:, :], hT[:, u, c, :], w[:, c, :], start=c == 0, stop=c == KC - 1)
                        ins.then_inc(projected, 1)
                loop(pe, NG, group)


def end_second(nc, k):
    with ExitStack() as ctx:
        sb, ps, sem = scope(nc, ctx, "end_second")
        den = sb("den", [P, NT, 1])
        step = sem("step")
        with nc.Block() as block:
            @block.vector
            def _(dv):
                chain = Chain(dv, step, 4)
                chain.turn(0)
                chain(dv.tensor_scalar(den[:, :, :], k.sums[:, :, C:C + 1], 1e-30, None, ALU.max))
                chain(dv.reciprocal(den[:, :, :], den[:, :, :]))
                chain(dv.tensor_tensor(k.sums[:, :, 0:C], k.sums[:, :, 0:C], spread(den[:, :, 0], 2, C), ALU.mult))
                chain(dv.tensor_tensor(k.x[:, :, :], k.x[:, :, :], k.sums[:, :, 0:C], ALU.add))


def store(nc, k, out):
    with ExitStack() as ctx:
        sb, ps, sem = scope(nc, ctx, "store")
        done = sem("done")
        with nc.Block() as block:
            @block.sync
            def _(sp):
                sp.dma_start(out[0:FULL * P, :].rearrange("(t p) c -> p t c", p=P), k.x[:, 0:FULL, :]).then_inc(done, 16)
                sp.dma_start(out[FULL * P:NODES, :], k.x[0:LAST, FULL, :]).then_inc(done, 16)
                sp.wait_ge(done, 32)


def program(nc, a, out):
    k = Core()
    with ExitStack() as ctx:
        sb, ps, sem = scope(nc, ctx, "kept")
        k.x = sb("x", [P, NT, C])
        k.ident = sb("ident", [P, P])
        k.lane = sb("lane", [P, P])
        k.ones = sb("ones", [P, P])
        k.power = sb("power", [P, 64])
        k.share = sb("share", [P, NT])
        k.src_pad = nc.dram_tensor("src_pad", (EROWS, P), I32).ap()
        k.dst_pad = nc.dram_tensor("dst_pad", (EROWS, P), I32).ap()
        k.win_dram = nc.dram_tensor("win_dram", (4, PB), I32).ap()
        k.kv_table = nc.dram_tensor("kv_table", (ROWS, 2 * C), F32).ap()
        k.mix_qkv = nc.dram_tensor("mix_qkv", (ROWS, 3 * C), F32).ap()
        k.z_table = nc.dram_tensor("z_table", (ROWS, C), F32).ap()
        k.es_table1 = nc.dram_tensor("es_table1", (ROWS, H1), F32).ap()
        k.ed_table1 = nc.dram_tensor("ed_table1", (ROWS, H1), F32).ap()
        k.es_table2 = nc.dram_tensor("es_table2", (ROWS, 1), F32).ap()
        k.ed_table2 = nc.dram_tensor("ed_table2", (ROWS, 1), F32).ap()
        k.ex_table1 = nc.dram_tensor("ex_table1", (EROWS, P * H1), F32).ap()
        k.ex_table2 = nc.dram_tensor("ex_table2", (EROWS, P), F32).ap()
        with ExitStack() as edges:
            sb, ps, sem = scope(nc, edges, "edges")
            k.xn = sb("xn", [P, NT, C])
            k.sums = sb("sums", [P, NT, SW])
            k.src = sb("src", [P, NPX], I32)
            k.rel = sb("rel", [P, NPX])
            k.win = sb("win", [1, NPX], I32)
            k.tile_i = sb("tile_i", [PB, 4], I32)
            k.odds = sb("odds", [P, NPX, H1])
            prepare(nc, k, a)
            with ExitStack() as first:
                sb, ps, sem = scope(nc, first, "first")
                k.node = sb("node", [P, NT, C])
                project_first(nc, k, a)
                attend_first(nc, k)
            with ExitStack() as mixing:
                sb, ps, sem = scope(nc, mixing, "mixing")
                k.mixed = sb("mixed", [P, FCH, SW])
                mix_keys(nc, k, a)
                mix_queries(nc, k, a)
            layer_first(nc, k, a)
            experts(nc, k, a, False)
            with ExitStack() as mixing:
                sb, ps, sem = scope(nc, mixing, "mixing_again")
                k.dots = sb("dots", [P, HM * DM // P, P])
                project_second(nc, k, a)
                mix_second(nc, k, a)
            edge_odds(nc, k, a, H1, k.es_table1, k.ed_table1, k.ex_table1)
            edge_sums(nc, k, H1, k.z_table)
            between_second(nc, k, a)
            edge_odds(nc, k, a, 1, k.es_table2, k.ed_table2, k.ex_table2)
            edge_sums(nc, k, 1, k.z_table)
            end_second(nc, k)
        experts(nc, k, a, True)
        store(nc, k, out)


def layout(v):
    c = np.ascontiguousarray

    def r(b):
        return c(np.reshape(b, (1, -1)))

    def columns(b):
        return c(np.reshape(b, (-1, P)).T)

    def by_expert(b):
        return c(np.reshape(b, (NE, -1, P)).transpose(2, 1, 0).reshape(P, -1))

    mix_w = v["L0_mix_Wqkv"].T
    mix_b = v["L0_mix_bqkv"]
    a1, a2 = v["L1_gnn_a1"], v["L1_gnn_a2"]
    vectors1 = np.zeros((C, 2 * H1), np.float32)
    for h in range(H1):
        vectors1[h * D1:(h + 1) * D1, h] = a1[h, :D1]
        vectors1[h * D1:(h + 1) * D1, H1 + h] = a1[h, D1:]
    w_z = np.reshape(v["L1_gnn_W1"], (C, C))
    w_qkv = v["L1_mix_w_qkv"]
    return {
        "x": c(v["x"]), "src": c(v["src"]), "dst": c(v["dst"]),
        "w_z1": c(w_z.T), "w_natural1": c(w_z), "vectors1": vectors1,
        "w_z2": c(v["L1_gnn_W2"].T), "w_natural2": c(v["L1_gnn_W2"]), "vectors2": c(np.stack([a2[:C], a2[C:]], axis=1)),
        "w_mixkv": c(w_qkv[:, HM * DM:]), "w_mixq": c(w_qkv[:, :HM * DM].T), "w_mixout": c(v["L1_mix_w_out"]),
        "b_mixout": r(v["L1_mix_b_out"]),
        "w_first": c(np.concatenate([v["L0_gnn_Wk"].T, v["L0_gnn_Wv"].T, v["L0_gnn_Wq"].T, mix_w[:, C:2 * C],
                                     mix_w[:, 2 * C:], mix_w[:, :C]], axis=1)),
        "b_first": r(np.concatenate([v["L0_gnn_bk"], v["L0_gnn_bv"], v["L0_gnn_bq"], mix_b[C:2 * C], mix_b[2 * C:],
                                     mix_b[:C]])),
        "w_mixproj": c(v["L0_mix_Wproj"].T), "b_mixproj": r(v["L0_mix_bproj"]), "temperature": r(v["L0_mix_temperature"]),
        "w_p": c(v["L0_gnn_Wp"].T), "b_p": r(v["L0_gnn_bp"]), "w_1": c(v["L0_gnn_W1"].T), "w_2": c(v["L0_gnn_W2"].T),
        "b_1": columns(v["L0_gnn_b1"]), "b_2": r(v["L0_gnn_b2"]), "ln_g": columns(v["L0_gnn_ln_g"]),
        "ln_b": columns(v["L0_gnn_ln_b"]),
        "w_r1": c(v["L0_ffn_Wr"]), "b_r1": r(v["L0_ffn_br"]), "b_o1": c(v["L0_ffn_bo"]), "w_hidden1": c(v["L0_ffn_W1"]),
        "w_deep": c(v["L0_ffn_W2"]), "w_out1": c(v["L0_ffn_Wo"]),
        "bn": c(np.stack([np.stack([by_expert(v["L0_ffn_" + name + str(n)]) for name in ("g", "be", "m", "v", "b")], axis=1)
                          for n in (1, 2)], axis=1)),
        "w_r2": c(v["L1_ffn_Wr"]), "b_r2": r(v["L1_ffn_br"]), "b_o2": c(v["L1_ffn_b2"]), "w_hidden2": c(v["L1_ffn_W1"]),
        "w_out2": c(v["L1_ffn_W2"]), "b_hidden": by_expert(v["L1_ffn_b1"]), "gamma": columns(v["L1_ffn_gamma"]),
        "beta": columns(v["L1_ffn_beta"]),
    }


def kernel(**inputs):
    import concourse.bacc as bacc
    from concourse.bass_utils import run_bass_kernel_spmd

    arrays = layout({name: np.asarray(value) for name, value in inputs.items()})
    nc = bacc.Bacc("TRN2", target_bir_lowering=False, num_devices=1)
    parts = {name: nc.dram_tensor(f"in_{name}_dram", a.shape, mybir.dt.from_np(a.dtype), kind="ExternalInput").ap()
             for name, a in arrays.items()}
    out = nc.dram_tensor("out_0_dram", (NODES, C), F32, kind="ExternalOutput").ap()
    program(nc, parts, out)
    ran = run_bass_kernel_spmd(nc, [{f"in_{name}_dram": a for name, a in arrays.items()}], core_ids=[0])
    return ran.results[0]["out_0_dram"]
```

```python
from contextlib import ExitStack

import numpy as np

import concourse.bass as bass
from concourse import mybir

F32 = mybir.dt.float32
BF16 = mybir.dt.bfloat16
I32 = mybir.dt.int32
ALU = mybir.AluOpType
ACT = mybir.ActivationFunctionType
AX = mybir.AxisListType.X

P = 128
NODES = 3125
C = 256
KC = C // P
NT = -(-NODES // P)
ROWS = NT * P
FULL = NODES // P
LAST = NODES - FULL * P
GT = 5
NG = NT // GT
GN = GT * P
EDGES = 50000
SUB = 2
EW = SUB * P
ET = -(-EDGES // EW)
EROWS = ET + 1
BP = 2
BATCH = BP * SUB
DEEP = 4
NB = -(-(ET + NT - 1) // (BP * 2 * DEEP)) * 2 * DEEP
NP = NB * BP
BLK = 2
PB = NP // BLK
NPX = NP + 2 * BP
FAR = 8191
H0, D0 = 8, C // 8
H1, D1 = 4, C // 4
HM, DM = 8, 64
SW = C + H0
BIG = 2.0 ** 100
NE = 8


def after(eng, sem, value):
    if not isinstance(value, int) or value > 0:
        eng.wait_ge(sem, value)


def loop(eng, count, body):
    body(0)
    if count > 1:
        with eng.Fori(1, count) as i:
            body(i)


BEHIND = [1, 3, 2, 2, 2]
USES = [3, 2]


BUF3 = [0, 1, 0, 1, 2]
BEHIND3 = [3, 3, 2, 2, 5]


def uses(g, j):
    return g * USES[j % 2] + j // 2


def real(b, back):
    return not isinstance(b, int) or b >= back


def spread(ap, axis, n):
    shape = list(ap.shape)
    shape.insert(axis, n)
    return ap.unsqueeze(axis).broadcast_to(shape)


class Core:
    pass


def scope(nc, ctx, stage):
    def sb(name, shape, dt=F32):
        return ctx.enter_context(nc.sbuf_tensor(f"{stage}_{name}", shape, dt))

    def ps(name, shape, dt=F32):
        size = int(np.prod(shape[1:]))
        banks = -(-size // 512)
        whole = ctx.enter_context(nc.psum_tensor(f"{stage}_{name}", [P, banks * 512], dt))
        if len(shape) == 2:
            return whole[0:shape[0], 0:size]
        if len(shape) == 3:
            return whole[0:shape[0], 0:size].rearrange("p (a b) -> p a b", a=shape[1])
        return whole[0:shape[0], 0:size].rearrange("p (a b c) -> p a b c", a=shape[1], b=shape[2])

    sems = []

    def clear():
        if sems:
            nc.clear_and_free_semaphores(sems)
            nc.all_engine_barrier()
    ctx.callback(clear)

    def sem(name):
        sems.append(nc.alloc_semaphore(f"{stage}_{name}"))
        return sems[-1]

    return sb, ps, sem


def prepare(nc, k, a):
    with ExitStack() as ctx:
        sb, ps, sem = scope(nc, ctx, "prepare")
        tail = sb("tail", [1, 2, EROWS * EW - EDGES], I32)
        first = sb("first", [1, EROWS], I32)
        firstw = sb("firstw", [1, EROWS], I32)
        start = sb("start", [1, EROWS])
        rowno = sb("rowno", [1, EROWS])
        ones_row = sb("ones_row", [1, P])
        pairno = sb("pairno", [PB, BLK])
        hits = sb("hits", [PB, BLK, EROWS])
        count = sb("count", [PB, BLK])
        win_f = sb("win_f", [PB, BLK])
        win_o = sb("win_o", [PB, BLK])
        win_c = sb("win_c", [PB, BLK])
        win_i = sb("win_i", [PB, BLK], I32)
        srow = sb("srow", [PB, BLK, EW], I32)
        drow = sb("drow", [PB, BLK, EW], I32)
        sf = sb("sf", [PB, BLK, EW])
        df = sb("df", [PB, BLK, EW])
        dr = sb("dr", [PB, BLK, EW])
        pstart = ps("pstart", [P, EROWS])
        pT = ps("pT", [P, 2, 512])
        tails_set, padded, edges_in, x_in = sem("tails_set"), sem("padded"), sem("edges_in"), sem("x_in")
        firsts_in, zeroed, idf_set, consts = sem("firsts_in"), sem("zeroed"), sem("idf_set"), sem("consts")
        dve, bcast, tiles_ready = sem("dve"), sem("bcast"), sem("tiles_ready")
        rows_in, wins_out, wins_in, turned = sem("rows_in"), sem("wins_out"), sem("wins_in"), sem("turned")
        rel_ready, share_set = sem("rel_ready"), sem("share_set")

        with nc.Block() as block:
            @block.sync
            def _(sp):
                for name, pad in (("src", k.src_pad), ("dst", k.dst_pad)):
                    flat = pad.rearrange("a b -> (a b)")
                    sp.dma_start(flat[0:EDGES].rearrange("(a b) -> a b", a=80),
                                 a[name].rearrange("(a b) -> a b", a=80)).then_inc(edges_in, 16)
                sp.wait_ge(tails_set, 2)
                for n, pad in enumerate((k.src_pad, k.dst_pad)):
                    flat = pad.rearrange("(o a) b -> o (a b)", o=1)
                    sp.dma_start(flat[:, EDGES:EROWS * EW], tail[:, n, :]).then_inc(edges_in, 16)
                sp.wait_ge(zeroed, 1)
                sp.dma_start(k.x[:, 0:FULL, :], a["x"][0:FULL * P, :].rearrange("(t p) c -> p t c", p=P)).then_inc(x_in, 16)
                sp.dma_start(k.x[0:LAST, FULL, :], a["x"][FULL * P:NODES, :]).then_inc(x_in, 16)
                sp.wait_ge(edges_in, 64)
                sp.dma_start(first[:, :], k.dst_pad[:, 0:1].rearrange("a b -> b a"),
                             allow_slow_non_contiguous=True).then_inc(firsts_in, 16)
                sp.wait_ge(dve, 8)
                sp.dma_start(k.win_dram.rearrange("b p -> p b"), win_i[:, :],
                             allow_slow_non_contiguous=True).then_inc(wins_out, 16)
                sp.wait_ge(wins_out, 16)
                sp.dma_start(k.win[:, 0:NP], k.win_dram.rearrange("(o b) p -> o (b p)", o=1)).then_inc(wins_in, 16)
                sp.wait_ge(wins_in, 16)
                sp.wait_ge(x_in, 32)

            @block.gpsimd
            def _(pool):
                pool.memset(k.x[:, FULL, :], 0.0).then_inc(zeroed, 1)
                pool.memset(k.share[:, :], 1.0 / NODES).then_inc(share_set, 1)
                pool.wait_ge(share_set, 1)
                pool.affine_select(out=k.share[:, :], in_=k.share[:, :], compare_op=ALU.is_gt, fill=0.0, base=NODES,
                                   pattern=[[-P, NT]], channel_multiplier=-1).then_inc(share_set, 1)
                pool.memset(k.ident[:, :], 0.0).then_inc(idf_set, 1)
                pool.wait_ge(idf_set, 1)
                pool.affine_select(out=k.ident[:, :], in_=k.ident[:, :], compare_op=ALU.not_equal, fill=1.0, base=0,
                                   pattern=[[-1, P]], channel_multiplier=1).then_inc(idf_set, 1)
                pool.iota(k.lane[:, :], [[1, P]], base=0, channel_multiplier=0,
                          allow_small_or_imprecise_dtypes=True).then_inc(consts, 1)
                pool.iota(rowno[:, :], [[1, EROWS]], base=0, channel_multiplier=0,
                          allow_small_or_imprecise_dtypes=True).then_inc(consts, 1)
                pool.iota(pairno[:, :], [[PB, BLK]], base=0, channel_multiplier=1,
                          allow_small_or_imprecise_dtypes=True).then_inc(consts, 1)
                pool.memset(ones_row[:, :], 1.0).then_inc(consts, 1)
                pool.memset(k.power[:, :], -0.5).then_inc(consts, 1)
                pool.memset(k.win[:, NP:NPX], 0).then_inc(consts, 1)
                pool.memset(k.rel[:, NP * SUB:NPX * SUB], -1.0).then_inc(consts, 1)
                pool.wait_ge(tiles_ready, 1)
                for b in range(BLK):
                    for table, rows in ((k.src_pad, srow), (k.dst_pad, drow)):
                        pool.indirect_dma_start(rows[:, b, :], None, table,
                                                bass.IndirectOffsetOnAxis(ap=k.tile_i[:, b:b + 1], axis=0)).then_inc(rows_in, 16)

            @block.vector
            def _(dv):
                dv.memset(tail[:, 0, :], 0).then_inc(tails_set, 1)
                dv.memset(tail[:, 1, :], FAR).then_inc(tails_set, 1)
                dv.memset(k.ones[:, :], 1.0).then_inc(dve, 1)
                dv.wait_ge(firsts_in, 16)
                dv.tensor_scalar(firstw[:, :], first[:, :], 7, None, ALU.arith_shift_right).then_inc(dve, 1)
                dv.wait_ge(consts, 7)
                dv.wait_ge(dve, 2)
                dv.tensor_tensor(start[:, :], firstw[:, :], rowno[:, :], ALU.add).then_inc(dve, 1)
                dv.wait_ge(dve, 3)
                dv.memset(start[:, 0:1], 0.0).then_inc(dve, 1)
                dv.wait_ge(bcast, 1)
                for b in range(BLK):
                    ins = dv.tensor_scalar(hits[:, b, :], pstart[0:PB, :], pairno[:, b:b + 1], None, ALU.is_le, ALU.add,
                                           accum_out=count[:, b:b + 1])
                ins.then_inc(dve, 1)
                dv.wait_ge(dve, 5)
                dv.tensor_scalar(k.tile_i[:, :], count[:, :], -1.0, None, ALU.add).then_inc(tiles_ready, 1)
                dv.tensor_tensor(win_f[:, :], pairno[:, :], count[:, :], ALU.subtract).then_inc(dve, 1)
                dv.wait_ge(dve, 6)
                dv.tensor_scalar(win_o[:, :], win_f[:, :], 1.0, float(P), ALU.add, ALU.mult).then_inc(dve, 1)
                dv.tensor_scalar(win_i[:, :], win_f[:, :], 1.0, float(NT - 1), ALU.add, ALU.min).then_inc(dve, 1)
                dv.wait_ge(dve, 8)
                dv.wait_ge(rows_in, 32 * BLK)
                dv.tensor_tensor(dr[:, :, :], drow[:, :, :], spread(win_o[:, :], 2, EW), ALU.subtract).then_inc(rel_ready, 1)
                dv.tensor_copy(sf[:, :, :], srow[:, :, :]).then_inc(rel_ready, 1)
                dv.wait_ge(turned, 2 * BLK * SUB)
                for b in range(BLK):
                    for n, to in enumerate((k.rel, k.src)):
                        pairs = to[:, b * PB * SUB:(b + 1) * PB * SUB].rearrange("p (i s) -> p s i", s=SUB)
                        dv.tensor_copy(pairs, pT[:, n, b * EW:(b + 1) * EW].rearrange("p (s i) -> p s i", s=SUB)[:, :, 0:PB]).then_inc(dve, 1)

            @block.tensor
            def _(pe):
                pe.wait_ge(dve, 4)
                pe.wait_ge(consts, 7)
                pe.matmul(pstart[:, :], ones_row[:, :], start[:, :], start=True, stop=True).then_inc(bcast, 1)
                pe.wait_ge(idf_set, 2)
                pe.wait_ge(rel_ready, 2)
                for n, rows in enumerate((dr, sf)):
                    for b in range(BLK):
                        for m in range(SUB):
                            pe.transpose(pT[:, n, b * EW + m * P:b * EW + m * P + PB], rows[:, b, m * P:(m + 1) * P],
                                         k.ident[0:PB, 0:PB]).then_inc(turned, 1)


def normalise(dv, g, source, s, t):
    for j in range(GT):
        dv.bn_stats(t.stats[:, j, :], source(g, j)).then_inc(s.stats_ready, 1)
    dv.wait_ge(s.stats_ready, g * GT + GT)
    dv.sem_inc(s.stats_fence, 1)
    for j in range(GT):
        dv.bn_aggr(t.moments[:, j, :], t.stats[:, j, :]).then_inc(s.moments_ready, 1)
    dv.wait_ge(s.moments_ready, g * GT + GT)
    dv.tensor_scalar(t.vareps[:, :], t.moments[:, :, 1], 1e-5, None, ALU.add).then_inc(s.vareps_ready, 1)
    dv.wait_ge(s.rstd_ready, g + 1)
    for j in range(GT):
        dv.tensor_scalar(t.normed[:, j, :], source(g, j), t.moments[:, j, 0:1], t.rstd[:, j:j + 1],
                         ALU.subtract, ALU.mult).then_inc(s.normed_ready, 1)


def deviations(pool, g, k, s, t):
    pool.wait_ge(s.vareps_ready, g + 1)
    pool.tensor_tensor(t.rstd[:, :], t.vareps[:, :], k.power[:, 0:GT], ALU.pow).then_inc(s.rstd_ready, 1)


class Chain:

    def __init__(self, eng, sem, per):
        self.eng, self.sem, self.per = eng, sem, per

    def turn(self, i):
        self.count = i * self.per
        self.left = self.per

    def __call__(self, instruction):
        self.left -= 1
        instruction.then_inc(self.sem, 1)
        self.eng.wait_ge(self.sem, self.count + self.per - self.left)


def norm_tensors(sb, sem, tag=""):
    t, s = Core(), Core()
    t.stats = sb(f"stats{tag}", [P, GT, 6])
    t.moments = sb(f"moments{tag}", [P, GT, 2])
    t.vareps = sb(f"vareps{tag}", [P, GT])
    t.rstd = sb(f"rstd{tag}", [P, GT])
    t.normed = sb(f"normed{tag}", [P, GT, C])
    s.stats_ready = sem("stats_ready" + tag)
    s.stats_fence = sem("stats_fence" + tag)
    s.moments_ready = sem("moments_ready" + tag)
    s.vareps_ready = sem("vareps_ready" + tag)
    s.rstd_ready = sem("rstd_ready" + tag)
    s.normed_ready = sem("normed_ready" + tag)
    return t, s


def project_first(nc, k, a):
    with ExitStack() as ctx:
        sb, ps, sem = scope(nc, ctx, "project_first")
        t, s = norm_tensors(sb, sem)
        W = 1536
        CH = W // 512
        w = sb("w", [P, KC, W])
        bias = sb("bias", [P, W])
        xT = sb("xT", [P, 2, KC, P])
        outs = sb("outs", [P, 2, W])
        pT = [ps(f"pT{i}", [P, 512]) for i in range(2)]
        pM = [[ps(f"pM{i}{c}", [P, 512]) for c in range(CH)] for i in range(2)]
        loaded, kept, xT_psum, xT_ready = sem("loaded"), sem("kept"), sem("xT_psum"), sem("xT_ready")
        projected, outs_ready, xn_kept = sem("projected"), sem("outs_ready"), sem("xn_kept")
        stored = [sem("stored0"), sem("stored1")]
        sums_clear = sem("sums_clear")

        with nc.Block() as block:
            @block.sync
            def _(sp):
                for n in range(KC):
                    sp.dma_start(w[:, n, :], a["w_first"][n * P:(n + 1) * P, :]).then_inc(loaded, 16)
                sp.dma_start(bias[:, :], a["b_first"].partition_broadcast(P)).then_inc(loaded, 16)

                def group(g):
                    for j in range(GT):
                        n, u = g * GT + j, j % 2
                        sp.wait_ge(outs_ready, CH * n + CH)
                        sp.dma_start(k.kv_table[bass.ds(n * P, P), :], outs[:, u, 0:512]).then_inc(stored[u], 16)
                        sp.dma_start(k.mix_qkv[bass.ds(n * P, P), :], outs[:, u, 768:1536]).then_inc(stored[u], 16)
                loop(sp, NG, group)
                for u in range(2):
                    sp.wait_ge(stored[u], 32 * USES[u] * NG)

            @block.gpsimd
            def _(pool):
                pool.memset(k.sums[:, :, :], 0.0).then_inc(sums_clear, 1)
                loop(pool, NG, lambda g: deviations(pool, g, k, s, t))

            @block.vector
            def _(dv):
                dv.wait_ge(loaded, 48)

                def group(g):
                    after(dv, xT_psum, GT * g)
                    after(dv, xn_kept, g)
                    normalise(dv, g, lambda g, j: k.x[:, bass.ds(g * GT + j, 1), :], s, t)
                    for j in range(GT):
                        n, u = g * GT + j, j % 2
                        after(dv, stored[u], 32 * uses(g, j))
                        after(dv, kept, n - BEHIND[j] + 1)
                        for c in range(CH):
                            dv.wait_ge(projected, CH * n + c + 1)
                            dv.tensor_tensor(outs[:, u, c * 512:(c + 1) * 512], pM[u][c][:, :],
                                             bias[:, c * 512:(c + 1) * 512], ALU.add).then_inc(outs_ready, 1)
                loop(dv, NG, group)

            @block.scalar
            def _(ac):
                def group(g):
                    for j in range(GT):
                        n, u = g * GT + j, j % 2
                        ac.wait_ge(xT_psum, n + 1)
                        after(ac, projected, CH * (n - BEHIND[j] + 1))
                        ac.copy(xT[:, u, :, :], pT[u][:, 0:C].rearrange("p (k n) -> p k n", k=KC)).then_inc(xT_ready, 1)
                        if j >= 1:
                            ac.wait_ge(outs_ready, CH * (n - 1) + 2)
                            ac.copy(k.node[:, bass.ds(n - 1, 1), :], outs[:, 1 - u:2 - u, 512:768]).then_inc(kept, 1)
                    ac.wait_ge(outs_ready, CH * n + 2)
                    ac.copy(k.node[:, bass.ds(n, 1), :], outs[:, 0:1, 512:768]).then_inc(kept, 1)
                    ac.copy(k.xn[:, bass.ds(g * GT, GT), :], t.normed[:, :, :]).then_inc(xn_kept, 1)
                loop(ac, NG, group)

            @block.tensor
            def _(pe):
                pe.wait_ge(loaded, 48)

                def group(g):
                    for j in range(GT):
                        n, u = g * GT + j, j % 2
                        pe.wait_ge(s.normed_ready, n + 1)
                        after(pe, xT_ready, n - BEHIND[j] + 1)
                        for c in range(KC):
                            ins = pe.transpose(pT[u][:, c * P:(c + 1) * P], t.normed[:, j, c * P:(c + 1) * P], k.ident[:, :])
                        ins.then_inc(xT_psum, 1)
                        pe.wait_ge(xT_ready, n + 1)
                        after(pe, outs_ready, CH * (n - BEHIND[j] + 1))
                        for c in range(CH):
                            for q in range(KC):
                                ins = pe.matmul(pM[u][c][:, :], xT[:, u, q, :], w[:, q, c * 512:(c + 1) * 512],
                                                start=q == 0, stop=q == KC - 1)
                            ins.then_inc(projected, 1)
                loop(pe, NG, group)


def edge_gather(pool, k, t, s, table, rows_free):
    def steps(i):
        for half in range(2):
            first = (2 * i + half) * DEEP
            for u in range(DEEP):
                b = first + u
                after(pool, rows_free, b - DEEP + 1)
                if u == 0:
                    pool.sem_inc(s.fence, 1)
                    pool.tensor_copy(t.index[:, half, :], k.src[:, bass.ds(b * BATCH, DEEP * BATCH)]).then_inc(s.index_ready, 1)
                    pool.wait_ge(s.index_ready, 2 * i + half + 1)
                pool.sem_inc(s.fence, 1)
                for m in range(BATCH):
                    at = u * BATCH + m
                    pool.indirect_dma_start(t.rows[:, u, m, :], None, table,
                                            bass.IndirectOffsetOnAxis(ap=t.index[:, half, at:at + 1], axis=0)).then_inc(s.rows_in[u], 16)
    loop(pool, NB // (2 * DEEP), steps)
    for u in range(DEEP):
        pool.wait_ge(s.rows_in[u], 16 * BATCH * NB // DEEP)


def edge_hot(dv, b, u, k, t, s, free):
    after(dv, free, b - DEEP + 1)
    for m in range(BATCH):
        ins = dv.tensor_scalar(t.hot[:, u % DEEP, m, :], k.lane[:, :], k.rel[:, bass.ds(b * BATCH + m, 1)], None, ALU.is_equal)
    ins.then_inc(s.hot_ready, 1)


def edge_turn(pe, b, u, k, t, s):
    pe.wait_ge(s.hot_ready, b + 1)
    after(pe, s.hotT_ready, b)
    for m in range(BATCH):
        ins = pe.transpose(t.p_hotT[:, m, :], t.hot[:, u % DEEP, m, :], k.ident[:, :])
    ins.then_inc(s.hotT_psum, 1)


def edge_keep(ac, b, u, t, s):
    ac.wait_ge(s.hotT_psum, b + 1)
    after(ac, s.looked_up, b - 1)
    ac.copy(t.hotT[:, u % 2, :, :], t.p_hotT[:, :, :]).then_inc(s.hotT_ready, 1)


def windows_of(eng, k, b):
    return [eng.value_load(k.win[0:1, bass.ds(b * BP + m, 1)], min_val=0, max_val=NT - 1) for m in range(BP)]


def edge_look(pe, b, u, k, t, s, node, into, look_free):
    windows = windows_of(pe, k, b)
    pe.wait_ge(s.hotT_ready, b + 1)
    after(pe, look_free, b)
    for m in range(BATCH):
        ins = pe.matmul(into[:, m, :], t.hotT[:, u % 2, m, :], node[:, bass.ds(windows[m // SUB], 1), :], start=True, stop=True)
    ins.then_inc(s.looked_up, 1)


def edge_sum(pe, b, u, t, s, width):
    pe.wait_ge(s.weighted_ready, b + 1)
    after(pe, s.added, (b - 1) * BP)
    for m in range(BP):
        for n in range(SUB):
            c = m * SUB + n
            ins = pe.matmul(t.p_sum[:, u % 2 * BP + m, 0:width], t.hot[:, u % DEEP, c, :], t.weighted[:, u % 2, c, 0:width],
                            start=n == 0, stop=n == SUB - 1)
    ins.then_inc(s.summed, 1)


def edge_add(dv, b, u, k, t, s, width):
    windows = windows_of(dv, k, b)
    dv.wait_ge(s.summed, b + 1)
    for m in range(BP):
        into = k.sums[:, bass.ds(windows[m], 1), 0:width]
        after(dv, s.added, b * BP + m)
        c = u % 2 * BP + m
        dv.tensor_tensor(into, into, t.p_sum[:, c:c + 1, 0:width], ALU.add).then_inc(s.added, 1)


def edge_loop(eng, slot):
    def steps(i):
        for u in range(DEEP):
            slot(i * DEEP + u, u, i)
    loop(eng, NB // DEEP, steps)


def attend_first(nc, k):
    with ExitStack() as ctx:
        sb, ps, sem = scope(nc, ctx, "attend_first")
        t, s = Core(), Core()
        t.index = sb("index", [P, 2, DEEP * BATCH], I32)
        t.rows = sb("rows", [P, DEEP, BATCH, 2 * C])
        t.hot = sb("hot", [P, DEEP, BATCH, P])
        t.hotT = sb("hotT", [P, 2, BATCH, P])
        score = sb("score", [P, 2, BATCH, H0])
        clip = sb("clip", [P, 2, BATCH, H0])
        t.weighted = sb("weighted", [P, 2, BATCH, SW])
        product = sb("product", [P, BATCH, C])
        t.p_hotT = ps("p_hotT", [P, BATCH, P])
        look = ps("p_look", [P, BATCH, C])
        t.p_sum = ps("p_sum", [P, 2 * BP, 512])
        s.fence, s.index_ready, s.hot_ready, s.hotT_psum = sem("fence"), sem("index_ready"), sem("hot_ready"), sem("hotT_psum")
        s.hotT_ready, s.looked_up, s.weighted_ready = sem("hotT_ready"), sem("looked_up"), sem("weighted_ready")
        s.summed, s.added = sem("summed"), sem("added")
        products_ready, scores_ready, clipped, exp_ready = sem("products_ready"), sem("scores_ready"), sem("clipped"), sem("exp_ready")
        s.rows_in = [sem(f"rows_in{u}") for u in range(DEEP)]
        root = D0 ** 0.5
        with nc.Block() as block:
            @block.gpsimd
            def _(pool):
                edge_gather(pool, k, t, s, k.kv_table, s.weighted_ready)

            @block.tensor
            def _(pe):
                edge_turn(pe, 0, 0, k, t, s)
                edge_turn(pe, 1, 1, k, t, s)
                edge_look(pe, 0, 0, k, t, s, k.node, look, products_ready)

                def slot(b, u, i):
                    if real(b, 2):
                        edge_sum(pe, b - 2, u + 2, t, s, SW)
                    edge_look(pe, b + 1, u + 1, k, t, s, k.node, look, products_ready)
                    edge_turn(pe, b + 2, u + 2, k, t, s)
                edge_loop(pe, slot)
                edge_sum(pe, NB - 2, 2, t, s, SW)
                edge_sum(pe, NB - 1, 3, t, s, SW)

            @block.scalar
            def _(ac):
                edge_keep(ac, 0, 0, t, s)
                edge_keep(ac, 1, 1, t, s)

                def slot(b, u, i):
                    ac.wait_ge(clipped, b + 1)
                    after(ac, s.summed, b - 1)
                    ac.activation(t.weighted[:, u % 2, :, C:SW], clip[:, u % 2, :, :], ACT.Exp, scale=1.0 / root).then_inc(exp_ready, 1)
                    edge_keep(ac, b + 2, u, t, s)
                edge_loop(ac, slot)

            @block.vector
            def _(dv):
                edge_hot(dv, 0, 0, k, t, s, s.summed)
                edge_hot(dv, 1, 1, k, t, s, s.summed)

                def weigh(b, u):
                    dv.wait_ge(exp_ready, b + 1)
                    dv.tensor_tensor(t.weighted[:, u % 2, :, 0:C].rearrange("p m (h d) -> p m h d", h=H0),
                                     t.rows[:, u % DEEP, :, C:2 * C].rearrange("p m (h d) -> p m h d", h=H0),
                                     spread(t.weighted[:, u % 2, :, C:SW], 3, D0), ALU.mult).then_inc(s.weighted_ready, 1)

                def slot(b, u, i):
                    dv.wait_ge(s.looked_up, b + 1)
                    dv.wait_ge(s.rows_in[u], (i + 1) * 16 * BATCH)
                    dv.tensor_tensor(product[:, :, :], look[:, :, :], t.rows[:, u, :, 0:C], ALU.mult).then_inc(products_ready, 1)
                    dv.wait_ge(products_ready, b + 1)
                    dv.tensor_reduce(score[:, u % 2, :, :], product[:, :, :].rearrange("p m (h d) -> p m h d", h=H0),
                                     AX, ALU.add).then_inc(scores_ready, 1)
                    if real(b, 1):
                        weigh(b - 1, u + 3)
                    dv.wait_ge(scores_ready, b + 1)
                    after(dv, exp_ready, b - 1)
                    dv.tensor_scalar(clip[:, u % 2, :, :], score[:, u % 2, :, :], -10.0 * root, 10.0 * root, ALU.max,
                                     ALU.min).then_inc(clipped, 1)
                    if real(b, 2):
                        edge_add(dv, b - 2, u + 2, k, t, s, SW)
                    edge_hot(dv, b + 2, u + 2, k, t, s, s.summed)
                edge_loop(dv, slot)
                weigh(NB - 1, DEEP - 1)
                edge_add(dv, NB - 2, DEEP - 2, k, t, s, SW)
                edge_add(dv, NB - 1, DEEP - 1, k, t, s, SW)


SHIFTS = D0 // 2 + 1
FEAT = SHIFTS * D0 + D0 + 1
FCH = -(-FEAT // P)
FLAST = FEAT - (FCH - 1) * P
ROOT4 = float(D0) ** 0.25
VW = D0 + 1


def features(dv, double, phi, ready):
    ap = double
    steps = [list(x) for x in ap.ap]
    onward = bass.AP(tensor=ap.tensor, offset=ap.offset, ap=[steps[0], steps[1], [1, SHIFTS], [1, D0]])
    dv.tensor_tensor(phi[:, :, 0:SHIFTS * D0].rearrange("p h (s d) -> p h s d", s=SHIFTS),
                     spread(double[:, :, 0:D0], 2, SHIFTS), onward, ALU.mult).then_inc(ready, 1)


def feature_norms(dv, g, part, square, norm2, s):
    dv.tensor_tensor(square[:, :, :], part, part, ALU.mult).then_inc(s.squared, 1)
    dv.wait_ge(s.squared, g + 1)
    dv.tensor_reduce(norm2[:, :, :], square[:, :, :].rearrange("p t (h d) -> p t h d", h=H0), AX, ALU.add).then_inc(s.norm2_ready, 1)
    dv.wait_ge(s.norm2_ready, g + 1)


def feature_double(dv, g, part, factor, double, s):
    heads = double.rearrange("p t h (two d) -> p t h two d", two=2)
    for n in range(2):
        ins = dv.tensor_tensor(heads[:, :, :, n, :], part.rearrange("p t (h d) -> p t h d", h=H0), spread(factor[:, :, :], 3, D0), ALU.mult)
    ins.then_inc(s.doubled, 1)
    dv.wait_ge(s.doubled, g + 1)


def mix_keys(nc, k, a):
    with ExitStack() as ctx:
        sb, ps, sem = scope(nc, ctx, "mix_keys")
        kv = sb("kv", [P, 2, GT, C])
        square = sb("square", [P, GT, C])
        norm2 = sb("norm2", [P, GT, H0])
        factor = sb("factor", [P, GT, H0])
        double = sb("double", [P, GT, H0, 2 * D0])
        phi = sb("phi", [P, 3, H0, FEAT])
        vals = sb("vals", [P, 3, H0, VW])
        zeros = sb("zeros", [P, 512])
        sums = sb("sums", [P, H0 // 2, FEAT])
        long = [ps(f"long{n}", [P, 512]) for n in range(H0 // 2)]
        short = ps("short", [P, H0 // 2, FEAT - 512])
        turn = [ps(f"turn{u}", [P, 512]) for u in range(2)]
        s = Core()
        s.squared, s.norm2_ready, s.doubled = sem("squared"), sem("norm2_ready"), sem("doubled")
        kv_in, clamped, factor_ready = sem("kv_in"), sem("clamped"), sem("factor_ready")
        phi_ready, vals_ready, summed = sem("phi_ready"), sem("vals_ready"), sem("summed")
        zeroed, consts, kept, turned, sums_kept = sem("zeroed"), sem("consts"), sem("kept"), sem("turned"), sem("sums_kept")

        with nc.Block() as block:
            @block.sync
            def _(sp):
                def group(g):
                    after(sp, vals_ready, g * GT)
                    for n in range(2):
                        sp.dma_start(kv[:, n, :, :], k.mix_qkv[bass.ds(g * GN, GN), n * C:(n + 1) * C]
                                     .rearrange("(t p) c -> p t c", p=P)).then_inc(kv_in, 16)
                loop(sp, NG, group)

            @block.gpsimd
            def _(pool):
                for u in range(3):
                    pool.memset(phi[:, u, :, FEAT - 1:FEAT], 1.0).then_inc(consts, 1)
                pool.memset(zeros[:, :], 0.0).then_inc(zeroed, 1)

                def group(g):
                    pool.wait_ge(clamped, g + 1)
                    pool.tensor_tensor(factor[:, :, :], norm2[:, :, :], k.power[:, 0:GT * H0].rearrange("p (t h) -> p t h", t=GT),
                                       ALU.pow).then_inc(factor_ready, 1)
                loop(pool, NG, group)

            @block.vector
            def _(dv):
                dv.wait_ge(consts, 3)

                def feature(n, j):
                    features(dv, double[:, j], phi[:, BUF3[j]], phi_ready)

                def group(g):
                    keys = kv[:, 0, :, :]
                    dv.wait_ge(kv_in, 32 * (g + 1))
                    feature_norms(dv, g, keys, square, norm2, s)
                    dv.tensor_scalar(norm2[:, :, :], norm2[:, :, :], 1e-24, ROOT4 ** -2, ALU.max, ALU.mult).then_inc(clamped, 1)
                    if real(g, 1):
                        feature(g * GT - 1, GT - 1)
                    dv.wait_ge(factor_ready, g + 1)
                    after(dv, phi_ready, g * GT)
                    feature_double(dv, g, keys, factor, double, s)
                    for j in range(GT):
                        n, u = g * GT + j, BUF3[j]
                        after(dv, summed, n - BEHIND3[j] + 1)
                        dv.tensor_scalar(vals[:, u, :, 0:1], spread(k.share[:, bass.ds(n, 1)], 1, H0), 1.0, None, ALU.mult)
                        dv.tensor_scalar(vals[:, u, :, 1:VW], kv[:, 1, j, :].rearrange("p (h d) -> p h d", h=H0),
                                         k.share[:, bass.ds(n, 1)], None, ALU.mult)
                        dv.tensor_copy(phi[:, u, :, SHIFTS * D0:FEAT - 1], double[:, j, :, 0:D0]).then_inc(vals_ready, 1)
                        if j < GT - 1:
                            feature(n, j)
                loop(dv, NG, group)
                feature(NT - 1, GT - 1)
                dv.wait_ge(summed, NT)
                for n in range(H0 // 2):
                    dv.tensor_copy(sums[:, n, 0:512], long[n][:, :])
                dv.tensor_copy(sums[:, :, 512:FEAT], short[:, :, :]).then_inc(sums_kept, 1)
                for c in range(FCH):
                    m = P if c < FCH - 1 else FLAST
                    dv.wait_ge(turned, c + 1)
                    if c == 0:
                        parts = [(0, D0, 0.5), (D0, 2 * D0, 1.0), (2 * D0, P, 1.0)]
                    elif c < FCH - 1:
                        parts = [(0, P, 1.0)]
                    else:
                        parts = [(0, D0, 0.5), (D0, 2 * D0, ROOT4 ** 2), (2 * D0, m, ROOT4 ** 4)]
                    for lo, hi, weight in parts:
                        ins = dv.tensor_scalar(k.mixed[lo:hi, c, :].rearrange("p (h d) -> p h d", h=H0),
                                               turn[c % 2][lo:hi, :].rearrange("p (h d) -> p h d", h=H0)[:, :, 0:VW],
                                               weight, None, ALU.mult)
                    ins.then_inc(kept, 1)

            @block.tensor
            def _(pe):
                pe.wait_ge(zeroed, 1)
                for bank in long:
                    pe.matmul(bank[:, :], zeros[:, 0:P], zeros[:, :], start=True, stop=False, skip_group_check=True)
                pe.matmul(short[:, :, :], zeros[:, 0:P], zeros[:, 0:H0 // 2 * (FEAT - 512)], start=True, stop=False, skip_group_check=True)

                def group(g):
                    for j in range(GT):
                        n, u = g * GT + j, BUF3[j]
                        pe.wait_ge(phi_ready, n + 1)
                        for h in range(H0):
                            lanes = slice(h % 2 * 64, h % 2 * 64 + VW)
                            pe.matmul(long[h // 2][lanes, :], vals[:, u, h, :], phi[:, u, h, 0:512],
                                      start=False, stop=False, skip_group_check=True)
                            ins = pe.matmul(short[lanes, h // 2, :], vals[:, u, h, :], phi[:, u, h, 512:FEAT],
                                            start=False, stop=False, skip_group_check=True)
                        ins.then_inc(summed, 1)
                loop(pe, NG, group)
                pe.wait_ge(sums_kept, 1)
                for c in range(FCH):
                    m = P if c < FCH - 1 else FLAST
                    after(pe, kept, c - 1)
                    for n in range(H0 // 2):
                        ins = pe.transpose(turn[c % 2][0:m, n * P:(n + 1) * P], sums[:, n, c * P:c * P + m], k.ident[:, :])
                    ins.then_inc(turned, 1)


def mix_queries(nc, k, a):
    with ExitStack() as ctx:
        sb, ps, sem = scope(nc, ctx, "mix_queries")
        q = sb("q", [P, 1, GT, C])
        square = sb("square", [P, GT, C])
        norm2 = sb("norm2", [P, GT, H0])
        factor = sb("factor", [P, GT, H0])
        scaled = sb("scaled", [P, GT, H0])
        temper = sb("temper", [P, H0])
        double = sb("double", [P, GT, H0, 2 * D0])
        phi = sb("phi", [P, 3, H0, FEAT])
        headT = sb("headT", [P, 2, 4, P])
        restT = sb("restT", [P, H0, P])
        recip = sb("recip", [P, 2, H0])
        y = sb("y", [P, 2, C])
        yT = sb("yT", [P, KC, P])
        w = sb("w", [P, KC, C])
        bias = sb("bias", [P, C])
        part = sb("part", [P, 2, C])
        pT = [ps(f"pT{i}", [P, 4, P]) for i in range(2)]
        pH = [ps(f"pH{i}", [P, H0 // 2, P]) for i in range(2)]
        pY = ps("pY", [P, H0 // 2, P])
        heads = sb("heads", [P, H0 // 2, P])
        zeros = sb("zeros", [P, 512])
        pYT = ps("pYT", [P, KC, P])
        pO = [ps(f"pO{i}", [P, C]) for i in range(2)]
        s = Core()
        s.squared, s.norm2_ready, s.doubled = sem("squared"), sem("norm2_ready"), sem("doubled")
        loaded, q_in, clamped, factor_ready = sem("loaded"), sem("q_in"), sem("clamped"), sem("factor_ready")
        tempered, phi_ready = sem("tempered"), sem("phi_ready")
        turned, kept, head_done, recip_ready = sem("turned"), sem("kept"), sem("head_done"), sem("recip_ready")
        y_ready, yT_psum, yT_ready, projected = sem("y_ready"), sem("yT_psum"), sem("yT_ready"), sem("projected")
        part_ready, consts, done = sem("part_ready"), sem("consts"), sem("done")
        heads_kept, turned_back, zeroed = sem("heads_kept"), sem("turned_back"), sem("zeroed")
        QUADS = H0 + 2

        with nc.Block() as block:
            @block.sync
            def _(sp):
                for n in range(KC):
                    sp.dma_start(w[:, n, :], a["w_mixproj"][n * P:(n + 1) * P, :]).then_inc(loaded, 16)
                sp.dma_start(bias[:, :], a["b_mixproj"].partition_broadcast(P)).then_inc(loaded, 16)
                sp.dma_start(temper[:, :], a["temperature"].partition_broadcast(P)).then_inc(loaded, 16)

                def group(g):
                    after(sp, s.doubled, g)
                    sp.dma_start(q[:, 0, :, :], k.mix_qkv[bass.ds(g * GN, GN), 2 * C:3 * C]
                                 .rearrange("(t p) c -> p t c", p=P)).then_inc(q_in, 16)
                loop(sp, NG, group)

            @block.gpsimd
            def _(pool):
                pool.memset(zeros[:, :], 0.0).then_inc(zeroed, 1)
                for u in range(3):
                    pool.memset(phi[:, u, :, FEAT - 1:FEAT], 1.0).then_inc(consts, 1)

                def group(g):
                    pool.wait_ge(clamped, g + 1)
                    pool.tensor_tensor(factor[:, :, :], norm2[:, :, :], k.power[:, 0:GT * H0].rearrange("p (t h) -> p t h", t=GT),
                                       ALU.pow).then_inc(factor_ready, 1)
                loop(pool, NG, group)

            @block.vector
            def _(dv):
                dv.wait_ge(consts, 3)
                dv.wait_ge(loaded, 64)

                def divide(n, j):
                    u, found = j % 2, pY.rearrange("p n (m d) -> p (n m) d", m=2)
                    after(dv, yT_psum, n - BEHIND[j] + 1)
                    dv.wait_ge(turned_back, n + 1)
                    dv.reciprocal(recip[:, u, :], found[:, :, 0]).then_inc(recip_ready, 1)
                    dv.wait_ge(recip_ready, n + 1)
                    dv.tensor_tensor(y[:, u, :].rearrange("p (h d) -> p h d", h=H0), found[:, :, 1:VW],
                                     spread(recip[:, u, :], 2, D0), ALU.mult).then_inc(y_ready, 1)

                def add(n, u):
                    dv.wait_ge(projected, n + 1)
                    dv.tensor_tensor(part[:, u, :], pO[u][:, :], bias[:, :], ALU.add).then_inc(part_ready, 1)
                    dv.wait_ge(part_ready, n + 1)
                    nodes = k.x[:, bass.ds(n, 1), :]
                    dv.tensor_tensor(nodes, nodes, part[:, u:u + 1, :], ALU.add).then_inc(done, 1)

                def group(g):
                    queries = q[:, 0, :, :]
                    dv.wait_ge(q_in, 16 * (g + 1))
                    feature_norms(dv, g, queries, square, norm2, s)
                    dv.tensor_scalar(norm2[:, :, :], norm2[:, :, :], ROOT4 ** 2, 1e-24, ALU.mult, ALU.max).then_inc(clamped, 1)
                    if real(g, 1):
                        divide(g * GT - 2, GT - 2)
                    dv.wait_ge(factor_ready, g + 1)
                    dv.scalar_tensor_tensor(out=scaled[:, :, :], in0=factor[:, :, :], scalar=ROOT4 ** 2, in1=spread(temper[:, :], 1, GT),
                                            op0=ALU.mult, op1=ALU.mult).then_inc(tempered, 1)
                    dv.wait_ge(tempered, g + 1)
                    after(dv, phi_ready, g * GT)
                    feature_double(dv, g, queries, scaled, double, s)
                    for j in range(GT):
                        n, u = g * GT + j, BUF3[j]
                        after(dv, turned, QUADS * (n - BEHIND3[j] + 1))
                        dv.tensor_copy(phi[:, u, :, SHIFTS * D0:FEAT - 1], double[:, j, :, 0:D0])
                        features(dv, double[:, j], phi[:, u], phi_ready)
                        if j > 0 and real(n, 2):
                            divide(n - 2, (j - 2) % GT)
                        if real(n, 3):
                            add(n - 3, (j - 3) % GT % 2)
                loop(dv, NG, group)
                divide(NT - 2, GT - 2)
                add(NT - 3, (GT - 3) % 2)
                divide(NT - 1, GT - 1)
                add(NT - 2, (GT - 2) % 2)
                add(NT - 1, (GT - 1) % 2)

            @block.scalar
            def _(ac):
                def keep(n):
                    ac.wait_ge(yT_psum, n + 1)
                    after(ac, projected, n)
                    ac.copy(yT[:, :, :], pYT[:, :, :]).then_inc(yT_ready, 1)

                def keep_heads(n, j):
                    ac.wait_ge(head_done, n * H0 + H0)
                    after(ac, turned_back, n)
                    ac.copy(heads[:, :, :], pH[j % 2][:, :, :]).then_inc(heads_kept, 1)

                def group(g):
                    for j in range(GT):
                        n = g * GT + j
                        if real(n, 1):
                            keep_heads(n - 1, (j - 1) % GT)
                        for c in range(QUADS):
                            ac.wait_ge(turned, n * QUADS + c + 1)
                            if c < 2:
                                after(ac, head_done, n * H0)
                                ac.copy(restT[0:FLAST, 4 * c:4 * c + 4, :], pT[c % 2][0:FLAST, :, :]).then_inc(kept, 1)
                            else:
                                after(ac, head_done, n * H0 + c - 3)
                                ac.copy(headT[:, c % 2, :, :], pT[c % 2][:, :, :]).then_inc(kept, 1)
                        if real(n, 2):
                            keep(n - 2)
                loop(ac, NG, group)
                keep_heads(NT - 1, GT - 1)
                keep(NT - 2)
                keep(NT - 1)

            @block.tensor
            def _(pe):
                pe.wait_ge(loaded, 64)
                pe.wait_ge(zeroed, 1)
                for bank in pH:
                    pe.matmul(bank[:, :, :], zeros[:, 0:P], zeros[:, :], start=True, stop=True)

                def turn_back(n):
                    pe.wait_ge(heads_kept, n + 1)
                    after(pe, y_ready, n)
                    for m in range(H0 // 2):
                        ins = pe.transpose(pY[:, m, :], heads[:, m, :], k.ident[:, :])
                    ins.then_inc(turned_back, 1)

                def project(n, u):
                    pe.wait_ge(y_ready, n + 1)
                    after(pe, yT_ready, n)
                    for c in range(KC):
                        ins = pe.transpose(pYT[:, c, :], y[:, u, c * P:(c + 1) * P], k.ident[:, :])
                    ins.then_inc(yT_psum, 1)

                def product(n, u, j):
                    pe.wait_ge(yT_ready, n + 1)
                    after(pe, part_ready, n - BEHIND[j % GT] + 1)
                    for c in range(KC):
                        ins = pe.matmul(pO[u][:, :], yT[:, c, :], w[:, c, :], start=c == 0, stop=c == KC - 1)
                    ins.then_inc(projected, 1)

                def group(g):
                    for j in range(GT):
                        n, u = g * GT + j, BUF3[j]
                        pe.wait_ge(phi_ready, n + 1)
                        for c in range(QUADS + 1):
                            if c == 3 and real(n, 1):
                                turn_back(n - 1)
                            if c < QUADS:
                                after(pe, kept, n * QUADS + c - 1)
                                for m in range(4):
                                    if c < 2:
                                        ins = pe.transpose(pT[c % 2][0:FLAST, m, :], phi[:, u, 4 * c + m, (FCH - 1) * P:FEAT],
                                                           k.ident[:, :])
                                    else:
                                        ins = pe.transpose(pT[c % 2][:, m, :], phi[:, u, c - 2, m * P:(m + 1) * P], k.ident[:, :])
                                ins.then_inc(turned, 1)
                            if c >= 3:
                                h = c - 3
                                pe.wait_ge(kept, n * QUADS + c)
                                if h == 0:
                                    after(pe, heads_kept, n - BEHIND[j] + 1)
                                to = pH[j % 2][h % 2 * 64:h % 2 * 64 + VW, h // 2, :]
                                pe.matmul(to, k.mixed[0:FLAST, FCH - 1, h * VW:(h + 1) * VW], restT[0:FLAST, h, :],
                                          start=True, stop=False)
                                for m in range(4):
                                    ins = pe.matmul(to, k.mixed[:, m, h * VW:(h + 1) * VW], headT[:, (h + 2) % 2, m, :],
                                                    start=False, stop=m == 3)
                                ins.then_inc(head_done, 1)
                        if real(n, 2):
                            i = (j - 2) % GT
                            project(n - 2, i % 2)
                            product(n - 2, i % 2, i)
                loop(pe, NG, group)
                turn_back(NT - 1)
                for i in (GT - 2, GT - 1):
                    project(NT - GT + i, i % 2)
                    product(NT - GT + i, i % 2, i)


def layer_first(nc, k, a):
    HID = 4 * C
    HC = HID // P
    HALF = GN // 2
    with ExitStack() as ctx:
        sb, ps, sem = scope(nc, ctx, "layer_first")
        t, s = norm_tensors(sb, sem)
        wp = sb("wp", [P, KC, C])
        w1 = sb("w1", [P, KC, HID])
        w2 = sb("w2", [P, HC, C])
        b1 = sb("b1", [P, HC])
        bp = sb("bp", [P, C])
        b2 = sb("b2", [P, C])
        gain = sb("gain", [P, KC])
        shift = sb("shift", [P, KC])
        den = sb("den", [P, GT, H0])
        rec = sb("rec", [P, GT, H0])
        mean = sb("mean", [P, GT, C])
        meanT = sb("meanT", [P, 2, KC, P])
        based = sb("based", [P, GT, C])
        mid = sb("mid", [P, GT, C])
        result = sb("result", [P, GT, C])
        hT = sb("hT", [P, KC, GN])
        hid = sb("hid", [P, HC, GN])
        pT = [ps(f"pT{i}", [P, KC, P]) for i in range(2)]
        pS = [ps(f"pS{i}", [P, C]) for i in range(2)]
        pW = [ps(f"pW{i}", [P, 2, 512]) for i in range(2)]
        loaded, den_ready, rec_ready, mean_ready = sem("loaded"), sem("den_ready"), sem("rec_ready"), sem("mean_ready")
        turned, kept, multiplied, taken = sem("turned"), sem("kept"), sem("multiplied"), sem("taken")
        wide_ready, gelu_ready, based_ready, result_base = sem("wide_ready"), sem("gelu_ready"), sem("based_ready"), sem("result_base")
        fence, done = sem("fence"), sem("done")

        with nc.Block() as block:
            @block.sync
            def _(sp):
                for n in range(KC):
                    sp.dma_start(wp[:, n, :], a["w_p"][n * P:(n + 1) * P, :]).then_inc(loaded, 16)
                    sp.dma_start(w1[:, n, :], a["w_1"][n * P:(n + 1) * P, :]).then_inc(loaded, 16)
                sp.dma_start(w2[:, :, :], a["w_2"].rearrange("(c p) n -> p c n", p=P)).then_inc(loaded, 16)
                for to, name in ((b1, "b_1"), (gain, "ln_g"), (shift, "ln_b")):
                    sp.dma_start(to[:, :], a[name]).then_inc(loaded, 16)
                sp.dma_start(bp[:, :], a["b_p"].partition_broadcast(P)).then_inc(loaded, 16)
                sp.dma_start(b2[:, :], a["b_2"].partition_broadcast(P)).then_inc(loaded, 16)
                sp.wait_ge(loaded, 160)

            @block.gpsimd
            def _(pool):
                pool.wait_ge(loaded, 160)

                def group(g):
                    after(pool, taken, 10 * g - 5)
                    pool.sem_inc(fence, 1)
                    pool.tensor_tensor(based[:, :, :], k.xn[:, bass.ds(g * GT, GT), :], spread(bp[:, :], 1, GT),
                                       ALU.add).then_inc(based_ready, 1)
                    deviations(pool, g, k, s, t)
                    after(pool, done, g * GT)
                    pool.wait_ge(taken, 10 * g + 5)
                    pool.tensor_tensor(result[:, :, :], mid[:, :, :], spread(b2[:, :], 1, GT), ALU.add).then_inc(result_base, 1)
                loop(pool, NG, group)

            @block.vector
            def _(dv):
                def group(g):
                    sums = k.sums[:, bass.ds(g * GT, GT), :]
                    dv.tensor_scalar(den[:, :, :], sums[:, :, C:SW], 1e-30, None, ALU.max).then_inc(den_ready, 1)
                    dv.wait_ge(den_ready, g + 1)
                    dv.reciprocal(rec[:, :, :], den[:, :, :]).then_inc(rec_ready, 1)
                    dv.wait_ge(rec_ready, g + 1)
                    after(dv, turned, 10 * g - 5)
                    dv.tensor_tensor(mean[:, :, :].rearrange("p t (h d) -> p t h d", h=H0),
                                     sums[:, :, 0:C].rearrange("p t (h d) -> p t h d", h=H0),
                                     spread(rec[:, :, :], 3, D0), ALU.mult).then_inc(mean_ready, 1)
                    dv.wait_ge(based_ready, g + 1)
                    after(dv, result_base, g)
                    for j in range(GT):
                        dv.wait_ge(multiplied, 10 * g + j + 1)
                        dv.tensor_tensor(mid[:, j, :], pS[j % 2][:, :], based[:, j, :], ALU.add).then_inc(taken, 1)
                    dv.wait_ge(taken, 10 * g + 5)
                    after(dv, turned, 10 * g)
                    normalise(dv, g, lambda g, j: mid[:, j, :], s, t)
                    dv.wait_ge(result_base, g + 1)
                    for j in range(GT):
                        dv.wait_ge(multiplied, 10 * g + 5 + j + 1)
                        dv.tensor_tensor(result[:, j, :], pS[(5 + j) % 2][:, :], result[:, j, :], ALU.add).then_inc(taken, 1)
                        dv.wait_ge(taken, 10 * g + 5 + j + 1)
                        nodes = k.x[:, bass.ds(g * GT + j, 1), :]
                        dv.tensor_tensor(nodes, nodes, result[:, j:j + 1, :], ALU.add).then_inc(done, 1)
                loop(dv, NG, group)

            @block.scalar
            def _(ac):
                ac.wait_ge(loaded, 160)

                def group(g):
                    for j in range(GT):
                        ac.wait_ge(turned, 10 * g + j + 1)
                        after(ac, multiplied, 10 * g + j - 1 if j >= 2 else 10 * g - GT)
                        ac.copy(meanT[:, j % 2, :, :], pT[j % 2][:, :, :]).then_inc(kept, 1)
                    for j in range(GT):
                        ac.wait_ge(turned, 10 * g + GT + j + 1)
                        after(ac, wide_ready, HC * g)
                        for c in range(KC):
                            ins = ac.activation(hT[:, c, j * P:(j + 1) * P], pT[(GT + j) % 2][:, c, :], ACT.Identity,
                                                bias=shift[:, c:c + 1], scale=gain[:, c:c + 1])
                        ins.then_inc(kept, 1)
                    after(ac, multiplied, 10 * g)
                    for m in range(HC):
                        ac.wait_ge(wide_ready, HC * g + m + 1)
                        ac.activation(hid[:, m, :].rearrange("p (a b) -> p a b", a=2), pW[m % 2][:, :, 0:HALF], ACT.Gelu,
                                      bias=b1[:, m:m + 1]).then_inc(gelu_ready, 1)
                loop(ac, NG, group)

            @block.tensor
            def _(pe):
                pe.wait_ge(loaded, 160)

                def turn(g, n, source, j):
                    after(pe, kept, 10 * g + n - 1)
                    for c in range(KC):
                        ins = pe.transpose(pT[n % 2][:, c, :], source[:, j, c * P:(c + 1) * P], k.ident[:, :])
                    ins.then_inc(turned, 1)

                def group(g):
                    pe.wait_ge(mean_ready, g + 1)
                    for j in range(GT + 1):
                        if j < GT:
                            turn(g, j, mean, j)
                        if j > 0:
                            m = j - 1
                            pe.wait_ge(kept, 10 * g + m + 1)
                            after(pe, taken, 10 * g + m - 1)
                            for c in range(KC):
                                ins = pe.matmul(pS[m % 2][:, :], meanT[:, m % 2, c, :], wp[:, c, :], start=c == 0, stop=c == KC - 1)
                            ins.then_inc(multiplied, 1)
                    for j in range(GT):
                        pe.wait_ge(s.normed_ready, g * GT + j + 1)
                        turn(g, GT + j, t.normed, j)
                    pe.wait_ge(kept, 10 * g + 10)
                    for m in range(HC):
                        after(pe, gelu_ready, HC * g + m - 1)
                        for half in range(2):
                            for c in range(KC):
                                ins = pe.matmul(pW[m % 2][:, half, 0:HALF], w1[:, c, m * P:(m + 1) * P],
                                                hT[:, c, half * HALF:(half + 1) * HALF], start=c == 0, stop=c == KC - 1)
                        ins.then_inc(wide_ready, 1)
                    for j in range(GT):
                        pe.wait_ge(gelu_ready, HC * g + HC)
                        after(pe, taken, 10 * g + GT + j - 1)
                        for m in range(HC):
                            ins = pe.matmul(pS[(GT + j) % 2][:, :], hid[:, m, j * P:(j + 1) * P], w2[:, m, :],
                                            start=m == 0, stop=m == HC - 1)
                        ins.then_inc(multiplied, 1)
                loop(pe, NG, group)


def experts(nc, k, a, second):
    wide = 2 * C if second else C
    MC = wide // P
    layers = 1 if second else 2
    HALF = GN // 2
    stage = "experts2" if second else "experts1"
    TURNS = GT + 3
    SMALL = 1 + GT + GT * NE
    WIDE = NE * layers * MC
    plan = []
    if second:
        plan = [("hidden", 0, 0), ("gates", 0, 0)]
        for e in range(NE):
            plan += [("hidden", 0, e + 1)] * (e + 1 < NE) + [("out", 0, e)]
    else:
        plan = [("hidden", 0, 0), ("hidden", 0, 1), ("hidden", 1, 0), ("gates", 0, 0)]
        for e in range(NE):
            plan += [("hidden", 0, e + 2)] * (e + 2 < NE) + [("hidden", 1, e + 1)] * (e + 1 < NE) + [("out", 0, e)]
    wides = [(layer, e, m) for what, layer, e in plan if what == "hidden" for m in range(MC)]
    nth = {w: i for i, w in enumerate(wides)}
    with ExitStack() as ctx:
        sb, ps, sem = scope(nc, ctx, stage)
        t, s = norm_tensors(sb, sem)
        if second:
            t2, s2 = norm_tensors(sb, sem, "_again")
            gain, shift = sb("gain", [P, KC]), sb("shift", [P, KC])
        else:
            t2, s2 = t, s
        w1 = sb("w1", [P, NE, KC, wide])
        w2 = sb("w2", [P, NE, KC, C]) if not second else None
        wo = sb("wo", [P, NE, MC, C])
        wr = sb("wr", [P, KC, NE])
        bo = sb("bo", [NE, C])
        br = sb("br", [P, NE])
        bn = sb("bn", [P, 2, 5, MC * NE]) if not second else None
        bn_eps = sb("bn_eps", [P, 2, MC * NE]) if not second else None
        scale = sb("scale", [P, 2, MC * NE]) if not second else None
        offset = sb("offset", [P, 2, MC * NE])
        hT = sb("hT", [P, KC, GN])
        act = [sb(f"act{n}", [P, 2, MC, GN]) for n in range(layers)]
        y = sb("y", [P, GT, C])
        logits = sb("logits", [P, GT, NE])
        shifted = sb("shifted", [P, GT, NE])
        odds = sb("odds", [P, GT, NE])
        gate = sb("gate", [P, GT, NE])
        gateT = sb("gateT", [NE, GN])
        top = sb("top", [P, GT])
        total = sb("total", [P, GT])
        if second:
            place = sb("place", [P, NE])
            found = sb("found", [P, GT, NE])
            one = [sb(f"one{n}", [P, GT, NE]) for n in range(2)]
            best = sb("best", [P, 2, GT])
            where = sb("where", [P, GT])
        pT = [ps(f"pT{i}", [P, KC, P]) for i in range(2)]
        pS = [ps(f"pS{i}", [P, 512]) for i in range(2)]
        pW = [ps(f"pW{i}", [P, 2, 512]) for i in range(2)]
        loaded, bn_ready, bn_power, offset_ready = sem("loaded"), sem("bn_ready"), sem("bn_power"), sem("offset_ready")
        turned, kept, wide_ready, act_ready = sem("turned"), sem("kept"), sem("wide_ready"), sem("act_ready")
        multiplied, taken, small, shifted_ready = sem("multiplied"), sem("taken"), sem("small"), sem("shifted_ready")
        odds_ready, gate_ready, done, placed = sem("odds_ready"), sem("gate_ready"), sem("done"), sem("placed")
        fold = sem("fold")
        LOADS = (2 * NE + 6) if second else (3 * NE + 4)

        with nc.Block() as block:
            @block.sync
            def _(sp):
                sp.dma_start(wr[:, :, :], a["w_r" + stage[-1]].rearrange("(c p) n -> p c n", p=P)).then_inc(loaded, 16)
                sp.dma_start(bo[:, :], a["b_o" + stage[-1]]).then_inc(loaded, 16)
                sp.dma_start(br[:, :], a["b_r" + stage[-1]].partition_broadcast(P)).then_inc(loaded, 16)
                if second:
                    sp.dma_start(offset[:, 0, :], a["b_hidden"]).then_inc(loaded, 16)
                    sp.dma_start(gain[:, :], a["gamma"]).then_inc(loaded, 16)
                    sp.dma_start(shift[:, :], a["beta"]).then_inc(loaded, 16)
                else:
                    sp.dma_start(bn[:, :, :, :], a["bn"]).then_inc(loaded, 16)
                for e in range(NE):
                    sp.dma_start(w1[:, e, :, :], a["w_hidden" + stage[-1]][e].rearrange("(c p) n -> p c n", p=P)).then_inc(loaded, 16)
                    if not second:
                        sp.dma_start(w2[:, e, :, :], a["w_deep"][e].rearrange("(c p) n -> p c n", p=P)).then_inc(loaded, 16)
                    sp.dma_start(wo[:, e, :, :], a["w_out" + stage[-1]][e].rearrange("(c p) n -> p c n", p=P)).then_inc(loaded, 16)
                sp.wait_ge(loaded, 16 * LOADS)

            @block.gpsimd
            def _(pool):
                if second:
                    pool.iota(place[:, :], [[1, NE]], base=0, channel_multiplier=0,
                              allow_small_or_imprecise_dtypes=True).then_inc(placed, 1)
                else:
                    pool.wait_ge(bn_ready, 1)
                    pool.tensor_tensor(scale[:, :, :].rearrange("p l n -> p (l n)"), bn_eps[:, :, :].rearrange("p l n -> p (l n)"),
                                       k.power[:, 0:2 * MC * NE], ALU.pow).then_inc(bn_power, 1)

                def group(g):
                    deviations(pool, g, k, s, t)
                    if second:
                        deviations(pool, g, k, s2, t2)
                loop(pool, NG, group)

            @block.vector
            def _(dv):
                dv.wait_ge(loaded, 16 * LOADS)
                if not second:
                    dv.tensor_scalar(bn_eps[:, :, :], bn[:, :, 3, :], 1e-3, None, ALU.add).then_inc(bn_ready, 1)
                    dv.wait_ge(bn_power, 1)
                    chain = Chain(dv, fold, 4)
                    chain.turn(0)
                    chain(dv.tensor_tensor(scale[:, :, :], scale[:, :, :], bn[:, :, 0, :], ALU.mult))
                    chain(dv.tensor_tensor(offset[:, :, :], bn[:, :, 4, :], bn[:, :, 2, :], ALU.subtract))
                    chain(dv.tensor_tensor(offset[:, :, :], offset[:, :, :], scale[:, :, :], ALU.mult))
                    chain(dv.tensor_tensor(offset[:, :, :], offset[:, :, :], bn[:, :, 1, :], ALU.add))
                else:
                    dv.wait_ge(placed, 1)
                chain = Chain(dv, small, 17 if second else 4)

                def softmax(g):
                    chain(dv.tensor_reduce(top[:, :], logits[:, :, :], AX, ALU.max))
                    dv.tensor_tensor(shifted[:, :, :], logits[:, :, :], spread(top[:, :], 2, NE), ALU.subtract).then_inc(shifted_ready, 1)
                    dv.wait_ge(odds_ready, g + 1)
                    chain(dv.tensor_reduce(total[:, :], odds[:, :, :], AX, ALU.add))
                    chain(dv.reciprocal(total[:, :], total[:, :]))
                    dv.tensor_tensor(gate[:, :, :], odds[:, :, :], spread(total[:, :], 2, NE), ALU.mult).then_inc(gate_ready, 1)

                def two_best(g):
                    places = spread(place[:, :], 1, GT)
                    for n in range(2):
                        chain(dv.tensor_reduce(best[:, n, :], logits[:, :, :], AX, ALU.max))
                        chain(dv.tensor_tensor(found[:, :, :], logits[:, :, :], spread(best[:, n, :], 2, NE), ALU.is_lt))
                        chain(dv.tensor_scalar(found[:, :, :], found[:, :, :], float(NE), None, ALU.mult))
                        chain(dv.tensor_tensor(found[:, :, :], found[:, :, :], places, ALU.add))
                        chain(dv.tensor_reduce(where[:, :], found[:, :, :], AX, ALU.min))
                        chain(dv.tensor_tensor(one[n][:, :, :], places, spread(where[:, :], 2, NE), ALU.is_equal))
                        if n == 0:
                            chain(dv.scalar_tensor_tensor(out=logits[:, :, :], in0=one[0][:, :, :], scalar=-BIG, in1=logits[:, :, :],
                                                          op0=ALU.mult, op1=ALU.add))
                    dv.tensor_tensor(shifted[:, :, 0], best[:, 1, :], best[:, 0, :], ALU.subtract).then_inc(shifted_ready, 1)
                    dv.wait_ge(odds_ready, g + 1)
                    chain(dv.tensor_scalar(total[:, :], odds[:, :, 0], 1.0, None, ALU.add))
                    chain(dv.reciprocal(total[:, :], total[:, :]))
                    chain(dv.tensor_tensor(top[:, :], odds[:, :, 0], total[:, :], ALU.mult))
                    dv.tensor_tensor(one[0][:, :, :], one[0][:, :, :], spread(total[:, :], 2, NE), ALU.mult)
                    dv.tensor_tensor(one[1][:, :, :], one[1][:, :, :], spread(top[:, :], 2, NE), ALU.mult).then_inc(small, 1)
                    chain.left -= 1
                    dv.wait_ge(small, chain.count + chain.per - chain.left)
                    dv.tensor_tensor(gate[:, :, :], one[0][:, :, :], one[1][:, :, :], ALU.add).then_inc(gate_ready, 1)

                def group(g):
                    chain.turn(g)
                    after(dv, turned, TURNS * g)
                    nodes = lambda g, j: k.x[:, bass.ds(g * GT + j, 1), :]
                    normalise(dv, g, nodes, s, t)
                    if second:
                        dv.wait_ge(s.normed_ready, g * GT + GT)
                        normalise(dv, g, lambda g, j: t.normed[:, j, :], s2, t2)
                    dv.wait_ge(multiplied, SMALL * g + 1)
                    dv.tensor_tensor(logits[:, :, :], pS[0][:, 0:GT * NE].rearrange("p (t e) -> p t e", t=GT),
                                     spread(br[:, :], 1, GT), ALU.add).then_inc(taken, 1)
                    dv.wait_ge(taken, SMALL * g + 1)
                    (two_best if second else softmax)(g)
                    if not second:
                        chain.left -= 1
                        dv.tensor_copy(top[:, :], total[:, :]).then_inc(small, 1)
                    assert chain.left == 0, chain.left
                    for j in range(GT):
                        dv.wait_ge(multiplied, SMALL * g + 2 + j)
                        dv.tensor_copy(y[:, j, :], pS[(1 + j) % 2][:, 0:C]).then_inc(taken, 1)
                    for e in range(NE):
                        for j in range(GT):
                            n = 1 + GT + e * GT + j
                            dv.wait_ge(multiplied, SMALL * g + n + 1)
                            dv.wait_ge(taken, SMALL * g + n - GT + 1)
                            dv.scalar_tensor_tensor(out=y[:, j, :], in0=pS[n % 2][:, 0:C], scalar=gate[:, j, e:e + 1], in1=y[:, j, :],
                                                    op0=ALU.mult, op1=ALU.add).then_inc(taken, 1)
                    dv.wait_ge(taken, SMALL * g + SMALL)
                    nodes = k.x[:, bass.ds(g * GT, GT), :]
                    dv.tensor_tensor(nodes, nodes, y[:, :, :], ALU.add).then_inc(done, 1)
                loop(dv, NG, group)

            @block.scalar
            def _(ac):
                ac.wait_ge(loaded, 16 * LOADS)
                if not second:
                    ac.wait_ge(fold, 4)

                def group(g):
                    for j in range(GT):
                        ac.wait_ge(turned, TURNS * g + j + 1)
                        after(ac, wide_ready, WIDE * g)
                        for c in range(KC):
                            if second:
                                ins = ac.activation(hT[:, c, j * P:(j + 1) * P], pT[j % 2][:, c, :], ACT.Identity,
                                                    bias=shift[:, c:c + 1], scale=gain[:, c:c + 1])
                            else:
                                ins = ac.copy(hT[:, c, j * P:(j + 1) * P], pT[j % 2][:, c, :])
                        ins.then_inc(kept, 1)
                    for what, layer, e in plan:
                        if what == "hidden":
                            for m in range(MC):
                                n = nth[layer, e, m]
                                ac.wait_ge(wide_ready, WIDE * g + n + 1)
                                if layer < layers - 1:
                                    after(ac, wide_ready, WIDE * g + nth[layer + 1, e - 2, MC - 1] + 1 if e >= 2
                                          else WIDE * (g - 1) + nth[layer + 1, NE - 2 + e, MC - 1] + 1)
                                else:
                                    after(ac, multiplied, SMALL * g + 1 + GT + (e - 1) * GT if e >= 2
                                          else SMALL * (g - 1) + 1 + GT + (NE - 1 + e) * GT)
                                to = act[layer][:, e % 2, m, :].rearrange("p (a b) -> p a b", a=2)
                                if second:
                                    ac.activation(to, pW[n % 2][:, :, 0:HALF], ACT.Gelu,
                                                  bias=offset[:, 0, m * NE + e:m * NE + e + 1]).then_inc(act_ready, 1)
                                else:
                                    ac.activation(to, pW[n % 2][:, :, 0:HALF], ACT.Relu,
                                                  bias=offset[:, layer, m * NE + e:m * NE + e + 1],
                                                  scale=scale[:, layer, m * NE + e:m * NE + e + 1]).then_inc(act_ready, 1)
                        elif what == "gates":
                            ac.wait_ge(shifted_ready, g + 1)
                            n = 1 if second else NE
                            ac.activation(odds[:, :, 0:n], shifted[:, :, 0:n], ACT.Exp).then_inc(odds_ready, 1)
                            for q in range(3):
                                i = GT + q
                                tiles = 2 if q < 2 else 1
                                ac.wait_ge(turned, TURNS * g + i + 1)
                                after(ac, multiplied, SMALL * g - GT * NE)
                                ac.copy(gateT[:, q * 2 * P:(q * 2 + tiles) * P].rearrange("e (t n) -> e t n", n=P),
                                        pT[i % 2][0:NE, 0:tiles, :]).then_inc(kept, 1)
                loop(ac, NG, group)

            @block.tensor
            def _(pe):
                pe.wait_ge(loaded, 16 * LOADS)

                def group(g):
                    for j in range(GT):
                        pe.wait_ge(s2.normed_ready, g * GT + j + 1)
                        after(pe, kept, TURNS * g + j - 1)
                        for c in range(KC):
                            ins = pe.transpose(pT[j % 2][:, c, :], t2.normed[:, j, c * P:(c + 1) * P], k.ident[:, :])
                        ins.then_inc(turned, 1)
                    pe.wait_ge(kept, TURNS * g + GT)
                    after(pe, taken, SMALL * g - 1)
                    for j in range(GT):
                        for c in range(KC):
                            ins = pe.matmul(pS[0][:, j * NE:(j + 1) * NE], hT[:, c, j * P:(j + 1) * P], wr[:, c, :],
                                            start=c == 0, stop=c == KC - 1)
                    ins.then_inc(multiplied, 1)
                    for what, layer, e in plan:
                        if what == "hidden":
                            if layer:
                                pe.wait_ge(act_ready, WIDE * g + nth[layer - 1, e, MC - 1] + 1)
                            weights = w2 if layer else w1
                            for m in range(MC):
                                n = nth[layer, e, m]
                                after(pe, act_ready, WIDE * g + n - 1)
                                for half in range(2):
                                    span = slice(half * HALF, (half + 1) * HALF)
                                    for c in range(KC):
                                        moving = act[0][:, e % 2, c, span] if layer else hT[:, c, span]
                                        ins = pe.matmul(pW[n % 2][:, half, 0:HALF], weights[:, e, c, m * P:(m + 1) * P], moving,
                                                        start=c == 0, stop=c == KC - 1)
                                ins.then_inc(wide_ready, 1)
                        elif what == "gates":
                            pe.wait_ge(gate_ready, g + 1)
                            for q in range(3):
                                i = GT + q
                                after(pe, kept, TURNS * g + i - 1)
                                for j in range(2 * q, min(2 * q + 2, GT)):
                                    ins = pe.transpose(pT[i % 2][0:NE, j % 2, :], gate[:, j, :], k.ident[:, :])
                                ins.then_inc(turned, 1)
                            pe.wait_ge(kept, TURNS * g + TURNS)
                            for j in range(GT):
                                n = 1 + j
                                after(pe, taken, SMALL * g + n - 1)
                                pe.matmul(pS[n % 2][:, 0:C], gateT[:, j * P:(j + 1) * P], bo[:, :], start=True,
                                          stop=True).then_inc(multiplied, 1)
                        else:
                            pe.wait_ge(act_ready, WIDE * g + nth[layers - 1, e, MC - 1] + 1)
                            for j in range(GT):
                                n = 1 + GT + e * GT + j
                                after(pe, taken, SMALL * g + n - 1)
                                for m in range(MC):
                                    ins = pe.matmul(pS[n % 2][:, 0:C], act[layers - 1][:, e % 2, m, j * P:(j + 1) * P], wo[:, e, m, :],
                                                    start=m == 0, stop=m == MC - 1)
                                ins.then_inc(multiplied, 1)
                loop(pe, NG, group)


EP = 125
EJ = EDGES // EP
GB = 8


def project_second(nc, k, a):
    HK = 2 * HM
    ZW = C + 2 * H1
    W = ZW + HK * DM
    PAIRS = HM * DM // P
    with ExitStack() as ctx:
        sb, ps, sem = scope(nc, ctx, "project_second")
        t, s = norm_tensors(sb, sem)
        w = sb("w", [P, KC, W])
        natural = sb("natural", [P, KC, C])
        vectors = sb("vectors", [P, KC, 2 * H1])
        xT = sb("xT", [P, 2, KC, P])
        outs = sb("outs", [P, 2, ZW])
        total = sb("total", [P, HK])
        mean = sb("mean", [P, HK])
        centred = sb("centred", [P, 2, HK, DM])
        square = sb("square", [P, HK, DM])
        var = sb("var", [P, HK])
        vareps = sb("vareps2", [P, HK])
        rstd = sb("rstd2", [P, HK])
        factor = sb("factor", [P, 2, HK])
        kv = sb("kv", [P, 2, HK * DM])
        zeros = sb("zeros", [P, 512])
        pT = ps("pT", [P, KC, P])
        pM = [ps(f"pM{i}", [P, 3, 512]) for i in range(2)]
        pD = ps("pD", [P, PAIRS, P])
        loaded, folded, fold_kept, zeroed = sem("loaded"), sem("folded"), sem("fold_kept"), sem("zeroed")
        xT_psum, xT_ready, xT_kept, projected = sem("xT_psum"), sem("xT_ready"), sem("xT_kept"), sem("projected")
        z_ready, summed, mean_ready, centred_ready = sem("z_ready"), sem("summed"), sem("mean_ready"), sem("centred_ready")
        squared, var_ready, vareps_ready, rstd_ready = sem("squared"), sem("var_ready"), sem("vareps2_ready"), sem("rstd2_ready")
        factor_ready, kv_ready, dots_done, cleared = sem("factor_ready"), sem("kv_ready"), sem("dots_done"), sem("cleared")
        kept = sem("kept")
        stored = [sem("stored0"), sem("stored1")]

        def running(g, j, back):
            return j >= back or not isinstance(g, int)

        with nc.Block() as block:
            @block.sync
            def _(sp):
                for n in range(KC):
                    rows = slice(n * P, (n + 1) * P)
                    sp.dma_start(w[:, n, 0:C], a["w_z1"][rows, :]).then_inc(loaded, 16)
                    sp.dma_start(w[:, n, ZW:W], a["w_mixkv"][rows, :]).then_inc(loaded, 16)
                    sp.dma_start(natural[:, n, :], a["w_natural1"][rows, :]).then_inc(loaded, 16)
                    sp.dma_start(vectors[:, n, :], a["vectors1"][rows, :]).then_inc(loaded, 16)

                def group(g):
                    for j in range(GT):
                        n, u = g * GT + j, j % 2
                        sp.wait_ge(z_ready, n + 1)
                        rows = bass.ds(n * P, P)
                        sp.dma_start(k.z_table[rows, :], outs[:, u, 0:C]).then_inc(stored[u], 16)
                        sp.dma_start(k.es_table1[rows, :], outs[:, u, C:C + H1]).then_inc(stored[u], 16)
                loop(sp, NG, group)
                for u in range(2):
                    sp.wait_ge(stored[u], 32 * USES[u] * NG)

            @block.gpsimd
            def _(pool):
                pool.memset(zeros[:, :], 0.0).then_inc(zeroed, 1)

                def scale(n, u, j):
                    pool.wait_ge(vareps_ready, n + 1)
                    pool.tensor_tensor(rstd[:, :], vareps[:, :], k.power[:, 0:HK], ALU.pow).then_inc(rstd_ready, 1)
                    pool.wait_ge(factor_ready, n + 1)
                    after(pool, dots_done, n - BEHIND[j] + 1)
                    pool.tensor_tensor(kv[:, u, :].rearrange("p (h d) -> p h d", h=HK), centred[:, u, :, :],
                                       spread(factor[:, u, :], 2, DM), ALU.mult).then_inc(kv_ready, 1)

                def group(g):
                    deviations(pool, g, k, s, t)
                    for j in range(GT):
                        if running(g, j, 1):
                            i = (j - 1) % GT
                            scale(g * GT + j - 1, i % 2, i)
                loop(pool, NG, group)
                scale(NT - 1, (GT - 1) % 2, GT - 1)

            @block.vector
            def _(dv):
                dv.memset(k.dots[:, :, :], 0.0).then_inc(cleared, 1)
                dv.wait_ge(folded, 1)
                dv.tensor_copy(w[:, :, C:ZW], pT[:, :, 0:2 * H1]).then_inc(fold_kept, 1)

                def centre(n, u, j):
                    heads = pM[u][:, 1:3, :].rearrange("p b (h d) -> p (b h) d", d=DM)
                    dv.wait_ge(projected, 2 * n + 2)
                    dv.tensor_reduce(total[:, :], heads, AX, ALU.add).then_inc(summed, 1)
                    dv.wait_ge(summed, n + 1)
                    dv.tensor_scalar(mean[:, :], total[:, :], 1.0 / DM, None, ALU.mult).then_inc(mean_ready, 1)
                    dv.wait_ge(mean_ready, n + 1)
                    after(dv, kv_ready, n - BEHIND[j] + 1)
                    dv.tensor_tensor(centred[:, u, :, :], heads, spread(mean[:, :], 2, DM), ALU.subtract).then_inc(centred_ready, 1)

                def deviate(n, u):
                    dv.wait_ge(squared, n + 1)
                    dv.tensor_reduce(var[:, :], square[:, :, :], AX, ALU.add).then_inc(var_ready, 1)
                    dv.wait_ge(var_ready, n + 1)
                    dv.tensor_scalar(vareps[:, :], var[:, :], 1.0 / DM, 1e-5, ALU.mult, ALU.add).then_inc(vareps_ready, 1)
                    dv.wait_ge(rstd_ready, n + 1)
                    dv.tensor_copy(factor[:, u, 0:HM], rstd[:, 0:HM])
                    dv.tensor_scalar(factor[:, u, HM:HK], rstd[:, HM:HK], k.share[:, bass.ds(n, 1)], None,
                                     ALU.mult).then_inc(factor_ready, 1)

                def group(g):
                    after(dv, xT_psum, GT * g)
                    normalise(dv, g, lambda g, j: k.x[:, bass.ds(g * GT + j, 1), :], s, t)
                    for j in range(GT):
                        n = g * GT + j
                        if running(g, j, 1) and j == 0:
                            deviate(n - 1, (GT - 1) % 2)
                        centre(n, j % 2, j)
                        if j > 0:
                            deviate(n - 1, (j - 1) % 2)
                loop(dv, NG, group)
                deviate(NT - 1, (GT - 1) % 2)
                dv.wait_ge(dots_done, NT)
                dv.wait_ge(cleared, 1)
                for lo in (0, DM):
                    dv.tensor_copy(k.dots[lo:lo + DM, :, lo:lo + DM], pD[lo:lo + DM, :, lo:lo + DM]).then_inc(kept, 1)

            @block.scalar
            def _(ac):
                ac.wait_ge(fold_kept, 1)

                def keep(n, j):
                    u = j % 2
                    ac.wait_ge(xT_psum, n + 1)
                    after(ac, projected, 2 * (n - BEHIND[j] + 1))
                    ac.copy(xT[:, u, :, :], pT[:, :, :]).then_inc(xT_ready, 1)
                    ac.wait_ge(xT_ready, n + 1)
                    ac.copy(k.xn[:, bass.ds(n, 1), :], xT[:, u:u + 1, :, :].rearrange("p a c n -> p a (c n)")).then_inc(xT_kept, 1)

                def squares(n, u):
                    ac.wait_ge(centred_ready, n + 1)
                    after(ac, var_ready, n)
                    ac.activation(square[:, :, :], centred[:, u, :, :], ACT.Square).then_inc(squared, 1)

                def group(g):
                    keep(g * GT, 0)
                    for j in range(GT):
                        n, u = g * GT + j, j % 2
                        if j + 1 < GT:
                            keep(n + 1, j + 1)
                        if running(g, j, 1):
                            squares(n - 1, (j - 1) % GT % 2)
                        ac.wait_ge(projected, 2 * n + 1)
                        after(ac, stored[u], 32 * uses(g, j))
                        ac.copy(k.ed[:, bass.ds(n, 1), :], pM[u][:, 0:1, C + H1:ZW])
                        ac.copy(outs[:, u, :], pM[u][:, 0, 0:ZW]).then_inc(z_ready, 1)
                loop(ac, NG, group)
                squares(NT - 1, (GT - 1) % 2)

            @block.tensor
            def _(pe):
                pe.wait_ge(loaded, 128)
                for m in range(KC):
                    for c in range(KC):
                        ins = pe.matmul(pT[:, m, 0:2 * H1], natural[:, c, m * P:(m + 1) * P], vectors[:, c, :],
                                        start=c == 0, stop=c == KC - 1)
                ins.then_inc(folded, 1)
                pe.wait_ge(zeroed, 1)
                pe.matmul(pD[:, :, :], zeros[:, 0:P], zeros[:, :], start=True, stop=False, skip_group_check=True)
                pe.wait_ge(fold_kept, 1)

                def turn(n, j):
                    pe.wait_ge(s.normed_ready, n + 1)
                    after(pe, xT_ready, n)
                    for c in range(KC):
                        ins = pe.transpose(pT[:, c, :], t.normed[:, j, c * P:(c + 1) * P], k.ident[:, :])
                    ins.then_inc(xT_psum, 1)

                def dots(n, u):
                    pe.wait_ge(kv_ready, n + 1)
                    for m in range(PAIRS):
                        ins = pe.matmul(pD[:, m, :], kv[:, u, HM * DM + m * P:HM * DM + (m + 1) * P], kv[:, u, m * P:(m + 1) * P],
                                        start=False, stop=False, skip_group_check=True)
                    ins.then_inc(dots_done, 1)

                def group(g):
                    turn(g * GT, 0)
                    for j in range(GT):
                        n, u = g * GT + j, j % 2
                        if j + 1 < GT:
                            turn(n + 1, j + 1)
                        pe.wait_ge(xT_ready, n + 1)
                        for b, (lo, hi) in enumerate(((0, ZW), (ZW, ZW + 512), (ZW + 512, W))):
                            if b < 2:
                                after(pe, (z_ready, centred_ready)[b], n - BEHIND[j] + 1)
                            for q in range(KC):
                                ins = pe.matmul(pM[u][:, b, 0:hi - lo], xT[:, u, q, :], w[:, q, lo:hi], start=q == 0, stop=q == KC - 1)
                            if b != 1:
                                ins.then_inc(projected, 1)
                        if running(g, j, 2):
                            dots(n - 2, (j - 2) % GT % 2)
                loop(pe, NG, group)
                dots(NT - 2, (GT - 2) % 2)
                dots(NT - 1, (GT - 1) % 2)


def mix_second(nc, k, a):
    PAIRS = HM * DM // P
    with ExitStack() as ctx:
        sb, ps, sem = scope(nc, ctx, "mix_second")
        wq = sb("wq", [P, PAIRS, C])
        wo = sb("wo", [P, PAIRS, C])
        bias = sb("bias", [1, C])
        inner = sb("inner", [P, PAIRS, C])
        whole = sb("whole", [P, KC, C])
        xT = sb("xT", [P, 2, KC, P])
        pG = ps("pG", [P, PAIRS, C])
        pW = ps("pW", [P, KC, C])
        pO = [ps(f"pO{i}", [P, C]) for i in range(2)]
        loaded, inner_psum, inner_ready, whole_psum = sem("loaded"), sem("inner_psum"), sem("inner_ready"), sem("whole_psum")
        whole_ready, xT_ready, projected, done = sem("whole_ready"), sem("xT_ready"), sem("projected"), sem("done")

        with nc.Block() as block:
            @block.sync
            def _(sp):
                sp.dma_start(wq[:, :, :], a["w_mixq"].rearrange("(c p) n -> p c n", p=P)).then_inc(loaded, 16)
                sp.dma_start(wo[:, :, :], a["w_mixout"].rearrange("(c p) n -> p c n", p=P)).then_inc(loaded, 16)
                sp.dma_start(bias[:, :], a["b_mixout"]).then_inc(loaded, 16)

            @block.vector
            def _(dv):
                def group(g):
                    for j in range(GT):
                        n, u = g * GT + j, j % 2
                        dv.wait_ge(projected, n + 1)
                        nodes = k.x[:, bass.ds(n, 1), :]
                        dv.tensor_tensor(nodes, nodes, pO[u].rearrange("p (a c) -> p a c", a=1), ALU.add).then_inc(done, 1)
                loop(dv, NG, group)

            @block.scalar
            def _(ac):
                ac.wait_ge(inner_psum, 1)
                ac.copy(inner[:, :, :], pG[:, :, :]).then_inc(inner_ready, 1)
                ac.wait_ge(whole_psum, 1)
                ac.copy(whole[:, :, :], pW[:, :, :]).then_inc(whole_ready, 1)

                def group(g):
                    for j in range(GT):
                        n, u = g * GT + j, j % 2
                        after(ac, projected, n - BEHIND[j] + 1)
                        ac.copy(xT[:, u:u + 1, :, :].rearrange("p a c n -> p a (c n)"), k.xn[:, bass.ds(n, 1), :]).then_inc(xT_ready, 1)
                loop(ac, NG, group)

            @block.tensor
            def _(pe):
                pe.wait_ge(loaded, 48)
                for m in range(PAIRS):
                    ins = pe.matmul(pG[:, m, :], k.dots[:, m, :], wo[:, m, :], start=True, stop=True)
                ins.then_inc(inner_psum, 1)
                pe.wait_ge(inner_ready, 1)
                for m in range(KC):
                    for c in range(PAIRS):
                        ins = pe.matmul(pW[:, m, :], wq[:, c, m * P:(m + 1) * P], inner[:, c, :], start=c == 0, stop=c == PAIRS - 1)
                ins.then_inc(whole_psum, 1)
                pe.wait_ge(whole_ready, 1)

                def group(g):
                    for j in range(GT):
                        n, u = g * GT + j, j % 2
                        pe.wait_ge(xT_ready, n + 1)
                        after(pe, done, n - BEHIND[j] + 1)
                        pe.matmul(pO[u][:, :], k.ones[0:1, :], bias[:, :], start=True, stop=False)
                        for c in range(KC):
                            ins = pe.matmul(pO[u][:, :], xT[:, u, c, :], whole[:, c, :], start=False, stop=c == KC - 1)
                        ins.then_inc(projected, 1)
                loop(pe, NG, group)


def edge_odds(nc, k, a, H, es_table, ed, src_scores, src_most):
    stage = f"odds{H}"
    NBG = EJ // GB
    with ExitStack() as ctx:
        sb, ps, sem = scope(nc, ctx, stage)
        t, s = Core(), Core()
        t.hot = sb("hot", [P, DEEP, BATCH, P])
        t.hotT = sb("hotT", [P, 2, BATCH, P])
        t.p_hotT = ps("p_hotT", [P, BATCH, P])
        look = [ps(f"look{u}", [P, BATCH, H]) for u in range(2)]
        s.hot_ready, s.hotT_psum, s.hotT_ready, s.looked_up = sem("hot_ready"), sem("hotT_psum"), sem("hotT_ready"), sem("looked_up")
        look_kept = sem("look_kept")
        src = sb("src", [EP, EJ], I32)
        dst = sb("dst", [EP, EJ], I32)
        index = sb("index", [EP, 2, GB], I32)
        got = sb("got", [EP, 2, GB, H])
        es = sb("es", [EP, EJ, H])
        forth = sb("forth", [EP, EJ, H])
        back = sb("back", [EP, EJ, H])
        seg = sb("seg", [EP, EJ])
        enter = sb("enter", [EP, EJ])
        leave = sb("leave", [EP, EJ])
        other = sb("other", [EP, 2, EJ])
        NCOL = 2 + 2 * H
        diag = sb("diag", [EP, NCOL, P])
        lines = sb("lines", [EP, NCOL, P])
        barred = sb("barred", [EP, 2, 2, P])
        parts = sb("parts", [EP, 2, 2, H, P])
        ends = sb("ends", [EP, 2, 2, H])
        end = sb("end", [EP, 2, H])
        rows = sb("rows", [PB, 2, BLK, EW * H])
        rest = sb("rest", [1, (EROWS * EW - EDGES) * H])
        looked = sb("looked", [P, NP * SUB, H])
        score = sb("score", [P, 2, NP * SUB, H])
        pL = ps("pL", [P, NCOL, P])
        pR = ps("pR", [P, BLK * SUB, P])
        edges_in, fence, index_ready = sem("edges_in"), sem("fence"), sem("index_ready")
        rows_in, taken = [sem("rows_in0"), sem("rows_in1")], [sem("taken0"), sem("taken1")]
        step, diag_ready, lines_psum, most_ready = sem("step"), sem("diag_ready"), sem("lines_psum"), sem("most_ready")
        stored, rest_set, pair_rows, last = sem("stored"), sem("rest_set"), sem("pair_rows"), sem("last")
        turned, kept, cleared, less = sem("turned"), sem("kept"), sem("cleared"), sem("less")

        with nc.Block() as block:
            @block.sync
            def _(sp):
                sp.dma_start(src[:, :], a["src"].rearrange("(p j) -> p j", p=EP)).then_inc(edges_in, 16)
                sp.dma_start(dst[:, :], a["dst"].rearrange("(p j) -> p j", p=EP)).then_inc(edges_in, 16)

                def steps(i):
                    for u in range(2):
                        sp.wait_ge(rows_in[u], 16 * GB * (i + 1))
                        sp.dma_start(es[:, bass.ds((2 * i + u) * GB, GB), :], got[:, u, :, :]).then_inc(taken[u], 16)
                loop(sp, NBG // 2, steps)
                sp.wait_ge(rest_set, 1)
                for n, (table, values) in enumerate(((src_scores, es), (src_most, forth))):
                    flat = table.rearrange("a b -> (a b)")
                    if n == 0:
                        for u in range(2):
                            sp.wait_ge(taken[u], 16 * NBG // 2)
                    else:
                        sp.wait_ge(most_ready, 1)
                    sp.dma_start(flat[0:EDGES * H].rearrange("(p j) -> p j", p=EP),
                                 values.rearrange("p j h -> p (j h)")).then_inc(stored, 16)
                    sp.dma_start(flat[EDGES * H:EROWS * EW * H].rearrange("(p j) -> p j", p=1), rest[:, :]).then_inc(stored, 16)
                sp.wait_ge(stored, 64)

            @block.gpsimd
            def _(pool):
                pool.memset(rest[:, :], 0.0).then_inc(rest_set, 1)
                pool.memset(k.sums[:, :, :], 0.0).then_inc(cleared, 1)
                pool.wait_ge(edges_in, 32)

                def steps(i):
                    for u in range(2):
                        b = 2 * i + u
                        after(pool, taken[u], 16 * i)
                        pool.sem_inc(fence, 1)
                        pool.tensor_copy(index[:, u, :], src[:, bass.ds(b * GB, GB)]).then_inc(index_ready, 1)
                        pool.wait_ge(index_ready, b + 1)
                        pool.sem_inc(fence, 1)
                        for m in range(GB):
                            pool.indirect_dma_start(got[:, u, m, :], None, es_table,
                                                    bass.IndirectOffsetOnAxis(ap=index[:, u, m:m + 1], axis=0)).then_inc(rows_in[u], 16)
                loop(pool, NBG // 2, steps)
                pool.wait_ge(stored, 64)
                for n, table in enumerate((src_scores, src_most)):
                    for b in range(BLK):
                        pool.indirect_dma_start(rows[:, n, b, :], None, table,
                                                bass.IndirectOffsetOnAxis(ap=k.tile_i[:, b:b + 1], axis=0)).then_inc(pair_rows, 16)

            @block.vector
            def _(dv):
                edge_hot(dv, 0, 0, k, t, s, s.hotT_psum)
                edge_loop(dv, lambda b, u, i: edge_hot(dv, b + 1, u + 1, k, t, s, s.hotT_psum))
                chain = Chain(dv, step, 20)
                chain.turn(0)
                dv.wait_ge(edges_in, 32)
                chain(dv.tensor_copy(seg[:, :], dst[:, :]))
                chain(dv.tensor_tensor(leave[:, 0:EJ - 1], seg[:, 0:EJ - 1], seg[:, 1:EJ], ALU.is_equal))
                chain(dv.tensor_scalar(leave[:, 0:EJ - 1], leave[:, 0:EJ - 1], 1.0, BIG, ALU.subtract, ALU.mult))
                chain(dv.memset(leave[:, EJ - 1:EJ], -BIG))
                chain(dv.tensor_copy(enter[:, 1:EJ], leave[:, 0:EJ - 1]))
                chain(dv.memset(enter[:, 0:1], -BIG))
                for end_of in range(2):
                    at = (EJ - 1) * end_of
                    chain(dv.tensor_scalar(other[:, end_of, :], seg[:, :], seg[:, at:at + 1], 1.0, ALU.is_equal, ALU.subtract))
                chain(dv.tensor_scalar(other[:, :, :], other[:, :, :], BIG, None, ALU.mult))
                for u in range(2):
                    dv.wait_ge(taken[u], 16 * NBG // 2)
                for h in range(H):
                    dv.tensor_tensor_scan(forth[:, :, h], enter[:, :], es[:, :, h], -BIG, ALU.add, ALU.max)
                    ins = dv.tensor_tensor_scan(backwards(back[:, :, h]), backwards(leave[:, :]), backwards(es[:, :, h]), -BIG,
                                                ALU.add, ALU.max)
                chain(ins)
                columns = [seg[:, 0:1], seg[:, EJ - 1:EJ]] + [back[:, 0, h:h + 1] for h in range(H)] + \
                    [forth[:, EJ - 1, h:h + 1] for h in range(H)]
                for n, column in enumerate(columns):
                    ins = dv.tensor_scalar(diag[:, n, :], k.ident[0:EP, :], column, None, ALU.mult)
                ins.then_inc(diag_ready, 1)
                dv.wait_ge(lines_psum, 1)
                chain(dv.tensor_tensor(forth[:, :, :], forth[:, :, :], back[:, :, :], ALU.max))
                chain(dv.tensor_copy(lines[:, :, :], pL[0:EP, :, :]))
                for end_of in range(2):
                    at = (EJ - 1) * end_of
                    ins = dv.tensor_scalar(barred[:, end_of, :, 0:EP], lines[:, 0:2, 0:EP], seg[:, at:at + 1], 1.0, ALU.is_equal, ALU.subtract)
                chain(ins)
                chain(dv.tensor_scalar(barred[:, :, :, 0:EP], barred[:, :, :, 0:EP], BIG, None, ALU.mult))
                for end_of in range(2):
                    ins = dv.tensor_tensor(parts[:, end_of, :, :, 0:EP], spread(barred[:, end_of, :, 0:EP], 2, H),
                                           lines[:, 2:NCOL, 0:EP].rearrange("p (w h) n -> p w h n", w=2), ALU.add)
                chain(ins)
                for end_of in range(2):
                    ins = dv.tensor_reduce(ends[:, end_of, :, :], parts[:, end_of, :, :, 0:EP], AX, ALU.max)
                chain(ins)
                chain(dv.tensor_tensor(end[:, :, :], ends[:, :, 0, :], ends[:, :, 1, :], ALU.max))
                for end_of in range(2):
                    chain(dv.tensor_tensor(back[:, :, :], spread(other[:, end_of, :], 2, H), spread(end[:, end_of, :], 1, EJ), ALU.add))
                    if end_of == 0:
                        chain(dv.tensor_tensor(forth[:, :, :], forth[:, :, :], back[:, :, :], ALU.max))
                dv.tensor_tensor(forth[:, :, :], forth[:, :, :], back[:, :, :], ALU.max).then_inc(most_ready, 1)
                assert chain.left == 0, chain.left
                for n in range(2 * H):
                    dv.wait_ge(turned, n + 1)
                    dv.tensor_copy(score[:, n // H, :, n % H].rearrange("p (b i s) -> p b s i", b=BLK, s=SUB),
                                   pR.rearrange("p (b s) n -> p b s n", b=BLK)[:, :, :, 0:PB]).then_inc(kept, 1)
                dv.wait_ge(kept, 2 * H)
                dv.wait_ge(look_kept, NB)
                final = Chain(dv, last, 2)
                final.turn(0)
                final(dv.tensor_tensor(score[:, :, :, :], score[:, :, :, :], spread(looked[:, :, :], 1, 2), ALU.add))
                final(dv.scalar_tensor_tensor(out=score[:, :, :, :], in0=score[:, :, :, :], scalar=0.01, in1=score[:, :, :, :],
                                              op0=ALU.mult, op1=ALU.max))
                dv.tensor_tensor(score[:, 0, :, :], score[:, 0, :, :], score[:, 1, :, :], ALU.subtract).then_inc(less, 1)

            @block.scalar
            def _(ac):
                edge_keep(ac, 0, 0, t, s)

                def slot(b, u, i):
                    edge_keep(ac, b + 1, u + 1, t, s)
                    ac.wait_ge(s.looked_up, b + 1)
                    ac.copy(looked[:, bass.ds(b * BATCH, BATCH), :], look[u % 2][:, :, :]).then_inc(look_kept, 1)
                edge_loop(ac, slot)
                ac.wait_ge(less, 1)
                ac.activation(k.odds[:, :, 0:H], score[:, 0, :, :], ACT.Exp).then_inc(last, 1)

            @block.tensor
            def _(pe):
                edge_turn(pe, 0, 0, k, t, s)

                def slot(b, u, i):
                    edge_turn(pe, b + 1, u + 1, k, t, s)
                    windows = windows_of(pe, k, b)
                    pe.wait_ge(s.hotT_ready, b + 1)
                    after(pe, look_kept, b - 1)
                    for m in range(BATCH):
                        ins = pe.matmul(look[u % 2][:, m, :], t.hotT[:, u % 2, m, :], ed[:, bass.ds(windows[m // SUB], 1), 0:H],
                                        start=True, stop=True)
                    ins.then_inc(s.looked_up, 1)
                edge_loop(pe, slot)
                pe.wait_ge(diag_ready, 1)
                for n in range(NCOL):
                    ins = pe.matmul(pL[:, n, :], k.ones[0:EP, :], diag[:, n, :], start=True, stop=True)
                ins.then_inc(lines_psum, 1)
                pe.wait_ge(pair_rows, 32 * BLK)
                for n in range(2 * H):
                    after(pe, kept, n)
                    for b in range(BLK):
                        for m in range(SUB):
                            lanes = rows[:, n // H, b, m * P * H:(m + 1) * P * H].rearrange("p (n h) -> p n h", h=H)
                            ins = pe.transpose(pR[:, b * SUB + m, 0:PB], lanes[:, :, n % H], k.ident[0:PB, 0:PB])
                    ins.then_inc(turned, 1)


def backwards(ap):
    (partitions, lanes), (stride, n) = [list(x) for x in ap.ap]
    return bass.AP(tensor=ap.tensor, offset=ap.offset + (n - 1) * stride, ap=[[partitions, lanes], [-stride, n]])


def edge_sums(nc, k, H, table):
    W = C + H
    with ExitStack() as ctx:
        sb, ps, sem = scope(nc, ctx, f"sums{H}")
        t, s = Core(), Core()
        t.index = sb("index", [P, 2, DEEP * BATCH], I32)
        t.rows = sb("rows", [P, DEEP, BATCH, C])
        t.hot = sb("hot", [P, DEEP, BATCH, P])
        t.weighted = sb("weighted", [P, 2, BATCH, SW])
        t.p_sum = ps("p_sum", [P, 2 * BP, 512])
        s.fence, s.index_ready, s.hot_ready, s.weights_ready = sem("fence"), sem("index_ready"), sem("hot_ready"), sem("weights_ready")
        s.weighted_ready, s.summed, s.added = sem("weighted_ready"), sem("summed"), sem("added")
        s.rows_in = [sem(f"rows_in{u}") for u in range(DEEP)]

        with nc.Block() as block:
            @block.gpsimd
            def _(pool):
                edge_gather(pool, k, t, s, table, s.weighted_ready)

            @block.tensor
            def _(pe):
                def slot(b, u, i):
                    pe.wait_ge(s.weights_ready, b + 1)
                    edge_sum(pe, b, u, t, s, W)
                edge_loop(pe, slot)

            @block.scalar
            def _(ac):
                def slot(b, u, i):
                    after(ac, s.summed, b - 1)
                    ac.copy(t.weighted[:, u % 2, :, C:W], k.odds[:, bass.ds(b * BATCH, BATCH), 0:H]).then_inc(s.weights_ready, 1)
                edge_loop(ac, slot)

            @block.vector
            def _(dv):
                edge_hot(dv, 0, 0, k, t, s, s.summed)

                def slot(b, u, i):
                    edge_hot(dv, b + 1, u + 1, k, t, s, s.summed)
                    dv.wait_ge(s.rows_in[u], (i + 1) * 16 * BATCH)
                    after(dv, s.summed, b - 1)
                    dv.tensor_tensor(t.weighted[:, u % 2, :, 0:C].rearrange("p m (h d) -> p m h d", h=H),
                                     t.rows[:, u, :, :].rearrange("p m (h d) -> p m h d", h=H),
                                     spread(k.odds[:, bass.ds(b * BATCH, BATCH), 0:H], 3, C // H), ALU.mult).then_inc(s.weighted_ready, 1)
                    if real(b, 1):
                        edge_add(dv, b - 1, u + 3, k, t, s, W)
                edge_loop(dv, slot)
                edge_add(dv, NB - 1, DEEP - 1, k, t, s, W)


def between_second(nc, k, a):
    ZW = C + 2
    with ExitStack() as ctx:
        sb, ps, sem = scope(nc, ctx, "between")
        w = sb("w", [P, KC, ZW])
        natural = sb("natural", [P, KC, C])
        vectors = sb("vectors", [P, KC, 2])
        den = sb("den", [P, GT, H1])
        mean = sb("mean", [P, GT, C])
        below = sb("below", [P, GT, C])
        grown = sb("grown", [P, GT, C])
        hidden = sb("hidden", [P, GT, C])
        hT = sb("hT", [P, 2, KC, P])
        outs = sb("outs", [P, 2, ZW])
        pT = [ps(f"pT{i}", [P, KC, P]) for i in range(2)]
        pM = [ps(f"pM{i}", [P, ZW]) for i in range(2)]
        loaded, folded, fold_kept, small = sem("loaded"), sem("folded"), sem("fold_kept"), sem("small")
        mean_ready, below_ready, grown_ready, above_ready = sem("mean_ready"), sem("below_ready"), sem("grown_ready"), sem("above_ready")
        hidden_ready, turned, kept, projected, z_ready = sem("hidden_ready"), sem("turned"), sem("kept"), sem("projected"), sem("z_ready")
        stored = [sem("stored0"), sem("stored1")]

        with nc.Block() as block:
            @block.sync
            def _(sp):
                for n in range(KC):
                    rows = slice(n * P, (n + 1) * P)
                    sp.dma_start(w[:, n, 0:C], a["w_z2"][rows, :]).then_inc(loaded, 16)
                    sp.dma_start(natural[:, n, :], a["w_natural2"][rows, :]).then_inc(loaded, 16)
                    sp.dma_start(vectors[:, n, :], a["vectors2"][rows, :], allow_slow_non_contiguous=True).then_inc(loaded, 16)

                def group(g):
                    for j in range(GT):
                        n, u = g * GT + j, j % 2
                        sp.wait_ge(z_ready, n + 1)
                        rows = bass.ds(n * P, P)
                        sp.dma_start(k.z_table[rows, :], outs[:, u, 0:C]).then_inc(stored[u], 16)
                        sp.dma_start(k.es_table2[rows, :], outs[:, u, C:C + 1]).then_inc(stored[u], 16)
                loop(sp, NG, group)
                for u in range(2):
                    sp.wait_ge(stored[u], 32 * USES[u] * NG)

            @block.vector
            def _(dv):
                dv.wait_ge(folded, 1)
                dv.tensor_copy(w[:, :, C:ZW], pT[0][:, :, 0:2]).then_inc(fold_kept, 1)

                def group(g):
                    sums = k.sums[:, bass.ds(g * GT, GT), :]
                    dv.tensor_scalar(den[:, :, :], sums[:, :, C:C + H1], 1e-30, None, ALU.max).then_inc(small, 1)
                    dv.wait_ge(small, 2 * g + 1)
                    dv.reciprocal(den[:, :, :], den[:, :, :]).then_inc(small, 1)
                    dv.wait_ge(small, 2 * g + 2)
                    dv.tensor_tensor(mean[:, :, :].rearrange("p t (h d) -> p t h d", h=H1),
                                     sums[:, :, 0:C].rearrange("p t (h d) -> p t h d", h=H1),
                                     spread(den[:, :, :], 3, D1), ALU.mult).then_inc(mean_ready, 1)
                    dv.wait_ge(mean_ready, g + 1)
                    dv.tensor_scalar(below[:, :, :], mean[:, :, :], 0.0, None, ALU.min).then_inc(below_ready, 1)
                    dv.tensor_scalar(mean[:, :, :], mean[:, :, :], 0.0, None, ALU.max).then_inc(above_ready, 1)
                    dv.wait_ge(above_ready, g + 1)
                    dv.wait_ge(grown_ready, g + 1)
                    after(dv, turned, GT * g)
                    dv.scalar_tensor_tensor(out=hidden[:, :, :], in0=grown[:, :, :], scalar=-1.0, in1=mean[:, :, :],
                                            op0=ALU.add, op1=ALU.add).then_inc(hidden_ready, 1)
                    for j in range(GT):
                        n, u = g * GT + j, j % 2
                        dv.wait_ge(projected, n + 1)
                        after(dv, stored[u], 32 * uses(g, j))
                        dv.tensor_copy(k.ed[:, bass.ds(n, 1), 0:1], pM[u][:, C + 1:ZW].unsqueeze(1))
                        dv.tensor_copy(outs[:, u, :], pM[u][:, :]).then_inc(z_ready, 1)
                loop(dv, NG, group)

            @block.scalar
            def _(ac):
                ac.wait_ge(fold_kept, 1)

                def group(g):
                    ac.wait_ge(below_ready, g + 1)
                    after(ac, hidden_ready, g)
                    ac.activation(grown[:, :, :], below[:, :, :], ACT.Exp).then_inc(grown_ready, 1)
                    for j in range(GT):
                        n, u = g * GT + j, j % 2
                        ac.wait_ge(turned, n + 1)
                        after(ac, projected, n - BEHIND[j] + 1)
                        ac.copy(hT[:, u, :, :], pT[u][:, :, :]).then_inc(kept, 1)
                loop(ac, NG, group)

            @block.tensor
            def _(pe):
                pe.wait_ge(loaded, 96)
                for m in range(KC):
                    for c in range(KC):
                        ins = pe.matmul(pT[0][:, m, 0:2], natural[:, c, m * P:(m + 1) * P], vectors[:, c, :],
                                        start=c == 0, stop=c == KC - 1)
                ins.then_inc(folded, 1)
                pe.wait_ge(fold_kept, 1)

                def group(g):
                    pe.wait_ge(hidden_ready, g + 1)
                    for j in range(GT):
                        n, u = g * GT + j, j % 2
                        after(pe, kept, n - BEHIND[j] + 1)
                        for c in range(KC):
                            ins = pe.transpose(pT[u][:, c, :], hidden[:, j, c * P:(c + 1) * P], k.ident[:, :])
                        ins.then_inc(turned, 1)
                        pe.wait_ge(kept, n + 1)
                        after(pe, z_ready, n - BEHIND[j] + 1)
                        for c in range(KC):
                            ins = pe.matmul(pM[u][:, :], hT[:, u, c, :], w[:, c, :], start=c == 0, stop=c == KC - 1)
                        ins.then_inc(projected, 1)
                loop(pe, NG, group)


def end_second(nc, k):
    with ExitStack() as ctx:
        sb, ps, sem = scope(nc, ctx, "end_second")
        den = sb("den", [P, NT, 1])
        step = sem("step")
        with nc.Block() as block:
            @block.vector
            def _(dv):
                chain = Chain(dv, step, 4)
                chain.turn(0)
                chain(dv.tensor_scalar(den[:, :, :], k.sums[:, :, C:C + 1], 1e-30, None, ALU.max))
                chain(dv.reciprocal(den[:, :, :], den[:, :, :]))
                chain(dv.tensor_tensor(k.sums[:, :, 0:C], k.sums[:, :, 0:C], spread(den[:, :, 0], 2, C), ALU.mult))
                chain(dv.tensor_tensor(k.x[:, :, :], k.x[:, :, :], k.sums[:, :, 0:C], ALU.add))


def store(nc, k, out):
    with ExitStack() as ctx:
        sb, ps, sem = scope(nc, ctx, "store")
        done = sem("done")
        with nc.Block() as block:
            @block.sync
            def _(sp):
                sp.dma_start(out[0:FULL * P, :].rearrange("(t p) c -> p t c", p=P), k.x[:, 0:FULL, :]).then_inc(done, 16)
                sp.dma_start(out[FULL * P:NODES, :], k.x[0:LAST, FULL, :]).then_inc(done, 16)
                sp.wait_ge(done, 32)


def program(nc, a, out):
    k = Core()
    with ExitStack() as ctx:
        sb, ps, sem = scope(nc, ctx, "kept")
        k.x = sb("x", [P, NT, C])
        k.ident = sb("ident", [P, P])
        k.lane = sb("lane", [P, P])
        k.ones = sb("ones", [P, P])
        k.power = sb("power", [P, 64])
        k.share = sb("share", [P, NT])
        k.src_pad = nc.dram_tensor("src_pad", (EROWS, EW), I32).ap()
        k.dst_pad = nc.dram_tensor("dst_pad", (EROWS, EW), I32).ap()
        k.win_dram = nc.dram_tensor("win_dram", (BLK, PB), I32).ap()
        k.kv_table = nc.dram_tensor("kv_table", (ROWS, 2 * C), F32).ap()
        k.mix_qkv = nc.dram_tensor("mix_qkv", (ROWS, 3 * C), F32).ap()
        k.z_table = nc.dram_tensor("z_table", (ROWS, C), F32).ap()
        k.es_table1 = nc.dram_tensor("es_table1", (ROWS, H1), F32).ap()
        k.es_table2 = nc.dram_tensor("es_table2", (ROWS, 1), F32).ap()
        k.scores1, k.most1 = [nc.dram_tensor(name, (EROWS, EW * H1), F32).ap() for name in ("scores1", "most1")]
        k.scores2, k.most2 = [nc.dram_tensor(name, (EROWS, EW), F32).ap() for name in ("scores2", "most2")]
        with ExitStack() as edges:
            sb, ps, sem = scope(nc, edges, "edges")
            k.xn = sb("xn", [P, NT, C])
            k.sums = sb("sums", [P, NT, SW])
            k.src = sb("src", [P, NPX * SUB], I32)
            k.rel = sb("rel", [P, NPX * SUB])
            k.win = sb("win", [1, NPX], I32)
            k.tile_i = sb("tile_i", [PB, BLK], I32)
            prepare(nc, k, a)
            with ExitStack() as first:
                sb, ps, sem = scope(nc, first, "first")
                k.node = sb("node", [P, NT, C])
                project_first(nc, k, a)
                attend_first(nc, k)
            with ExitStack() as mixing:
                sb, ps, sem = scope(nc, mixing, "mixing")
                k.mixed = sb("mixed", [P, FCH, SW])
                mix_keys(nc, k, a)
                mix_queries(nc, k, a)
            layer_first(nc, k, a)
            experts(nc, k, a, False)
            sb, ps, sem = scope(nc, edges, "second")
            k.ed = sb("ed", [P, NT, H1])
            k.odds = sb("odds", [P, NP * SUB, H1])
            with ExitStack() as mixing:
                sb, ps, sem = scope(nc, mixing, "mixing_again")
                k.dots = sb("dots", [P, HM * DM // P, P])
                project_second(nc, k, a)
                mix_second(nc, k, a)
            edge_odds(nc, k, a, H1, k.es_table1, k.ed, k.scores1, k.most1)
            edge_sums(nc, k, H1, k.z_table)
            between_second(nc, k, a)
            edge_odds(nc, k, a, 1, k.es_table2, k.ed, k.scores2, k.most2)
            edge_sums(nc, k, 1, k.z_table)
            end_second(nc, k)
        experts(nc, k, a, True)
        store(nc, k, out)


def layout(v):
    c = np.ascontiguousarray

    def r(b):
        return c(np.reshape(b, (1, -1)))

    def columns(b):
        return c(np.reshape(b, (-1, P)).T)

    def by_expert(b):
        return c(np.reshape(b, (NE, -1, P)).transpose(2, 1, 0).reshape(P, -1))

    mix_w = v["L0_mix_Wqkv"].T
    mix_b = v["L0_mix_bqkv"]
    a1, a2 = v["L1_gnn_a1"], v["L1_gnn_a2"]
    vectors1 = np.zeros((C, 2 * H1), np.float32)
    for h in range(H1):
        vectors1[h * D1:(h + 1) * D1, h] = a1[h, :D1]
        vectors1[h * D1:(h + 1) * D1, H1 + h] = a1[h, D1:]
    w_z = np.reshape(v["L1_gnn_W1"], (C, C))
    w_qkv = v["L1_mix_w_qkv"]
    return {
        "x": c(v["x"]), "src": c(v["src"]), "dst": c(v["dst"]),
        "w_z1": c(w_z.T), "w_natural1": c(w_z), "vectors1": vectors1,
        "w_z2": c(v["L1_gnn_W2"].T), "w_natural2": c(v["L1_gnn_W2"]), "vectors2": c(np.stack([a2[:C], a2[C:]], axis=1)),
        "w_mixkv": c(w_qkv[:, HM * DM:]), "w_mixq": c(w_qkv[:, :HM * DM].T), "w_mixout": c(v["L1_mix_w_out"]),
        "b_mixout": r(v["L1_mix_b_out"]),
        "w_first": c(np.concatenate([v["L0_gnn_Wk"].T, v["L0_gnn_Wv"].T, v["L0_gnn_Wq"].T, mix_w[:, C:2 * C],
                                     mix_w[:, 2 * C:], mix_w[:, :C]], axis=1)),
        "b_first": r(np.concatenate([v["L0_gnn_bk"], v["L0_gnn_bv"], v["L0_gnn_bq"], mix_b[C:2 * C], mix_b[2 * C:],
                                     mix_b[:C]])),
        "w_mixproj": c(v["L0_mix_Wproj"].T), "b_mixproj": r(v["L0_mix_bproj"]), "temperature": r(v["L0_mix_temperature"]),
        "w_p": c(v["L0_gnn_Wp"].T), "b_p": r(v["L0_gnn_bp"]), "w_1": c(v["L0_gnn_W1"].T), "w_2": c(v["L0_gnn_W2"].T),
        "b_1": columns(v["L0_gnn_b1"]), "b_2": r(v["L0_gnn_b2"]), "ln_g": columns(v["L0_gnn_ln_g"]),
        "ln_b": columns(v["L0_gnn_ln_b"]),
        "w_r1": c(v["L0_ffn_Wr"]), "b_r1": r(v["L0_ffn_br"]), "b_o1": c(v["L0_ffn_bo"]), "w_hidden1": c(v["L0_ffn_W1"]),
        "w_deep": c(v["L0_ffn_W2"]), "w_out1": c(v["L0_ffn_Wo"]),
        "bn": c(np.stack([np.stack([by_expert(v["L0_ffn_" + name + str(n)]) for name in ("g", "be", "m", "v", "b")], axis=1)
                          for n in (1, 2)], axis=1)),
        "w_r2": c(v["L1_ffn_Wr"]), "b_r2": r(v["L1_ffn_br"]), "b_o2": c(v["L1_ffn_b2"]), "w_hidden2": c(v["L1_ffn_W1"]),
        "w_out2": c(v["L1_ffn_W2"]), "b_hidden": by_expert(v["L1_ffn_b1"]), "gamma": columns(v["L1_ffn_gamma"]),
        "beta": columns(v["L1_ffn_beta"]),
    }


def kernel(**inputs):
    import concourse.bacc as bacc
    from concourse.bass_utils import run_bass_kernel_spmd

    arrays = layout({name: np.asarray(value) for name, value in inputs.items()})
    nc = bacc.Bacc("TRN2", target_bir_lowering=False, num_devices=1)
    parts = {name: nc.dram_tensor(f"in_{name}_dram", a.shape, mybir.dt.from_np(a.dtype), kind="ExternalInput").ap()
             for name, a in arrays.items()}
    out = nc.dram_tensor("out_0_dram", (NODES, C), F32, kind="ExternalOutput").ap()
    program(nc, parts, out)
    ran = run_bass_kernel_spmd(nc, [{f"in_{name}_dram": a for name, a in arrays.items()}], core_ids=[0])
    return ran.results[0]["out_0_dram"]
```

```python
from contextlib import ExitStack

import numpy as np

import concourse.bass as bass
from concourse import mybir

F32 = mybir.dt.float32
BF16 = mybir.dt.bfloat16
I32 = mybir.dt.int32
ALU = mybir.AluOpType
ACT = mybir.ActivationFunctionType
AX = mybir.AxisListType.X

P = 128
NODES = 3125
C = 256
KC = C // P
NT = -(-NODES // P)
ROWS = NT * P
FULL = NODES // P
LAST = NODES - FULL * P
GT = 5
NG = NT // GT
GN = GT * P
EDGES = 50000
SUB = 2
EW = SUB * P
ET = -(-EDGES // EW)
EROWS = ET + 1
BP = 2
BATCH = BP * SUB
DEEP = 4
NB = -(-(ET + NT - 1) // (BP * 2 * DEEP)) * 2 * DEEP
NP = NB * BP
BLK = 2
PB = NP // BLK
NPX = NP + 2 * BP
FAR = 8191
H0, D0 = 8, C // 8
H1, D1 = 4, C // 4
HM, DM = 8, 64
SW = C + H0
BIG = 2.0 ** 100
NE = 8


def after(eng, sem, value):
    if not isinstance(value, int) or value > 0:
        eng.wait_ge(sem, value)


def loop(eng, count, body):
    body(0)
    if count > 1:
        with eng.Fori(1, count) as i:
            body(i)


BEHIND = [1, 3, 2, 2, 2]
USES = [3, 2]


BUF3 = [0, 1, 0, 1, 2]
BEHIND3 = [3, 3, 2, 2, 5]


def uses(g, j):
    return g * USES[j % 2] + j // 2


def real(b, back):
    return not isinstance(b, int) or b >= back


def spread(ap, axis, n):
    shape = list(ap.shape)
    shape.insert(axis, n)
    return ap.unsqueeze(axis).broadcast_to(shape)


class Core:
    pass


def scope(nc, ctx, stage):
    def sb(name, shape, dt=F32):
        return ctx.enter_context(nc.sbuf_tensor(f"{stage}_{name}", shape, dt))

    def ps(name, shape, dt=F32):
        size = int(np.prod(shape[1:]))
        banks = -(-size // 512)
        whole = ctx.enter_context(nc.psum_tensor(f"{stage}_{name}", [P, banks * 512], dt))
        if len(shape) == 2:
            return whole[0:shape[0], 0:size]
        if len(shape) == 3:
            return whole[0:shape[0], 0:size].rearrange("p (a b) -> p a b", a=shape[1])
        return whole[0:shape[0], 0:size].rearrange("p (a b c) -> p a b c", a=shape[1], b=shape[2])

    sems = []

    def clear():
        if sems:
            nc.clear_and_free_semaphores(sems)
            nc.all_engine_barrier()
    ctx.callback(clear)

    def sem(name):
        sems.append(nc.alloc_semaphore(f"{stage}_{name}"))
        return sems[-1]

    return sb, ps, sem


def prepare(nc, k, a):
    with ExitStack() as ctx:
        sb, ps, sem = scope(nc, ctx, "prepare")
        tail = sb("tail", [1, 2, EROWS * EW - EDGES], I32)
        first = sb("first", [1, EROWS], I32)
        firstw = sb("firstw", [1, EROWS], I32)
        start = sb("start", [1, EROWS])
        rowno = sb("rowno", [1, EROWS])
        ones_row = sb("ones_row", [1, P])
        pairno = sb("pairno", [PB, BLK])
        hits = sb("hits", [PB, BLK, EROWS])
        count = sb("count", [PB, BLK])
        win_f = sb("win_f", [PB, BLK])
        win_o = sb("win_o", [PB, BLK])
        win_c = sb("win_c", [PB, BLK])
        win_i = sb("win_i", [PB, BLK], I32)
        srow = sb("srow", [PB, BLK, EW], I32)
        drow = sb("drow", [PB, BLK, EW], I32)
        sf = sb("sf", [PB, BLK, EW])
        df = sb("df", [PB, BLK, EW])
        dr = sb("dr", [PB, BLK, EW])
        pstart = ps("pstart", [P, EROWS])
        pT = ps("pT", [P, 2, 512])
        tails_set, padded, edges_in, x_in = sem("tails_set"), sem("padded"), sem("edges_in"), sem("x_in")
        firsts_in, zeroed, idf_set, consts = sem("firsts_in"), sem("zeroed"), sem("idf_set"), sem("consts")
        dve, bcast, tiles_ready = sem("dve"), sem("bcast"), sem("tiles_ready")
        rows_in, wins_out, wins_in, turned = sem("rows_in"), sem("wins_out"), sem("wins_in"), sem("turned")
        rel_ready, share_set = sem("rel_ready"), sem("share_set")

        with nc.Block() as block:
            @block.sync
            def _(sp):
                for name, pad in (("src", k.src_pad), ("dst", k.dst_pad)):
                    flat = pad.rearrange("a b -> (a b)")
                    sp.dma_start(flat[0:EDGES].rearrange("(a b) -> a b", a=80),
                                 a[name].rearrange("(a b) -> a b", a=80)).then_inc(edges_in, 16)
                sp.wait_ge(tails_set, 2)
                for n, pad in enumerate((k.src_pad, k.dst_pad)):
                    flat = pad.rearrange("(o a) b -> o (a b)", o=1)
                    sp.dma_start(flat[:, EDGES:EROWS * EW], tail[:, n, :]).then_inc(edges_in, 16)
                sp.wait_ge(zeroed, 1)
                sp.dma_start(k.x[:, 0:FULL, :], a["x"][0:FULL * P, :].rearrange("(t p) c -> p t c", p=P)).then_inc(x_in, 16)
                sp.dma_start(k.x[0:LAST, FULL, :], a["x"][FULL * P:NODES, :]).then_inc(x_in, 16)
                sp.wait_ge(edges_in, 64)
                sp.dma_start(first[:, :], k.dst_pad[:, 0:1].rearrange("a b -> b a"),
                             allow_slow_non_contiguous=True).then_inc(firsts_in, 16)
                sp.wait_ge(dve, 8)
                sp.dma_start(k.win_dram.rearrange("b p -> p b"), win_i[:, :],
                             allow_slow_non_contiguous=True).then_inc(wins_out, 16)
                sp.wait_ge(wins_out, 16)
                sp.dma_start(k.win[:, 0:NP], k.win_dram.rearrange("(o b) p -> o (b p)", o=1)).then_inc(wins_in, 16)
                sp.wait_ge(wins_in, 16)
                sp.wait_ge(x_in, 32)

            @block.gpsimd
            def _(pool):
                pool.memset(k.x[:, FULL, :], 0.0).then_inc(zeroed, 1)
                pool.memset(k.share[:, :], 1.0 / NODES).then_inc(share_set, 1)
                pool.wait_ge(share_set, 1)
                pool.affine_select(out=k.share[:, :], in_=k.share[:, :], compare_op=ALU.is_gt, fill=0.0, base=NODES,
                                   pattern=[[-P, NT]], channel_multiplier=-1).then_inc(share_set, 1)
                pool.memset(k.ident[:, :], 0.0).then_inc(idf_set, 1)
                pool.wait_ge(idf_set, 1)
                pool.affine_select(out=k.ident[:, :], in_=k.ident[:, :], compare_op=ALU.not_equal, fill=1.0, base=0,
                                   pattern=[[-1, P]], channel_multiplier=1).then_inc(idf_set, 1)
                pool.iota(k.lane[:, :], [[1, P]], base=0, channel_multiplier=0,
                          allow_small_or_imprecise_dtypes=True).then_inc(consts, 1)
                pool.iota(rowno[:, :], [[1, EROWS]], base=0, channel_multiplier=0,
                          allow_small_or_imprecise_dtypes=True).then_inc(consts, 1)
                pool.iota(pairno[:, :], [[PB, BLK]], base=0, channel_multiplier=1,
                          allow_small_or_imprecise_dtypes=True).then_inc(consts, 1)
                pool.memset(ones_row[:, :], 1.0).then_inc(consts, 1)
                pool.memset(k.power[:, :], -0.5).then_inc(consts, 1)
                pool.memset(k.win[:, NP:NPX], 0).then_inc(consts, 1)
                pool.memset(k.rel[:, NP * SUB:NPX * SUB], -1.0).then_inc(consts, 1)
                pool.wait_ge(tiles_ready, 1)
                for b in range(BLK):
                    for table, rows in ((k.src_pad, srow), (k.dst_pad, drow)):
                        pool.indirect_dma_start(rows[:, b, :], None, table,
                                                bass.IndirectOffsetOnAxis(ap=k.tile_i[:, b:b + 1], axis=0)).then_inc(rows_in, 16)

            @block.vector
            def _(dv):
                dv.memset(tail[:, 0, :], 0).then_inc(tails_set, 1)
                dv.memset(tail[:, 1, :], FAR).then_inc(tails_set, 1)
                dv.memset(k.ones[:, :], 1.0).then_inc(dve, 1)
                dv.wait_ge(firsts_in, 16)
                dv.tensor_scalar(firstw[:, :], first[:, :], 7, None, ALU.arith_shift_right).then_inc(dve, 1)
                dv.wait_ge(consts, 7)
                dv.wait_ge(dve, 2)
                dv.tensor_tensor(start[:, :], firstw[:, :], rowno[:, :], ALU.add).then_inc(dve, 1)
                dv.wait_ge(dve, 3)
                dv.memset(start[:, 0:1], 0.0).then_inc(dve, 1)
                dv.wait_ge(bcast, 1)
                for b in range(BLK):
                    ins = dv.tensor_scalar(hits[:, b, :], pstart[0:PB, :], pairno[:, b:b + 1], None, ALU.is_le, ALU.add,
                                           accum_out=count[:, b:b + 1])
                ins.then_inc(dve, 1)
                dv.wait_ge(dve, 5)
                dv.tensor_scalar(k.tile_i[:, :], count[:, :], -1.0, None, ALU.add).then_inc(tiles_ready, 1)
                dv.tensor_tensor(win_f[:, :], pairno[:, :], count[:, :], ALU.subtract).then_inc(dve, 1)
                dv.wait_ge(dve, 6)
                dv.tensor_scalar(win_o[:, :], win_f[:, :], 1.0, float(P), ALU.add, ALU.mult).then_inc(dve, 1)
                dv.tensor_scalar(win_i[:, :], win_f[:, :], 1.0, float(NT - 1), ALU.add, ALU.min).then_inc(dve, 1)
                dv.wait_ge(dve, 8)
                dv.wait_ge(rows_in, 32 * BLK)
                dv.tensor_tensor(dr[:, :, :], drow[:, :, :], spread(win_o[:, :], 2, EW), ALU.subtract).then_inc(rel_ready, 1)
                dv.tensor_copy(sf[:, :, :], srow[:, :, :]).then_inc(rel_ready, 1)
                dv.wait_ge(turned, 2 * BLK * SUB)
                for b in range(BLK):
                    for n, to in enumerate((k.rel, k.src)):
                        pairs = to[:, b * PB * SUB:(b + 1) * PB * SUB].rearrange("p (i s) -> p s i", s=SUB)
                        dv.tensor_copy(pairs, pT[:, n, b * EW:(b + 1) * EW].rearrange("p (s i) -> p s i", s=SUB)[:, :, 0:PB]).then_inc(dve, 1)

            @block.tensor
            def _(pe):
                pe.wait_ge(dve, 4)
                pe.wait_ge(consts, 7)
                pe.matmul(pstart[:, :], ones_row[:, :], start[:, :], start=True, stop=True).then_inc(bcast, 1)
                pe.wait_ge(idf_set, 2)
                pe.wait_ge(rel_ready, 2)
                for n, rows in enumerate((dr, sf)):
                    for b in range(BLK):
                        for m in range(SUB):
                            pe.transpose(pT[:, n, b * EW + m * P:b * EW + m * P + PB], rows[:, b, m * P:(m + 1) * P],
                                         k.ident[0:PB, 0:PB]).then_inc(turned, 1)


def normalise(dv, g, source, s, t):
    for j in range(GT):
        dv.bn_stats(t.stats[:, j, :], source(g, j)).then_inc(s.stats_ready, 1)
    dv.wait_ge(s.stats_ready, g * GT + GT)
    dv.sem_inc(s.stats_fence, 1)
    for j in range(GT):
        dv.bn_aggr(t.moments[:, j, :], t.stats[:, j, :]).then_inc(s.moments_ready, 1)
    dv.wait_ge(s.moments_ready, g * GT + GT)
    dv.tensor_scalar(t.vareps[:, :], t.moments[:, :, 1], 1e-5, None, ALU.add).then_inc(s.vareps_ready, 1)
    dv.wait_ge(s.rstd_ready, g + 1)
    for j in range(GT):
        dv.tensor_scalar(t.normed[:, j, :], source(g, j), t.moments[:, j, 0:1], t.rstd[:, j:j + 1],
                         ALU.subtract, ALU.mult).then_inc(s.normed_ready, 1)


def deviations(pool, g, k, s, t):
    pool.wait_ge(s.vareps_ready, g + 1)
    pool.tensor_tensor(t.rstd[:, :], t.vareps[:, :], k.power[:, 0:GT], ALU.pow).then_inc(s.rstd_ready, 1)


class Chain:

    def __init__(self, eng, sem, per):
        self.eng, self.sem, self.per = eng, sem, per

    def turn(self, i):
        self.count = i * self.per
        self.left = self.per

    def __call__(self, instruction):
        self.left -= 1
        instruction.then_inc(self.sem, 1)
        self.eng.wait_ge(self.sem, self.count + self.per - self.left)


def norm_tensors(sb, sem, tag=""):
    t, s = Core(), Core()
    t.stats = sb(f"stats{tag}", [P, GT, 6])
    t.moments = sb(f"moments{tag}", [P, GT, 2])
    t.vareps = sb(f"vareps{tag}", [P, GT])
    t.rstd = sb(f"rstd{tag}", [P, GT])
    t.normed = sb(f"normed{tag}", [P, GT, C])
    s.stats_ready = sem("stats_ready" + tag)
    s.stats_fence = sem("stats_fence" + tag)
    s.moments_ready = sem("moments_ready" + tag)
    s.vareps_ready = sem("vareps_ready" + tag)
    s.rstd_ready = sem("rstd_ready" + tag)
    s.normed_ready = sem("normed_ready" + tag)
    return t, s


def project_first(nc, k, a):
    with ExitStack() as ctx:
        sb, ps, sem = scope(nc, ctx, "project_first")
        t, s = norm_tensors(sb, sem)
        W = 1536
        CH = W // 512
        w = sb("w", [P, KC, W])
        bias = sb("bias", [P, W])
        xT = sb("xT", [P, GT, KC, P])
        outs = sb("outs", [P, 2, W])
        pT = [ps(f"pT{i}", [P, 512]) for i in range(2)]
        pM = [[ps(f"pM{i}{c}", [P, 512]) for c in range(CH)] for i in range(2)]
        loaded, kept, xT_psum, xT_ready = sem("loaded"), sem("kept"), sem("xT_psum"), sem("xT_ready")
        projected, outs_ready, xn_kept = sem("projected"), sem("outs_ready"), sem("xn_kept")
        stored = [sem("stored0"), sem("stored1")]
        sums_clear = sem("sums_clear")

        with nc.Block() as block:
            @block.sync
            def _(sp):
                for n in range(KC):
                    sp.dma_start(w[:, n, :], a["w_first"][n * P:(n + 1) * P, :]).then_inc(loaded, 16)
                sp.dma_start(bias[:, :], a["b_first"].partition_broadcast(P)).then_inc(loaded, 16)

                def group(g):
                    for j in range(GT):
                        n, u = g * GT + j, j % 2
                        sp.wait_ge(outs_ready, CH * n + CH)
                        sp.dma_start(k.kv_table[bass.ds(n * P, P), :], outs[:, u, 0:512]).then_inc(stored[u], 16)
                        sp.dma_start(k.mix_qkv[bass.ds(n * P, P), :], outs[:, u, 768:1536]).then_inc(stored[u], 16)
                loop(sp, NG, group)
                for u in range(2):
                    sp.wait_ge(stored[u], 32 * USES[u] * NG)

            @block.gpsimd
            def _(pool):
                pool.memset(k.sums[:, :, :], 0.0).then_inc(sums_clear, 1)
                loop(pool, NG, lambda g: deviations(pool, g, k, s, t))

            @block.vector
            def _(dv):
                dv.wait_ge(loaded, 48)

                def norm(g):
                    after(dv, xT_psum, GT * g)
                    after(dv, xn_kept, g)
                    normalise(dv, g, lambda g, j: k.x[:, bass.ds(g * GT + j, 1), :], s, t)

                def group(g, last=False):
                    for j in range(GT):
                        n, u = g * GT + j, j % 2
                        after(dv, stored[u], 32 * uses(g, j))
                        after(dv, kept, n - BEHIND[j] + 1)
                        for c in range(CH):
                            dv.wait_ge(projected, CH * n + c + 1)
                            dv.tensor_tensor(outs[:, u, c * 512:(c + 1) * 512], pM[u][c][:, :],
                                             bias[:, c * 512:(c + 1) * 512], ALU.add).then_inc(outs_ready, 1)
                        if j == 1 and not last:
                            norm(g + 1)
                norm(0)
                loop(dv, NG - 1, group)
                group(NG - 1, True)

            @block.scalar
            def _(ac):
                def group(g):
                    for j in range(GT):
                        n, u = g * GT + j, j % 2
                        ac.wait_ge(xT_psum, n + 1)
                        after(ac, projected, CH * (n - GT + 1))
                        ac.copy(xT[:, j, :, :], pT[u][:, 0:C].rearrange("p (k n) -> p k n", k=KC)).then_inc(xT_ready, 1)
                    ac.copy(k.xn[:, bass.ds(g * GT, GT), :], t.normed[:, :, :]).then_inc(xn_kept, 1)
                    for j in range(GT):
                        n, u = g * GT + j, j % 2
                        ac.wait_ge(outs_ready, CH * n + 2)
                        ac.copy(k.node[:, bass.ds(n, 1), :], outs[:, u:u + 1, 512:768]).then_inc(kept, 1)
                loop(ac, NG, group)

            @block.tensor
            def _(pe):
                pe.wait_ge(loaded, 48)

                def group(g):
                    for j in range(GT):
                        n, u = g * GT + j, j % 2
                        pe.wait_ge(s.normed_ready, n + 1)
                        after(pe, xT_ready, n - BEHIND[j] + 1)
                        for c in range(KC):
                            ins = pe.transpose(pT[u][:, c * P:(c + 1) * P], t.normed[:, j, c * P:(c + 1) * P], k.ident[:, :])
                        ins.then_inc(xT_psum, 1)
                    for j in range(GT):
                        n, u = g * GT + j, j % 2
                        pe.wait_ge(xT_ready, n + 1)
                        after(pe, outs_ready, CH * (n - BEHIND[j] + 1))
                        for c in range(CH):
                            for q in range(KC):
                                ins = pe.matmul(pM[u][c][:, :], xT[:, j, q, :], w[:, q, c * 512:(c + 1) * 512],
                                                start=q == 0, stop=q == KC - 1)
                            ins.then_inc(projected, 1)
                loop(pe, NG, group)


def edge_gather(pool, k, t, s, table, rows_free):
    def steps(i):
        for half in range(2):
            first = (2 * i + half) * DEEP
            for u in range(DEEP):
                b = first + u
                after(pool, rows_free, b - DEEP + 1)
                if u == 0:
                    pool.sem_inc(s.fence, 1)
                    pool.tensor_copy(t.index[:, half, :], k.src[:, bass.ds(b * BATCH, DEEP * BATCH)]).then_inc(s.index_ready, 1)
                    pool.wait_ge(s.index_ready, 2 * i + half + 1)
                pool.sem_inc(s.fence, 1)
                for m in range(BATCH):
                    at = u * BATCH + m
                    pool.indirect_dma_start(t.rows[:, u, m, :], None, table,
                                            bass.IndirectOffsetOnAxis(ap=t.index[:, half, at:at + 1], axis=0)).then_inc(s.rows_in[u], 16)
    loop(pool, NB // (2 * DEEP), steps)
    for u in range(DEEP):
        pool.wait_ge(s.rows_in[u], 16 * BATCH * NB // DEEP)


def edge_hot(dv, b, u, k, t, s, free):
    after(dv, free, b - DEEP + 1)
    for m in range(BATCH):
        ins = dv.tensor_scalar(t.hot[:, u % DEEP, m, :], k.lane[:, :], k.rel[:, bass.ds(b * BATCH + m, 1)], None, ALU.is_equal)
    ins.then_inc(s.hot_ready, 1)


def edge_turn(pe, b, u, ident, t, s):
    pe.wait_ge(s.hot_ready, b + 1)
    after(pe, s.hotT_ready, b)
    for m in range(BATCH):
        ins = pe.transpose(t.p_hotT[:, m, :], t.hot[:, u % DEEP, m, :], ident[:, :])
    ins.then_inc(s.hotT_psum, 1)


def edge_keep(ac, b, u, t, s):
    ac.wait_ge(s.hotT_psum, b + 1)
    after(ac, s.looked_up, b - 1)
    ac.copy(t.hotT[:, u % 2, :, :], t.p_hotT[:, :, :]).then_inc(s.hotT_ready, 1)


def windows_of(eng, k, b, count=1):
    _, windows = k.nc.values_load_multi_w_load_instructions(k.win[0:1, bass.ds(b * BP, count * BP)], engines=[eng.engine],
                                                            min_val=0, max_val=NT - 1)
    return windows


def edge_look(pe, b, u, windows, t, s, node, into, look_free):
    pe.wait_ge(s.hotT_ready, b + 1)
    after(pe, look_free, b)
    for m in range(BATCH):
        ins = pe.matmul(into[:, m, :], t.hotT[:, u % 2, m, :], node[:, bass.ds(windows[m // SUB], 1), :], start=True, stop=True)
    ins.then_inc(s.looked_up, 1)


def edge_sum(pe, b, u, t, s, width):
    pe.wait_ge(s.weighted_ready, b + 1)
    after(pe, s.added, (b - 1) * BP)
    for m in range(BP):
        for n in range(SUB):
            c = m * SUB + n
            ins = pe.matmul(t.p_sum[:, u % 2 * BP + m, 0:width], t.hot[:, u % DEEP, c, :], t.weighted[:, u % 2, c, 0:width],
                            start=n == 0, stop=n == SUB - 1)
    ins.then_inc(s.summed, 1)


def edge_add(dv, b, u, windows, k, t, s, width):
    dv.wait_ge(s.summed, b + 1)
    for m in range(BP):
        into = k.sums[:, bass.ds(windows[m], 1), 0:width]
        after(dv, s.added, b * BP + m)
        c = u % 2 * BP + m
        dv.tensor_tensor(into, into, t.p_sum[:, c:c + 1, 0:width], ALU.add).then_inc(s.added, 1)


def edge_loop(eng, slot, k=None, ahead=0):
    def steps(i):
        first = i * DEEP + ahead
        missing = -first if isinstance(first, int) and first < 0 else 0
        windows = [None] * BP * missing + (list(windows_of(eng, k, first + missing, DEEP - missing)) if k else [None] * BP * DEEP)
        for u in range(DEEP):
            slot(i * DEEP + u, u, i, windows[u * BP:(u + 1) * BP])
    loop(eng, NB // DEEP, steps)


def attend_first(nc, k):
    with ExitStack() as ctx:
        sb, ps, sem = scope(nc, ctx, "attend_first")
        t, s = Core(), Core()
        t.index = sb("index", [P, 2, DEEP * BATCH], I32)
        t.rows = sb("rows", [P, DEEP, BATCH, 2 * C])
        t.hot = sb("hot", [P, DEEP, BATCH, P])
        t.hotT = sb("hotT", [P, 2, BATCH, P])
        score = sb("score", [P, 2, BATCH, H0])
        clip = sb("clip", [P, 2, BATCH, H0])
        t.weighted = sb("weighted", [P, 2, BATCH, SW])
        product = sb("product", [P, BATCH, C])
        distance, distance_ready = sb("distance", [P, BATCH, P]), sem("distance_ready")
        t.p_hotT = ps("p_hotT", [P, BATCH, P])
        look = ps("p_look", [P, BATCH, C])
        t.p_sum = ps("p_sum", [P, 2 * BP, 512])
        s.fence, s.index_ready, s.hot_ready, s.hotT_psum = sem("fence"), sem("index_ready"), sem("hot_ready"), sem("hotT_psum")
        s.hotT_ready, s.looked_up, s.weighted_ready = sem("hotT_ready"), sem("looked_up"), sem("weighted_ready")
        s.summed, s.added = sem("summed"), sem("added")
        products_ready, scores_ready, clipped, exp_ready = sem("products_ready"), sem("scores_ready"), sem("clipped"), sem("exp_ready")
        s.rows_in = [sem(f"rows_in{u}") for u in range(DEEP)]
        root = D0 ** 0.5
        with nc.Block() as block:
            @block.gpsimd
            def _(pool):
                edge_gather(pool, k, t, s, k.kv_table, s.weighted_ready)

            @block.tensor
            def _(pe):
                edge_turn(pe, 0, 0, k.ident, t, s)
                edge_turn(pe, 1, 1, k.ident, t, s)
                edge_look(pe, 0, 0, windows_of(pe, k, 0), t, s, k.node, look, products_ready)

                def slot(b, u, i, windows):
                    if real(b, 2):
                        edge_sum(pe, b - 2, u + 2, t, s, SW)
                    edge_look(pe, b + 1, u + 1, windows_of(pe, k, b + 1), t, s, k.node, look, products_ready)
                    edge_turn(pe, b + 2, u + 2, k.ident, t, s)
                edge_loop(pe, slot)
                edge_sum(pe, NB - 2, 2, t, s, SW)
                edge_sum(pe, NB - 1, 3, t, s, SW)

            @block.scalar
            def _(ac):
                def hot(b, u):
                    after(ac, s.hot_ready, b)
                    for m in range(BATCH):
                        ins = ac.activation(distance[:, m, :], k.lane[:, :], ACT.Abs, bias=k.rel[:, bass.ds(b * BATCH + m, 1)], scale=-1.0)
                    ins.then_inc(distance_ready, 1)
                    ac.wait_ge(distance_ready, b + 1)
                    after(ac, s.summed, b - DEEP + 1)
                    ac.activation(t.hot[:, u % DEEP, :, :], distance[:, :, :], ACT.Relu, bias=k.ones[:, 0:1], scale=-1.0).then_inc(s.hot_ready, 1)

                hot(0, 0)
                hot(1, 1)
                edge_keep(ac, 0, 0, t, s)
                edge_keep(ac, 1, 1, t, s)

                def slot(b, u, i, windows):
                    hot(b + 2, u + 2)
                    ac.wait_ge(clipped, b + 1)
                    after(ac, s.summed, b - 1)
                    ac.activation(t.weighted[:, u % 2, :, C:SW], clip[:, u % 2, :, :], ACT.Exp, scale=1.0 / root).then_inc(exp_ready, 1)
                    edge_keep(ac, b + 2, u, t, s)
                edge_loop(ac, slot)

            @block.vector
            def _(dv):
                def weigh(b, u):
                    dv.wait_ge(exp_ready, b + 1)
                    dv.tensor_tensor(t.weighted[:, u % 2, :, 0:C].rearrange("p m (h d) -> p m h d", h=H0),
                                     t.rows[:, u % DEEP, :, C:2 * C].rearrange("p m (h d) -> p m h d", h=H0),
                                     spread(t.weighted[:, u % 2, :, C:SW], 3, D0), ALU.mult).then_inc(s.weighted_ready, 1)

                def slot(b, u, i, windows):
                    dv.wait_ge(s.looked_up, b + 1)
                    dv.wait_ge(s.rows_in[u], (i + 1) * 16 * BATCH)
                    dv.tensor_tensor(product[:, :, :], look[:, :, :], t.rows[:, u, :, 0:C], ALU.mult).then_inc(products_ready, 1)
                    dv.wait_ge(products_ready, b + 1)
                    dv.tensor_reduce(score[:, u % 2, :, :], product[:, :, :].rearrange("p m (h d) -> p m h d", h=H0),
                                     AX, ALU.add).then_inc(scores_ready, 1)
                    if real(b, 1):
                        weigh(b - 1, u + 3)
                    dv.wait_ge(scores_ready, b + 1)
                    after(dv, exp_ready, b - 1)
                    dv.tensor_scalar(clip[:, u % 2, :, :], score[:, u % 2, :, :], -10.0 * root, 10.0 * root, ALU.max,
                                     ALU.min).then_inc(clipped, 1)
                    if real(b, 2):
                        edge_add(dv, b - 2, u + 2, windows_of(dv, k, b - 2), k, t, s, SW)
                edge_loop(dv, slot)
                weigh(NB - 1, DEEP - 1)
                edge_add(dv, NB - 2, DEEP - 2, windows_of(dv, k, NB - 2), k, t, s, SW)
                edge_add(dv, NB - 1, DEEP - 1, windows_of(dv, k, NB - 1), k, t, s, SW)


SHIFTS = D0 // 2 + 1
FEAT = SHIFTS * D0 + D0 + 1
FCH = -(-FEAT // P)
FLAST = FEAT - (FCH - 1) * P
ROOT4 = float(D0) ** 0.25
VW = D0 + 1


def features(dv, double, phi, ready):
    ap = double
    steps = [list(x) for x in ap.ap]
    onward = bass.AP(tensor=ap.tensor, offset=ap.offset, ap=[steps[0], steps[1], [1, SHIFTS], [1, D0]])
    dv.tensor_tensor(phi[:, :, 0:SHIFTS * D0].rearrange("p h (s d) -> p h s d", s=SHIFTS),
                     spread(double[:, :, 0:D0], 2, SHIFTS), onward, ALU.mult).then_inc(ready, 1)


def feature_norms(dv, g, part, square, norm2, s):
    dv.tensor_tensor(square[:, :, :], part, part, ALU.mult).then_inc(s.squared, 1)
    dv.wait_ge(s.squared, g + 1)
    dv.tensor_reduce(norm2[:, :, :], square[:, :, :].rearrange("p t (h d) -> p t h d", h=H0), AX, ALU.add).then_inc(s.norm2_ready, 1)
    dv.wait_ge(s.norm2_ready, g + 1)


def feature_double(dv, g, part, factor, double, s):
    heads = double.rearrange("p t h (two d) -> p t h two d", two=2)
    for n in range(2):
        ins = dv.tensor_tensor(heads[:, :, :, n, :], part.rearrange("p t (h d) -> p t h d", h=H0), spread(factor[:, :, :], 3, D0), ALU.mult)
    ins.then_inc(s.doubled, 1)
    dv.wait_ge(s.doubled, g + 1)


def mix_keys(nc, k, a):
    with ExitStack() as ctx:
        sb, ps, sem = scope(nc, ctx, "mix_keys")
        kv = sb("kv", [P, 2, GT, C])
        square = sb("square", [P, GT, C])
        norm2 = sb("norm2", [P, GT, H0])
        factor = sb("factor", [P, GT, H0])
        double = sb("double", [P, GT, H0, 2 * D0])
        phi = sb("phi", [P, 3, H0, FEAT])
        vals = sb("vals", [P, 3, H0, VW])
        zeros = sb("zeros", [P, 512])
        sums = sb("sums", [P, H0 // 2, FEAT])
        long = [ps(f"long{n}", [P, 512]) for n in range(H0 // 2)]
        short = ps("short", [P, H0 // 2, FEAT - 512])
        turn = [ps(f"turn{u}", [P, 512]) for u in range(2)]
        s = Core()
        s.squared, s.norm2_ready, s.doubled = sem("squared"), sem("norm2_ready"), sem("doubled")
        kv_in, clamped, factor_ready = sem("kv_in"), sem("clamped"), sem("factor_ready")
        phi_ready, vals_ready, summed = sem("phi_ready"), sem("vals_ready"), sem("summed")
        zeroed, consts, kept, turned, sums_kept = sem("zeroed"), sem("consts"), sem("kept"), sem("turned"), sem("sums_kept")

        with nc.Block() as block:
            @block.sync
            def _(sp):
                def group(g):
                    after(sp, vals_ready, g * GT)
                    for n in range(2):
                        sp.dma_start(kv[:, n, :, :], k.mix_qkv[bass.ds(g * GN, GN), n * C:(n + 1) * C]
                                     .rearrange("(t p) c -> p t c", p=P)).then_inc(kv_in, 16)
                loop(sp, NG, group)

            @block.gpsimd
            def _(pool):
                for u in range(3):
                    pool.memset(phi[:, u, :, FEAT - 1:FEAT], 1.0).then_inc(consts, 1)
                pool.memset(zeros[:, :], 0.0).then_inc(zeroed, 1)

                def group(g):
                    pool.wait_ge(clamped, g + 1)
                    pool.tensor_tensor(factor[:, :, :], norm2[:, :, :], k.power[:, 0:GT * H0].rearrange("p (t h) -> p t h", t=GT),
                                       ALU.pow).then_inc(factor_ready, 1)
                loop(pool, NG, group)

            @block.vector
            def _(dv):
                dv.wait_ge(consts, 3)

                def feature(n, j):
                    features(dv, double[:, j], phi[:, BUF3[j]], phi_ready)

                def group(g):
                    keys = kv[:, 0, :, :]
                    dv.wait_ge(kv_in, 32 * (g + 1))
                    feature_norms(dv, g, keys, square, norm2, s)
                    dv.tensor_scalar(norm2[:, :, :], norm2[:, :, :], 1e-24, ROOT4 ** -2, ALU.max, ALU.mult).then_inc(clamped, 1)
                    if real(g, 1):
                        feature(g * GT - 1, GT - 1)
                    dv.wait_ge(factor_ready, g + 1)
                    after(dv, phi_ready, g * GT)
                    feature_double(dv, g, keys, factor, double, s)
                    for j in range(GT):
                        n, u = g * GT + j, BUF3[j]
                        after(dv, summed, n - BEHIND3[j] + 1)
                        dv.tensor_scalar(vals[:, u, :, 0:1], spread(k.share[:, bass.ds(n, 1)], 1, H0), 1.0, None, ALU.mult)
                        dv.tensor_scalar(vals[:, u, :, 1:VW], kv[:, 1, j, :].rearrange("p (h d) -> p h d", h=H0),
                                         k.share[:, bass.ds(n, 1)], None, ALU.mult)
                        dv.tensor_copy(phi[:, u, :, SHIFTS * D0:FEAT - 1], double[:, j, :, 0:D0]).then_inc(vals_ready, 1)
                        if j < GT - 1:
                            feature(n, j)
                loop(dv, NG, group)
                feature(NT - 1, GT - 1)
                dv.wait_ge(summed, NT)
                for n in range(H0 // 2):
                    dv.tensor_copy(sums[:, n, 0:512], long[n][:, :])
                dv.tensor_copy(sums[:, :, 512:FEAT], short[:, :, :]).then_inc(sums_kept, 1)
                for c in range(FCH):
                    m = P if c < FCH - 1 else FLAST
                    dv.wait_ge(turned, c + 1)
                    if c == 0:
                        parts = [(0, D0, 0.5), (D0, 2 * D0, 1.0), (2 * D0, P, 1.0)]
                    elif c < FCH - 1:
                        parts = [(0, P, 1.0)]
                    else:
                        parts = [(0, D0, 0.5), (D0, 2 * D0, ROOT4 ** 2), (2 * D0, m, ROOT4 ** 4)]
                    for lo, hi, weight in parts:
                        ins = dv.tensor_scalar(k.mixed[lo:hi, c, :].rearrange("p (h d) -> p h d", h=H0),
                                               turn[c % 2][lo:hi, :].rearrange("p (h d) -> p h d", h=H0)[:, :, 0:VW],
                                               weight, None, ALU.mult)
                    ins.then_inc(kept, 1)

            @block.tensor
            def _(pe):
                pe.wait_ge(zeroed, 1)
                for bank in long:
                    pe.matmul(bank[:, :], zeros[:, 0:P], zeros[:, :], start=True, stop=False, skip_group_check=True)
                pe.matmul(short[:, :, :], zeros[:, 0:P], zeros[:, 0:H0 // 2 * (FEAT - 512)], start=True, stop=False, skip_group_check=True)

                def group(g):
                    for j in range(GT):
                        n, u = g * GT + j, BUF3[j]
                        pe.wait_ge(phi_ready, n + 1)
                        for h in range(H0):
                            lanes = slice(h % 2 * 64, h % 2 * 64 + VW)
                            pe.matmul(long[h // 2][lanes, :], vals[:, u, h, :], phi[:, u, h, 0:512],
                                      start=False, stop=False, skip_group_check=True)
                            ins = pe.matmul(short[lanes, h // 2, :], vals[:, u, h, :], phi[:, u, h, 512:FEAT],
                                            start=False, stop=False, skip_group_check=True)
                        ins.then_inc(summed, 1)
                loop(pe, NG, group)
                pe.wait_ge(sums_kept, 1)
                for c in range(FCH):
                    m = P if c < FCH - 1 else FLAST
                    after(pe, kept, c - 1)
                    for n in range(H0 // 2):
                        ins = pe.transpose(turn[c % 2][0:m, n * P:(n + 1) * P], sums[:, n, c * P:c * P + m], k.ident[:, :])
                    ins.then_inc(turned, 1)


def mix_queries(nc, k, a):
    with ExitStack() as ctx:
        sb, ps, sem = scope(nc, ctx, "mix_queries")
        q = sb("q", [P, 1, GT, C])
        square = sb("square", [P, GT, C])
        norm2 = sb("norm2", [P, GT, H0])
        factor = sb("factor", [P, GT, H0])
        scaled = sb("scaled", [P, GT, H0])
        temper = sb("temper", [P, H0])
        double = sb("double", [P, GT, H0, 2 * D0])
        phi = sb("phi", [P, 3, H0, FEAT])
        headT = sb("headT", [P, 3, 4, P])
        restT = sb("restT", [P, H0, P])
        recip = sb("recip", [P, 2, H0])
        y = sb("y", [P, 2, C])
        yT = sb("yT", [P, KC, P])
        w = sb("w", [P, KC, C])
        bias = sb("bias", [P, C])
        part = sb("part", [P, 2, C])
        pT = [ps(f"pT{i}", [P, 4, P]) for i in range(2)]
        pH = [ps(f"pH{i}", [P, H0 // 2, P]) for i in range(2)]
        pY = ps("pY", [P, H0 // 2, P])
        heads = sb("heads", [P, H0 // 2, P])
        zeros = sb("zeros", [P, 512])
        pYT = ps("pYT", [P, KC, P])
        pO = [ps(f"pO{i}", [P, C]) for i in range(2)]
        s = Core()
        s.squared, s.norm2_ready, s.doubled = sem("squared"), sem("norm2_ready"), sem("doubled")
        loaded, q_in, clamped, factor_ready = sem("loaded"), sem("q_in"), sem("clamped"), sem("factor_ready")
        tempered, phi_ready = sem("tempered"), sem("phi_ready")
        turned, kept, head_done, recip_ready = sem("turned"), sem("kept"), sem("head_done"), sem("recip_ready")
        y_ready, yT_psum, yT_ready, projected = sem("y_ready"), sem("yT_psum"), sem("yT_ready"), sem("projected")
        part_ready, consts, done = sem("part_ready"), sem("consts"), sem("done")
        heads_kept, turned_back, zeroed = sem("heads_kept"), sem("turned_back"), sem("zeroed")
        QUADS = H0 + 2

        with nc.Block() as block:
            @block.sync
            def _(sp):
                for n in range(KC):
                    sp.dma_start(w[:, n, :], a["w_mixproj"][n * P:(n + 1) * P, :]).then_inc(loaded, 16)
                sp.dma_start(bias[:, :], a["b_mixproj"].partition_broadcast(P)).then_inc(loaded, 16)
                sp.dma_start(temper[:, :], a["temperature"].partition_broadcast(P)).then_inc(loaded, 16)

                def group(g):
                    after(sp, s.doubled, g)
                    sp.dma_start(q[:, 0, :, :], k.mix_qkv[bass.ds(g * GN, GN), 2 * C:3 * C]
                                 .rearrange("(t p) c -> p t c", p=P)).then_inc(q_in, 16)
                loop(sp, NG, group)

            @block.gpsimd
            def _(pool):
                pool.memset(zeros[:, :], 0.0).then_inc(zeroed, 1)
                for u in range(3):
                    pool.memset(phi[:, u, :, FEAT - 1:FEAT], 1.0).then_inc(consts, 1)

                def group(g):
                    pool.wait_ge(clamped, g + 1)
                    pool.tensor_tensor(factor[:, :, :], norm2[:, :, :], k.power[:, 0:GT * H0].rearrange("p (t h) -> p t h", t=GT),
                                       ALU.pow).then_inc(factor_ready, 1)
                loop(pool, NG, group)

            @block.vector
            def _(dv):
                dv.wait_ge(consts, 3)
                dv.wait_ge(loaded, 64)

                def divide(n, j):
                    u, found = j % 2, pY.rearrange("p n (m d) -> p (n m) d", m=2)
                    after(dv, yT_psum, n - BEHIND[j] + 1)
                    dv.wait_ge(turned_back, n + 1)
                    dv.reciprocal(recip[:, u, :], found[:, :, 0]).then_inc(recip_ready, 1)
                    dv.wait_ge(recip_ready, n + 1)
                    dv.tensor_tensor(y[:, u, :].rearrange("p (h d) -> p h d", h=H0), found[:, :, 1:VW],
                                     spread(recip[:, u, :], 2, D0), ALU.mult).then_inc(y_ready, 1)

                def add(n, u):
                    dv.wait_ge(projected, n + 1)
                    dv.tensor_tensor(part[:, u, :], pO[u][:, :], bias[:, :], ALU.add).then_inc(part_ready, 1)
                    dv.wait_ge(part_ready, n + 1)
                    nodes = k.x[:, bass.ds(n, 1), :]
                    dv.tensor_tensor(nodes, nodes, part[:, u:u + 1, :], ALU.add).then_inc(done, 1)

                def group(g):
                    queries = q[:, 0, :, :]
                    dv.wait_ge(q_in, 16 * (g + 1))
                    feature_norms(dv, g, queries, square, norm2, s)
                    dv.tensor_scalar(norm2[:, :, :], norm2[:, :, :], ROOT4 ** 2, 1e-24, ALU.mult, ALU.max).then_inc(clamped, 1)
                    if real(g, 1):
                        divide(g * GT - 2, GT - 2)
                    dv.wait_ge(factor_ready, g + 1)
                    dv.scalar_tensor_tensor(out=scaled[:, :, :], in0=factor[:, :, :], scalar=ROOT4 ** 2, in1=spread(temper[:, :], 1, GT),
                                            op0=ALU.mult, op1=ALU.mult).then_inc(tempered, 1)
                    dv.wait_ge(tempered, g + 1)
                    after(dv, phi_ready, g * GT)
                    feature_double(dv, g, queries, scaled, double, s)
                    for j in range(GT):
                        n, u = g * GT + j, BUF3[j]
                        after(dv, turned, QUADS * (n - BEHIND3[j] + 1))
                        dv.tensor_copy(phi[:, u, :, SHIFTS * D0:FEAT - 1], double[:, j, :, 0:D0])
                        features(dv, double[:, j], phi[:, u], phi_ready)
                        if j > 0 and real(n, 2):
                            divide(n - 2, (j - 2) % GT)
                        if real(n, 3):
                            add(n - 3, (j - 3) % GT % 2)
                loop(dv, NG, group)
                divide(NT - 2, GT - 2)
                add(NT - 3, (GT - 3) % 2)
                divide(NT - 1, GT - 1)
                add(NT - 2, (GT - 2) % 2)
                add(NT - 1, (GT - 1) % 2)

            @block.scalar
            def _(ac):
                def keep(n):
                    ac.wait_ge(yT_psum, n + 1)
                    after(ac, projected, n)
                    ac.copy(yT[:, :, :], pYT[:, :, :]).then_inc(yT_ready, 1)

                def keep_heads(n, j):
                    ac.wait_ge(head_done, n * H0 + H0)
                    after(ac, turned_back, n)
                    ac.copy(heads[:, :, :], pH[j % 2][:, :, :]).then_inc(heads_kept, 1)

                def group(g):
                    for j in range(GT):
                        n = g * GT + j
                        if real(n, 1):
                            keep_heads(n - 1, (j - 1) % GT)
                        for c in range(QUADS):
                            ac.wait_ge(turned, n * QUADS + c + 1)
                            if c < 2:
                                after(ac, head_done, n * H0)
                                ac.copy(restT[0:FLAST, 4 * c:4 * c + 4, :], pT[c % 2][0:FLAST, :, :]).then_inc(kept, 1)
                            else:
                                after(ac, head_done, n * H0 + max(c - 4, 0))
                                ac.copy(headT[:, (c - 2) % 3, :, :], pT[c % 2][:, :, :]).then_inc(kept, 1)
                            if c == 8 and real(n, 2):
                                keep(n - 2)
                loop(ac, NG, group)
                keep_heads(NT - 1, GT - 1)
                keep(NT - 2)
                keep(NT - 1)

            @block.tensor
            def _(pe):
                pe.wait_ge(loaded, 64)
                pe.wait_ge(zeroed, 1)
                for bank in pH:
                    pe.matmul(bank[:, :, :], zeros[:, 0:P], zeros[:, :], start=True, stop=True)

                def turn_back(n):
                    pe.wait_ge(heads_kept, n + 1)
                    after(pe, y_ready, n)
                    for m in range(H0 // 2):
                        ins = pe.transpose(pY[:, m, :], heads[:, m, :], k.ident[:, :])
                    ins.then_inc(turned_back, 1)

                def project(n, u):
                    pe.wait_ge(y_ready, n + 1)
                    after(pe, yT_ready, n)
                    for c in range(KC):
                        ins = pe.transpose(pYT[:, c, :], y[:, u, c * P:(c + 1) * P], k.ident[:, :])
                    ins.then_inc(yT_psum, 1)

                def product(n, u, j):
                    pe.wait_ge(yT_ready, n + 1)
                    after(pe, part_ready, n - BEHIND[j % GT] + 1)
                    for c in range(KC):
                        ins = pe.matmul(pO[u][:, :], yT[:, c, :], w[:, c, :], start=c == 0, stop=c == KC - 1)
                    ins.then_inc(projected, 1)

                def group(g):
                    for j in range(GT):
                        n, u = g * GT + j, BUF3[j]
                        pe.wait_ge(phi_ready, n + 1)
                        for c in range(QUADS + 1):
                            if c == 3 and real(n, 1):
                                turn_back(n - 1)
                            if c == 7 and real(n, 2):
                                project(n - 2, (j - 2) % GT % 2)
                            if c < QUADS:
                                after(pe, kept, n * QUADS + c - 1)
                                for m in range(4):
                                    if c < 2:
                                        ins = pe.transpose(pT[c % 2][0:FLAST, m, :], phi[:, u, 4 * c + m, (FCH - 1) * P:FEAT],
                                                           k.ident[:, :])
                                    else:
                                        ins = pe.transpose(pT[c % 2][:, m, :], phi[:, u, c - 2, m * P:(m + 1) * P], k.ident[:, :])
                                ins.then_inc(turned, 1)
                            if c >= 3:
                                h = c - 3
                                pe.wait_ge(kept, n * QUADS + c)
                                if h == 0:
                                    after(pe, heads_kept, n - BEHIND[j] + 1)
                                to = pH[j % 2][h % 2 * 64:h % 2 * 64 + VW, h // 2, :]
                                pe.matmul(to, k.mixed[0:FLAST, FCH - 1, h * VW:(h + 1) * VW], restT[0:FLAST, h, :],
                                          start=True, stop=False)
                                for m in range(4):
                                    ins = pe.matmul(to, k.mixed[:, m, h * VW:(h + 1) * VW], headT[:, h % 3, m, :],
                                                    start=False, stop=m == 3)
                                ins.then_inc(head_done, 1)
                        if real(n, 2):
                            i = (j - 2) % GT
                            product(n - 2, i % 2, i)
                loop(pe, NG, group)
                turn_back(NT - 1)
                for i in (GT - 2, GT - 1):
                    project(NT - GT + i, i % 2)
                    product(NT - GT + i, i % 2, i)


def layer_first(nc, k, a):
    HID = 4 * C
    HC = HID // P
    HALF = GN // 2
    with ExitStack() as ctx:
        sb, ps, sem = scope(nc, ctx, "layer_first")
        t, s = norm_tensors(sb, sem)
        wp = sb("wp", [P, KC, C])
        w1 = sb("w1", [P, KC, HID])
        w2 = sb("w2", [P, HC, C])
        b1 = sb("b1", [P, HC])
        bp = sb("bp", [P, C])
        b2 = sb("b2", [P, C])
        gain = sb("gain", [P, KC])
        shift = sb("shift", [P, KC])
        den = sb("den", [P, GT, H0])
        rec = sb("rec", [P, GT, H0])
        mean = sb("mean", [P, GT, C])
        meanT = sb("meanT", [P, 2, KC, P])
        based = sb("based", [P, GT, C])
        mid = sb("mid", [P, GT, C])
        result = sb("result", [P, GT, C])
        hT = sb("hT", [P, KC, GN])
        hid = sb("hid", [P, HC, GN])
        pT = [ps(f"pT{i}", [P, KC, P]) for i in range(2)]
        pA = ps("pA", [P, C])
        pS = ps("pS", [P, C])
        pW = [ps(f"pW{i}", [P, 2, 512]) for i in range(2)]
        loaded, den_ready, rec_ready, mean_ready = sem("loaded"), sem("den_ready"), sem("rec_ready"), sem("mean_ready")
        turned, kept, multiplied, taken = sem("turned"), sem("kept"), sem("multiplied"), sem("taken")
        wide_ready, gelu_ready, based_ready, result_base = sem("wide_ready"), sem("gelu_ready"), sem("based_ready"), sem("result_base")
        fence, done, projected, mid_ready = sem("fence"), sem("done"), sem("projected"), sem("mid_ready")

        with nc.Block() as block:
            @block.sync
            def _(sp):
                for n in range(KC):
                    sp.dma_start(wp[:, n, :], a["w_p"][n * P:(n + 1) * P, :]).then_inc(loaded, 16)
                    sp.dma_start(w1[:, n, :], a["w_1"][n * P:(n + 1) * P, :]).then_inc(loaded, 16)
                sp.dma_start(w2[:, :, :], a["w_2"].rearrange("(c p) n -> p c n", p=P)).then_inc(loaded, 16)
                for to, name in ((b1, "b_1"), (gain, "ln_g"), (shift, "ln_b")):
                    sp.dma_start(to[:, :], a[name]).then_inc(loaded, 16)
                sp.dma_start(bp[:, :], a["b_p"].partition_broadcast(P)).then_inc(loaded, 16)
                sp.dma_start(b2[:, :], a["b_2"].partition_broadcast(P)).then_inc(loaded, 16)
                load_experts(sp, k, a)

            @block.gpsimd
            def _(pool):
                pool.wait_ge(loaded, 160)

                def group(g):
                    after(pool, mid_ready, g * GT)
                    pool.sem_inc(fence, 1)
                    pool.tensor_tensor(based[:, :, :], k.xn[:, bass.ds(g * GT, GT), :], spread(bp[:, :], 1, GT),
                                       ALU.add).then_inc(based_ready, 1)
                    deviations(pool, g, k, s, t)
                    after(pool, done, g * GT)
                    pool.wait_ge(mid_ready, g * GT + GT)
                    pool.tensor_tensor(result[:, :, :], mid[:, :, :], spread(b2[:, :], 1, GT), ALU.add).then_inc(result_base, 1)
                loop(pool, NG, group)

            @block.vector
            def _(dv):
                def begin(g):
                    sums = k.sums[:, bass.ds(g * GT, GT), :]
                    dv.tensor_scalar(den[:, :, :], sums[:, :, C:SW], 1e-30, None, ALU.max).then_inc(den_ready, 1)
                    dv.wait_ge(den_ready, g + 1)
                    dv.reciprocal(rec[:, :, :], den[:, :, :]).then_inc(rec_ready, 1)
                    dv.wait_ge(rec_ready, g + 1)
                    after(dv, turned, 10 * g - 5)
                    dv.tensor_tensor(mean[:, :, :].rearrange("p t (h d) -> p t h d", h=H0),
                                     sums[:, :, 0:C].rearrange("p t (h d) -> p t h d", h=H0),
                                     spread(rec[:, :, :], 3, D0), ALU.mult).then_inc(mean_ready, 1)
                    dv.wait_ge(based_ready, g + 1)
                    after(dv, result_base, g)
                    for j in range(GT):
                        dv.wait_ge(projected, GT * g + j + 1)
                        dv.tensor_tensor(mid[:, j, :], pA[:, :], based[:, j, :], ALU.add).then_inc(mid_ready, 1)
                    dv.wait_ge(mid_ready, GT * g + GT)
                    after(dv, turned, 10 * g)
                    normalise(dv, g, lambda g, j: mid[:, j, :], s, t)

                def group(g, last=False):
                    if not last:
                        begin(g + 1)
                    dv.wait_ge(result_base, g + 1)
                    for j in range(GT):
                        dv.wait_ge(multiplied, GT * g + j + 1)
                        dv.tensor_tensor(result[:, j, :], pS[:, :], result[:, j, :], ALU.add).then_inc(taken, 1)
                        dv.wait_ge(taken, GT * g + j + 1)
                        nodes = k.x[:, bass.ds(g * GT + j, 1), :]
                        dv.tensor_tensor(nodes, nodes, result[:, j:j + 1, :], ALU.add).then_inc(done, 1)
                begin(0)
                loop(dv, NG - 1, group)
                group(NG - 1, True)

            @block.scalar
            def _(ac):
                ac.wait_ge(loaded, 160)

                def begin(g):
                    for j in range(GT):
                        ac.wait_ge(turned, 10 * g + j + 1)
                        after(ac, projected, GT * g + j - 1)
                        ac.copy(meanT[:, j % 2, :, :], pT[j % 2][:, :, :]).then_inc(kept, 1)

                def group(g, last=False):
                    for j in range(GT):
                        ac.wait_ge(turned, 10 * g + GT + j + 1)
                        after(ac, wide_ready, HC * g)
                        for c in range(KC):
                            ins = ac.activation(hT[:, c, j * P:(j + 1) * P], pT[(GT + j) % 2][:, c, :], ACT.Identity,
                                                bias=shift[:, c:c + 1], scale=gain[:, c:c + 1])
                        ins.then_inc(kept, 1)
                    if not last:
                        begin(g + 1)
                    after(ac, multiplied, GT * g)
                    for m in range(HC):
                        ac.wait_ge(wide_ready, HC * g + m + 1)
                        ac.activation(hid[:, m, :].rearrange("p (a b) -> p a b", a=2), pW[m % 2][:, :, 0:HALF], ACT.Gelu,
                                      bias=b1[:, m:m + 1]).then_inc(gelu_ready, 1)
                begin(0)
                loop(ac, NG - 1, group)
                group(NG - 1, True)

            @block.tensor
            def _(pe):
                pe.wait_ge(loaded, 160)

                def turn(g, n, source, j):
                    after(pe, kept, 10 * g + n - 1)
                    for c in range(KC):
                        ins = pe.transpose(pT[n % 2][:, c, :], source[:, j, c * P:(c + 1) * P], k.ident[:, :])
                    ins.then_inc(turned, 1)

                def begin(g):
                    pe.wait_ge(mean_ready, g + 1)
                    for j in range(GT + 1):
                        if j < GT:
                            turn(g, j, mean, j)
                        if j > 0:
                            m = j - 1
                            pe.wait_ge(kept, 10 * g + m + 1)
                            after(pe, mid_ready, GT * g + m)
                            for c in range(KC):
                                ins = pe.matmul(pA[:, :], meanT[:, m % 2, c, :], wp[:, c, :], start=c == 0, stop=c == KC - 1)
                            ins.then_inc(projected, 1)

                def group(g, last=False):
                    for j in range(GT):
                        pe.wait_ge(s.normed_ready, g * GT + j + 1)
                        turn(g, GT + j, t.normed, j)
                    if not last:
                        begin(g + 1)
                    pe.wait_ge(kept, 10 * g + 10)
                    for m in range(HC):
                        after(pe, gelu_ready, HC * g + m - 1)
                        for half in range(2):
                            for c in range(KC):
                                ins = pe.matmul(pW[m % 2][:, half, 0:HALF], w1[:, c, m * P:(m + 1) * P],
                                                hT[:, c, half * HALF:(half + 1) * HALF], start=c == 0, stop=c == KC - 1)
                        ins.then_inc(wide_ready, 1)
                    for j in range(GT):
                        pe.wait_ge(gelu_ready, HC * g + HC)
                        after(pe, taken, GT * g + j)
                        for m in range(HC):
                            ins = pe.matmul(pS[:, :], hid[:, m, j * P:(j + 1) * P], w2[:, m, :],
                                            start=m == 0, stop=m == HC - 1)
                        ins.then_inc(multiplied, 1)
                begin(0)
                loop(pe, NG - 1, group)
                group(NG - 1, True)


def load_experts(sp, k, a):
    for e in range(NE):
        for to, name in ((k.w_hidden, "w_hidden1"), (k.w_deep, "w_deep"), (k.w_out, "w_out1")):
            sp.dma_start(to[:, e, :, :], a[name][e].rearrange("(c p) n -> p c n", p=P)).then_inc(k.expert_in[e], 16)


def experts(nc, k, a):
    wide = C
    MC = wide // P
    layers = 2
    HALF = GN // 2
    stage = "experts1"
    TURNS = GT + 3
    SMALL = 1 + GT + GT * NE
    WIDE = NE * layers * MC
    plan = [("hidden", 0, 0), ("hidden", 0, 1), ("hidden", 1, 0), ("gates", 0, 0)]
    for e in range(NE):
        plan += [("hidden", 0, e + 2)] * (e + 2 < NE) + [("hidden", 1, e + 1)] * (e + 1 < NE) + [("out", 0, e)]
    wides = [(layer, e, m) for what, layer, e in plan if what == "hidden" for m in range(MC)]
    nth = {w: i for i, w in enumerate(wides)}
    with ExitStack() as ctx:
        sb, ps, sem = scope(nc, ctx, stage)
        t, s = norm_tensors(sb, sem)
        w1, w2, wo = k.w_hidden, k.w_deep, k.w_out
        wr = sb("wr", [P, KC, NE])
        bo = sb("bo", [NE, C])
        br = sb("br", [P, NE])
        bn = sb("bn", [P, 2, 5, MC * NE])
        bn_eps = sb("bn_eps", [P, 2, MC * NE])
        scale = sb("scale", [P, 2, MC * NE])
        offset = sb("offset", [P, 2, MC * NE])
        hT = sb("hT", [P, KC, GN])
        act = [sb(f"act{n}", [P, 2, MC, GN]) for n in range(layers)]
        y = sb("y", [P, GT, C])
        logits = sb("logits", [P, GT, NE])
        shifted = sb("shifted", [P, GT, NE])
        odds = sb("odds", [P, GT, NE])
        gate = sb("gate", [P, GT, NE])
        gateT = sb("gateT", [NE, GN])
        top = sb("top", [P, GT])
        total = sb("total", [P, GT])
        pT = [ps(f"pT{i}", [P, KC, P]) for i in range(2)]
        pS = [ps(f"pS{i}", [P, 512]) for i in range(2)]
        pW = [ps(f"pW{i}", [P, 2, 512]) for i in range(2)]
        loaded, bn_ready, bn_power, offset_ready = sem("loaded"), sem("bn_ready"), sem("bn_power"), sem("offset_ready")
        turned, kept, wide_ready, act_ready = sem("turned"), sem("kept"), sem("wide_ready"), sem("act_ready")
        multiplied, taken, small, shifted_ready = sem("multiplied"), sem("taken"), sem("small"), sem("shifted_ready")
        odds_ready, gate_ready, done = sem("odds_ready"), sem("gate_ready"), sem("done")
        fold = sem("fold")
        LOADS = 4

        with nc.Block() as block:
            @block.sync
            def _(sp):
                sp.dma_start(wr[:, :, :], a["w_r" + stage[-1]].rearrange("(c p) n -> p c n", p=P)).then_inc(loaded, 16)
                sp.dma_start(bo[:, :], a["b_o" + stage[-1]]).then_inc(loaded, 16)
                sp.dma_start(br[:, :], a["b_r" + stage[-1]].partition_broadcast(P)).then_inc(loaded, 16)
                sp.dma_start(bn[:, :, :, :], a["bn"]).then_inc(loaded, 16)

            @block.gpsimd
            def _(pool):
                pool.wait_ge(bn_ready, 1)
                pool.tensor_tensor(scale[:, :, :].rearrange("p l n -> p (l n)"), bn_eps[:, :, :].rearrange("p l n -> p (l n)"),
                                   k.power[:, 0:2 * MC * NE], ALU.pow).then_inc(bn_power, 1)
                loop(pool, NG, lambda g: deviations(pool, g, k, s, t))

            @block.vector
            def _(dv):
                dv.wait_ge(loaded, 16 * LOADS)
                dv.tensor_scalar(bn_eps[:, :, :], bn[:, :, 3, :], 1e-3, None, ALU.add).then_inc(bn_ready, 1)
                dv.wait_ge(bn_power, 1)
                chain = Chain(dv, fold, 4)
                chain.turn(0)
                chain(dv.tensor_tensor(scale[:, :, :], scale[:, :, :], bn[:, :, 0, :], ALU.mult))
                chain(dv.tensor_tensor(offset[:, :, :], bn[:, :, 4, :], bn[:, :, 2, :], ALU.subtract))
                chain(dv.tensor_tensor(offset[:, :, :], offset[:, :, :], scale[:, :, :], ALU.mult))
                chain(dv.tensor_tensor(offset[:, :, :], offset[:, :, :], bn[:, :, 1, :], ALU.add))
                chain = Chain(dv, small, 3)

                def softmax(g):
                    chain(dv.tensor_reduce(top[:, :], logits[:, :, :], AX, ALU.max))
                    dv.tensor_tensor(shifted[:, :, :], logits[:, :, :], spread(top[:, :], 2, NE), ALU.subtract).then_inc(shifted_ready, 1)
                    dv.wait_ge(odds_ready, g + 1)
                    chain(dv.tensor_reduce(total[:, :], odds[:, :, :], AX, ALU.add))
                    chain(dv.reciprocal(total[:, :], total[:, :]))
                    dv.tensor_tensor(gate[:, :, :], odds[:, :, :], spread(total[:, :], 2, NE), ALU.mult).then_inc(gate_ready, 1)

                def norm(g):
                    after(dv, turned, TURNS * g - 3)
                    normalise(dv, g, lambda g, j: k.x[:, bass.ds(g * GT + j, 1), :], s, t)

                def group(g, last=False):
                    chain.turn(g)
                    dv.wait_ge(multiplied, SMALL * g + 1)
                    dv.tensor_tensor(logits[:, :, :], pS[0][:, 0:GT * NE].rearrange("p (t e) -> p t e", t=GT),
                                     spread(br[:, :], 1, GT), ALU.add).then_inc(taken, 1)
                    dv.wait_ge(taken, SMALL * g + 1)
                    softmax(g)
                    assert chain.left == 0, chain.left
                    for j in range(GT):
                        dv.wait_ge(multiplied, SMALL * g + 2 + j)
                        dv.tensor_copy(y[:, j, :], pS[(1 + j) % 2][:, 0:C]).then_inc(taken, 1)
                    for e in range(NE):
                        for j in range(GT):
                            n = 1 + GT + e * GT + j
                            dv.wait_ge(multiplied, SMALL * g + n + 1)
                            dv.wait_ge(taken, SMALL * g + n - GT + 1)
                            dv.scalar_tensor_tensor(out=y[:, j, :], in0=pS[n % 2][:, 0:C], scalar=gate[:, j, e:e + 1], in1=y[:, j, :],
                                                    op0=ALU.mult, op1=ALU.add).then_inc(taken, 1)
                        if e == NE // 2 and not last:
                            norm(g + 1)
                    dv.wait_ge(taken, SMALL * g + SMALL)
                    nodes = k.x[:, bass.ds(g * GT, GT), :]
                    dv.tensor_tensor(nodes, nodes, y[:, :, :], ALU.add).then_inc(done, 1)
                norm(0)
                loop(dv, NG - 1, group)
                group(NG - 1, True)

            @block.scalar
            def _(ac):
                ac.wait_ge(loaded, 16 * LOADS)
                ac.wait_ge(fold, 4)

                def group(g):
                    for j in range(GT):
                        ac.wait_ge(turned, TURNS * g + j + 1)
                        after(ac, wide_ready, WIDE * g)
                        for c in range(KC):
                            ins = ac.copy(hT[:, c, j * P:(j + 1) * P], pT[j % 2][:, c, :])
                        ins.then_inc(kept, 1)
                    for what, layer, e in plan:
                        if what == "hidden":
                            for m in range(MC):
                                n = nth[layer, e, m]
                                ac.wait_ge(wide_ready, WIDE * g + n + 1)
                                if layer < layers - 1:
                                    after(ac, wide_ready, WIDE * g + nth[layer + 1, e - 2, MC - 1] + 1 if e >= 2
                                          else WIDE * (g - 1) + nth[layer + 1, NE - 2 + e, MC - 1] + 1)
                                else:
                                    after(ac, multiplied, SMALL * g + 1 + GT + (e - 1) * GT if e >= 2
                                          else SMALL * (g - 1) + 1 + GT + (NE - 1 + e) * GT)
                                to = act[layer][:, e % 2, m, :].rearrange("p (a b) -> p a b", a=2)
                                ac.activation(to, pW[n % 2][:, :, 0:HALF], ACT.Relu,
                                              bias=offset[:, layer, m * NE + e:m * NE + e + 1],
                                              scale=scale[:, layer, m * NE + e:m * NE + e + 1]).then_inc(act_ready, 1)
                        elif what == "gates":
                            ac.wait_ge(shifted_ready, g + 1)
                            ac.activation(odds[:, :, :], shifted[:, :, :], ACT.Exp).then_inc(odds_ready, 1)
                            for q in range(3):
                                i = GT + q
                                tiles = 2 if q < 2 else 1
                                ac.wait_ge(turned, TURNS * g + i + 1)
                                after(ac, multiplied, SMALL * g - GT * NE)
                                ac.copy(gateT[:, q * 2 * P:(q * 2 + tiles) * P].rearrange("e (t n) -> e t n", n=P),
                                        pT[i % 2][0:NE, 0:tiles, :]).then_inc(kept, 1)
                loop(ac, NG, group)

            @block.tensor
            def _(pe):
                pe.wait_ge(loaded, 16 * LOADS)

                def group(g):
                    for j in range(GT):
                        pe.wait_ge(s.normed_ready, g * GT + j + 1)
                        after(pe, kept, TURNS * g + j - 1)
                        for c in range(KC):
                            ins = pe.transpose(pT[j % 2][:, c, :], t.normed[:, j, c * P:(c + 1) * P], k.ident[:, :])
                        ins.then_inc(turned, 1)
                    pe.wait_ge(kept, TURNS * g + GT)
                    after(pe, taken, SMALL * g - 1)
                    for j in range(GT):
                        for c in range(KC):
                            ins = pe.matmul(pS[0][:, j * NE:(j + 1) * NE], hT[:, c, j * P:(j + 1) * P], wr[:, c, :],
                                            start=c == 0, stop=c == KC - 1)
                    ins.then_inc(multiplied, 1)
                    for what, layer, e in plan:
                        if what == "hidden":
                            if layer:
                                pe.wait_ge(act_ready, WIDE * g + nth[layer - 1, e, MC - 1] + 1)
                            weights = w2 if layer else w1
                            if layer == 0:
                                pe.wait_ge(k.expert_in[e], 48)
                            for m in range(MC):
                                n = nth[layer, e, m]
                                after(pe, act_ready, WIDE * g + n - 1)
                                for half in range(2):
                                    span = slice(half * HALF, (half + 1) * HALF)
                                    for c in range(KC):
                                        moving = act[0][:, e % 2, c, span] if layer else hT[:, c, span]
                                        ins = pe.matmul(pW[n % 2][:, half, 0:HALF], weights[:, e, c, m * P:(m + 1) * P], moving,
                                                        start=c == 0, stop=c == KC - 1)
                                ins.then_inc(wide_ready, 1)
                        elif what == "gates":
                            pe.wait_ge(gate_ready, g + 1)
                            for q in range(3):
                                i = GT + q
                                after(pe, kept, TURNS * g + i - 1)
                                for j in range(2 * q, min(2 * q + 2, GT)):
                                    ins = pe.transpose(pT[i % 2][0:NE, j % 2, :], gate[:, j, :], k.ident[:, :])
                                ins.then_inc(turned, 1)
                            pe.wait_ge(kept, TURNS * g + TURNS)
                            for j in range(GT):
                                n = 1 + j
                                after(pe, taken, SMALL * g + n - 1)
                                pe.matmul(pS[n % 2][:, 0:C], gateT[:, j * P:(j + 1) * P], bo[:, :], start=True,
                                          stop=True).then_inc(multiplied, 1)
                        else:
                            pe.wait_ge(act_ready, WIDE * g + nth[layers - 1, e, MC - 1] + 1)
                            for j in range(GT):
                                n = 1 + GT + e * GT + j
                                after(pe, taken, SMALL * g + n - 1)
                                for m in range(MC):
                                    ins = pe.matmul(pS[n % 2][:, 0:C], act[layers - 1][:, e % 2, m, j * P:(j + 1) * P], wo[:, e, m, :],
                                                    start=m == 0, stop=m == MC - 1)
                                ins.then_inc(multiplied, 1)
                loop(pe, NG, group)


EP = 125
EJ = EDGES // EP
GB = 8


def running(g, j, back):
    return j >= back or not isinstance(g, int)


def project_second(nc, k, a):
    ZW = C + 2 * H1
    with ExitStack() as ctx:
        sb, ps, sem = scope(nc, ctx, "project_second")
        t, s = norm_tensors(sb, sem)
        w = sb("w", [P, KC, ZW])
        natural = sb("natural", [P, KC, C])
        vectors = sb("vectors", [P, KC, 2 * H1])
        xT = sb("xT", [P, GT, KC, P])
        outs = sb("outs", [P, 2, ZW])
        pT = [ps(f"pT{i}", [P, KC, P]) for i in range(2)]
        pM = [ps(f"pM{i}", [P, ZW]) for i in range(2)]
        loaded, folded, fold_kept = sem("loaded"), sem("folded"), sem("fold_kept")
        xT_psum, xT_ready, projected, z_ready = sem("xT_psum"), sem("xT_ready"), sem("projected"), sem("z_ready")
        stored = [sem("stored0"), sem("stored1")]

        with nc.Block() as block:
            @block.sync
            def _(sp):
                for n in range(KC):
                    rows = slice(n * P, (n + 1) * P)
                    sp.dma_start(w[:, n, 0:C], a["w_z1"][rows, :]).then_inc(loaded, 16)
                    sp.dma_start(natural[:, n, :], a["w_natural1"][rows, :]).then_inc(loaded, 16)
                    sp.dma_start(vectors[:, n, :], a["vectors1"][rows, :]).then_inc(loaded, 16)

                def group(g):
                    for j in range(GT):
                        n, u = g * GT + j, j % 2
                        sp.wait_ge(z_ready, n + 1)
                        rows = bass.ds(n * P, P)
                        sp.dma_start(k.z_table[rows, :], outs[:, u, 0:C]).then_inc(stored[u], 16)
                        sp.dma_start(k.es_table1[rows, :], outs[:, u, C:C + H1]).then_inc(stored[u], 16)
                loop(sp, NG, group)
                for u in range(2):
                    sp.wait_ge(stored[u], 32 * USES[u] * NG)

            @block.gpsimd
            def _(pool):
                loop(pool, NG, lambda g: deviations(pool, g, k, s, t))

            @block.vector
            def _(dv):
                dv.wait_ge(folded, 1)
                dv.tensor_copy(w[:, :, C:ZW], pT[0][:, :, 0:2 * H1]).then_inc(fold_kept, 1)

                def norm(g):
                    after(dv, xT_psum, GT * g)
                    normalise(dv, g, lambda g, j: k.x[:, bass.ds(g * GT + j, 1), :], s, t)

                def group(g, last=False):
                    for j in range(GT):
                        n, u = g * GT + j, j % 2
                        dv.wait_ge(projected, n + 1)
                        after(dv, stored[u], 32 * uses(g, j))
                        dv.tensor_copy(k.ed[:, bass.ds(n, 1), :], pM[u][:, C + H1:ZW].unsqueeze(1))
                        dv.tensor_copy(outs[:, u, :], pM[u][:, 0:ZW]).then_inc(z_ready, 1)
                        if j == 0 and not last:
                            norm(g + 1)
                norm(0)
                loop(dv, NG - 1, group)
                group(NG - 1, True)

            @block.scalar
            def _(ac):
                ac.wait_ge(fold_kept, 1)

                def group(g):
                    for j in range(GT):
                        n, u = g * GT + j, j % 2
                        ac.wait_ge(xT_psum, n + 1)
                        after(ac, projected, n - GT + 1)
                        ac.copy(k.xn[:, bass.ds(n, 1), :], pT[u].rearrange("p c n -> p (c n)").unsqueeze(1))
                        ac.copy(xT[:, j, :, :], pT[u][:, :, :]).then_inc(xT_ready, 1)
                loop(ac, NG, group)

            @block.tensor
            def _(pe):
                pe.wait_ge(loaded, 96)
                for m in range(KC):
                    for c in range(KC):
                        ins = pe.matmul(pT[0][:, m, 0:2 * H1], natural[:, c, m * P:(m + 1) * P], vectors[:, c, :],
                                        start=c == 0, stop=c == KC - 1)
                ins.then_inc(folded, 1)
                pe.wait_ge(fold_kept, 1)

                def turn(n, j):
                    pe.wait_ge(s.normed_ready, n + 1)
                    after(pe, xT_ready, n - BEHIND[j] + 1)
                    for c in range(KC):
                        ins = pe.transpose(pT[j % 2][:, c, :], t.normed[:, j, c * P:(c + 1) * P], k.ident[:, :])
                    ins.then_inc(xT_psum, 1)

                def group(g):
                    for j in range(GT):
                        turn(g * GT + j, j)
                    for j in range(GT):
                        n, u = g * GT + j, j % 2
                        pe.wait_ge(xT_ready, n + 1)
                        after(pe, z_ready, n - BEHIND[j] + 1)
                        for q in range(KC):
                            ins = pe.matmul(pM[u][:, :], xT[:, j, q, :], w[:, q, :], start=q == 0, stop=q == KC - 1)
                        ins.then_inc(projected, 1)
                loop(pe, NG, group)


class SecondMixing:

    HK = 2 * HM
    W = HK * DM
    PAIRS = HM * DM // P

    def __init__(self, k, sb, sem, banks, dots, work, kv, weights, sums):
        HK, W, PAIRS = self.HK, self.W, self.PAIRS
        self.k, self.banks, self.dots = k, banks, dots
        self.w = sb("mix_w", [P, KC, W])
        self.xT = sb("mix_xT", [P, 2, KC, P])
        self.small = [sb(f"mix_{name}", [P, HK]) for name in ("total", "mean", "var", "vareps", "root", "rstd")]
        self.factor = sb("mix_factor", [P, HK])
        self.centred = work[:, 0:2 * W].rearrange("p (u h d) -> p u h d", u=2, h=HK)
        self.square = work[:, 2 * W:3 * W].rearrange("p (h d) -> p h d", h=HK)
        self.kv = kv.rearrange("p (u n) -> p u n", u=2)
        self.zeros = kv[:, 0:512]
        self.sums = sums[:, 0:PAIRS, :]
        self.wq, self.wo = [self.centred_as(tensor.rearrange("p j h -> p (j h)"), PAIRS) for tensor in weights]
        self.bias = sb("mix_bias", [1, C])
        self.inner = self.centred_as(work, PAIRS)
        self.whole = self.w[:, 0, 0:KC * C].rearrange("p (c n) -> p c n", c=KC)
        self.loaded, self.xT_ready, self.projected = sem("mix_loaded"), sem("mix_xT_ready"), sem("mix_projected")
        self.summed, self.mean_ready, self.centred_ready = sem("mix_summed"), sem("mix_mean_ready"), sem("mix_centred_ready")
        self.squared, self.var_ready, self.vareps_ready = sem("mix_squared"), sem("mix_var_ready"), sem("mix_vareps_ready")
        self.root_ready, self.rstd_ready, self.factor_ready = sem("mix_root_ready"), sem("mix_rstd_ready"), sem("mix_factor_ready")
        self.kv_ready, self.dots_done, self.zeroed, self.cleared = sem("mix_kv_ready"), sem("mix_dots_done"), sem("mix_zeroed"), sem("mix_cleared")
        self.sums_ready, self.inner_psum, self.inner_ready = sem("mix_sums_ready"), sem("mix_inner_psum"), sem("mix_inner_ready")
        self.whole_psum, self.whole_ready, self.applied, self.done = sem("mix_whole_psum"), sem("mix_whole_ready"), sem("mix_applied"), sem("mix_done")

    def centred_as(self, work, n):
        return work[:, 0:n * C].rearrange("p (c n) -> p c n", c=n)

    def load(self, sp, a):
        for n in range(KC):
            sp.dma_start(self.w[:, n, :], a["w_mixkv"][n * P:(n + 1) * P, :]).then_inc(self.loaded, 16)
        sp.dma_start(self.bias[:, :], a["b_mixout"]).then_inc(self.loaded, 16)
        sp.dma_start(self.wq, a["w_mixq"].rearrange("(c p) n -> p c n", p=P)).then_inc(self.loaded, 16)
        sp.dma_start(self.wo, a["w_mixout"].rearrange("(c p) n -> p c n", p=P)).then_inc(self.loaded, 16)

    def bank(self, u):
        return self.banks[:, u * self.W:(u + 1) * self.W]

    def vector(self, dv):
        HK, HALF = self.HK, HM
        total, mean, var, vareps, root, rstd = self.small
        dv.memset(self.zeros[:, :], 0.0).then_inc(self.zeroed, 1)
        dv.memset(self.sums[:, :, :], 0.0).then_inc(self.cleared, 1)

        def centre(n, u, j):
            heads = self.bank(u).rearrange("p (h d) -> p h d", h=HK)
            dv.wait_ge(self.projected, n + 1)
            dv.tensor_reduce(total[:, :], heads, AX, ALU.add).then_inc(self.summed, 1)
            dv.wait_ge(self.summed, n + 1)
            dv.tensor_scalar(mean[:, :], total[:, :], 1.0 / DM, None, ALU.mult).then_inc(self.mean_ready, 1)
            dv.wait_ge(self.mean_ready, n + 1)
            dv.tensor_tensor(self.centred[:, u, :, :], heads, spread(mean[:, :], 2, DM), ALU.subtract).then_inc(self.centred_ready, 1)

        def deviate(n, u):
            dv.wait_ge(self.squared, n + 1)
            dv.tensor_reduce(var[:, :], self.square[:, :, :], AX, ALU.add).then_inc(self.var_ready, 1)
            dv.wait_ge(self.var_ready, n + 1)
            dv.tensor_scalar(vareps[:, :], var[:, :], 1.0 / DM, 1e-5, ALU.mult, ALU.add).then_inc(self.vareps_ready, 1)

        def scale(n, u, j):
            dv.wait_ge(self.root_ready, n + 1)
            dv.reciprocal(rstd[:, :], root[:, :]).then_inc(self.rstd_ready, 1)
            dv.wait_ge(self.rstd_ready, n + 1)
            dv.tensor_copy(self.factor[:, 0:HALF], rstd[:, 0:HALF])
            dv.tensor_scalar(self.factor[:, HALF:HK], rstd[:, HALF:HK], self.k.share[:, bass.ds(n, 1)], None,
                             ALU.mult).then_inc(self.factor_ready, 1)
            dv.wait_ge(self.factor_ready, n + 1)
            after(dv, self.dots_done, n - BEHIND[j] + 1)
            dv.tensor_tensor(self.kv[:, u, :].rearrange("p (h d) -> p h d", h=HK), self.centred[:, u, :, :],
                             spread(self.factor[:, :], 2, DM), ALU.mult).then_inc(self.kv_ready, 1)

        def group(g):
            for j in range(GT):
                n, i = g * GT + j, (j - 1) % GT
                if running(g, j, 1):
                    deviate(n - 1, i % 2)
                    if j == 0:
                        scale(n - 1, i % 2, i)
                centre(n, j % 2, j)
                if j > 0:
                    scale(n - 1, i % 2, i)
        loop(dv, NG, group)
        deviate(NT - 1, (GT - 1) % 2)
        scale(NT - 1, (GT - 1) % 2, GT - 1)
        dv.wait_ge(self.dots_done, NT)
        dv.wait_ge(self.cleared, 1)
        for lo in (0, DM):
            ins = dv.tensor_copy(self.sums[lo:lo + DM, :, lo:lo + DM], self.dots[lo:lo + DM, :, lo:lo + DM])
        ins.then_inc(self.sums_ready, 1)

        def apply(g):
            for j in range(GT):
                n = g * GT + j
                dv.wait_ge(self.applied, n + 1)
                nodes = self.k.x[:, bass.ds(n, 1), :]
                dv.tensor_tensor(nodes, nodes, self.bank(j % 2)[:, 0:C].unsqueeze(1), ALU.add).then_inc(self.done, 1)
        loop(dv, NG, apply)

    def scalar(self, ac):
        total, mean, var, vareps, root, rstd = self.small

        def nodes(n, j, free):
            after(ac, free, n - BEHIND[j] + 1)
            ac.copy(self.xT[:, j % 2:j % 2 + 1, :, :].rearrange("p a c n -> p a (c n)"),
                    self.k.xn[:, bass.ds(n, 1), :]).then_inc(self.xT_ready, 1)

        def squares(n, u):
            ac.wait_ge(self.centred_ready, n + 1)
            after(ac, self.var_ready, n)
            ac.activation(self.square[:, :, :], self.centred[:, u, :, :], ACT.Square).then_inc(self.squared, 1)

        def roots(n):
            ac.wait_ge(self.vareps_ready, n + 1)
            after(ac, self.rstd_ready, n)
            ac.activation(root[:, :], vareps[:, :], ACT.Sqrt).then_inc(self.root_ready, 1)

        def group(g):
            nodes(g * GT, 0, self.projected)
            for j in range(GT):
                n = g * GT + j
                if j + 1 < GT:
                    nodes(n + 1, j + 1, self.projected)
                if running(g, j, 1):
                    roots(n - 1)
                squares(n, j % 2)
        loop(ac, NG, group)
        roots(NT - 1)
        ac.wait_ge(self.inner_psum, 1)
        ac.copy(self.inner[:, :, :], self.banks[:, 0:self.PAIRS * C].rearrange("p (c n) -> p c n", c=self.PAIRS)).then_inc(self.inner_ready, 1)
        ac.wait_ge(self.whole_psum, 1)
        ac.copy(self.whole[:, :, :], self.dots.rearrange("p a b -> p (a b)").rearrange("p (c n) -> p c n", c=KC)).then_inc(self.whole_ready, 1)

        def again(g):
            for j in range(GT):
                nodes(g * GT + j, j, self.applied)
        loop(ac, NG, again)

    def tensor(self, pe):
        pe.wait_ge(self.loaded, 80)
        pe.wait_ge(self.zeroed, 1)
        dots2d = self.dots.rearrange("p a b -> p (a b)")
        pe.matmul(dots2d, self.zeros[:, 0:P], self.zeros[:, :], start=True, stop=False, skip_group_check=True)

        def dots(n, u):
            pe.wait_ge(self.kv_ready, n + 1)
            for m in range(self.PAIRS):
                v = HM * DM + m * P
                ins = pe.matmul(self.dots[:, m, :], self.kv[:, u, v:v + P], self.kv[:, u, m * P:(m + 1) * P],
                                start=False, stop=False, skip_group_check=True)
            ins.then_inc(self.dots_done, 1)

        def group(g):
            for j in range(GT):
                n, u = g * GT + j, j % 2
                pe.wait_ge(self.xT_ready, n + 1)
                after(pe, self.centred_ready, n - BEHIND[j] + 1)
                for half in range(2):
                    for q in range(KC):
                        ins = pe.matmul(self.bank(u)[:, half * 512:(half + 1) * 512], self.xT[:, u, q, :],
                                        self.w[:, q, half * 512:(half + 1) * 512], start=q == 0, stop=q == KC - 1)
                ins.then_inc(self.projected, 1)
                if running(g, j, 2):
                    dots(n - 2, (j - 2) % GT % 2)
        loop(pe, NG, group)
        dots(NT - 2, (GT - 2) % 2)
        dots(NT - 1, (GT - 1) % 2)
        pe.wait_ge(self.sums_ready, 1)
        for m in range(self.PAIRS):
            ins = pe.matmul(self.banks[:, m * C:(m + 1) * C], self.sums[:, m, :], self.wo[:, m, :], start=True, stop=True)
        ins.then_inc(self.inner_psum, 1)
        pe.wait_ge(self.inner_ready, 1)
        for m in range(KC):
            for c in range(self.PAIRS):
                ins = pe.matmul(dots2d[:, m * C:(m + 1) * C], self.wq[:, c, m * P:(m + 1) * P], self.inner[:, c, :],
                                start=c == 0, stop=c == self.PAIRS - 1)
        ins.then_inc(self.whole_psum, 1)
        pe.wait_ge(self.whole_ready, 1)

        def apply(g):
            for j in range(GT):
                n, u = g * GT + j, j % 2
                pe.wait_ge(self.xT_ready, NT + n + 1)
                after(pe, self.done, n - BEHIND[j] + 1)
                pe.matmul(self.bank(u)[:, 0:C], self.k.ones[0:1, :], self.bias[:, :], start=True, stop=False)
                for c in range(KC):
                    ins = pe.matmul(self.bank(u)[:, 0:C], self.xT[:, u, c, :], self.whole[:, c, :], start=False, stop=c == KC - 1)
                ins.then_inc(self.applied, 1)
        loop(pe, NG, apply)


def edge_odds(nc, k, a, H, es_table, ed, src_scores, src_most, mixing):
    stage = f"odds{H}"
    NBG = EJ // GB
    with ExitStack() as ctx:
        sb, ps, sem = scope(nc, ctx, stage)
        t, s = Core(), Core()
        t.hot = sb("hot", [P, DEEP, BATCH, P], BF16)
        t.hotT = sb("hotT", [P, 2, BATCH, P], BF16)
        t.p_hotT = ps("p_hotT", [P, 1024], BF16)[:, 0:BATCH * P].rearrange("p (m n) -> p m n", m=BATCH)
        ident = sb("ident", [P, P], BF16)
        ed_parts = sb("ed_parts", [P, 3, NT, H], BF16)
        ed_rest = sb("ed_rest", [P, 2, NT, H])
        split = sem("split")
        look = [ps(f"look{u}", [P, BATCH, H]) for u in range(2)]
        s.hot_ready, s.hotT_psum, s.hotT_ready, s.looked_up = sem("hot_ready"), sem("hotT_psum"), sem("hotT_ready"), sem("looked_up")
        look_kept = sem("look_kept")
        src = sb("src", [EP, EJ], I32)
        dst = sb("dst", [EP, EJ], I32)
        index = sb("index", [EP, 2, GB], I32)
        got = sb("got", [EP, 2, GB, H])
        es = sb("es", [EP, EJ, H])
        forth_all, back_all = sb("forth", [P, EJ, H]), sb("back", [P, EJ, H])
        forth, back = forth_all[0:EP], back_all[0:EP]
        seg = sb("seg", [EP, EJ])
        enter = sb("enter", [EP, EJ])
        leave = sb("leave", [EP, EJ])
        other = sb("other", [EP, 2, EJ])
        NCOL = 2 + 2 * H
        diag_all = sb("diag", [P, NCOL, P])
        diag = diag_all[0:EP]
        lines = sb("lines", [EP, NCOL, P])
        barred = sb("barred", [EP, 2, 2, P])
        both = sb("both", [P, 2 * 2 * H1 * P])
        parts = both[0:EP, 0:2 * 2 * H * P].rearrange("p (a b h n) -> p a b h n", a=2, b=2, h=H)
        ends = sb("ends", [EP, 2, 2, H])
        end = sb("end", [EP, 2, H])
        work = sb("work", [P, 2 * BLK * EW * H1])
        rows = work[0:PB, 0:2 * BLK * EW * H].rearrange("p (a b n) -> p a b n", a=2, b=BLK)
        rest = sb("rest", [1, (EROWS * EW - EDGES) * H])
        looked = sb("looked", [P, NP * SUB, H])
        score = sb("score", [P, 2, NP * SUB, H])
        banks = ps("banks", [P, 4 * 512])
        pL = banks[:, 0:NCOL * P].rearrange("p (n m) -> p n m", n=NCOL)
        pR = banks[:, 3 * 512:4 * 512].rearrange("p (n m) -> p n m", n=BLK * SUB)
        dots = ps("dots", [P, 4, P])
        edges_in, fence, index_ready = sem("edges_in"), sem("fence"), sem("index_ready")
        rows_in, taken = [sem("rows_in0"), sem("rows_in1")], [sem("taken0"), sem("taken1")]
        step, diag_ready, lines_psum, most_ready = sem("step"), sem("diag_ready"), sem("lines_psum"), sem("most_ready")
        stored, rest_set, pair_rows, last = sem("stored"), sem("rest_set"), sem("pair_rows"), sem("last")
        turned, kept, cleared, less = sem("turned"), sem("kept"), sem("cleared"), sem("less")
        mix = SecondMixing(k, sb, sem, banks, dots, work, both, (forth_all, back_all), diag_all) if mixing else None

        with nc.Block() as block:
            @block.sync
            def _(sp):
                sp.dma_start(src[:, :], a["src"].rearrange("(p j) -> p j", p=EP)).then_inc(edges_in, 16)
                sp.dma_start(dst[:, :], a["dst"].rearrange("(p j) -> p j", p=EP)).then_inc(edges_in, 16)

                if mixing:
                    mix.load(sp, a)

                def steps(i):
                    for u in range(2):
                        sp.wait_ge(rows_in[u], 16 * GB * (i + 1))
                        sp.dma_start(es[:, bass.ds((2 * i + u) * GB, GB), :], got[:, u, :, :]).then_inc(taken[u], 16)
                loop(sp, NBG // 2, steps)
                sp.wait_ge(rest_set, 1)
                for n, (table, values) in enumerate(((src_scores, es), (src_most, forth))):
                    flat = table.rearrange("a b -> (a b)")
                    if n == 0:
                        for u in range(2):
                            sp.wait_ge(taken[u], 16 * NBG // 2)
                    else:
                        sp.wait_ge(most_ready, 1)
                    sp.dma_start(flat[0:EDGES * H].rearrange("(p j) -> p j", p=EP),
                                 values.rearrange("p j h -> p (j h)")).then_inc(stored, 16)
                    sp.dma_start(flat[EDGES * H:EROWS * EW * H].rearrange("(p j) -> p j", p=1), rest[:, :]).then_inc(stored, 16)
                sp.wait_ge(stored, 64)

            @block.gpsimd
            def _(pool):
                pool.memset(rest[:, :], 0.0).then_inc(rest_set, 1)
                pool.memset(k.sums[:, :, :], 0.0).then_inc(cleared, 1)
                pool.wait_ge(edges_in, 32)

                def steps(i):
                    for u in range(2):
                        b = 2 * i + u
                        after(pool, taken[u], 16 * i)
                        pool.sem_inc(fence, 1)
                        pool.tensor_copy(index[:, u, :], src[:, bass.ds(b * GB, GB)]).then_inc(index_ready, 1)
                        pool.wait_ge(index_ready, b + 1)
                        pool.sem_inc(fence, 1)
                        for m in range(GB):
                            pool.indirect_dma_start(got[:, u, m, :], None, es_table,
                                                    bass.IndirectOffsetOnAxis(ap=index[:, u, m:m + 1], axis=0)).then_inc(rows_in[u], 16)
                loop(pool, NBG // 2, steps)
                pool.wait_ge(stored, 64)
                for n, table in enumerate((src_scores, src_most)):
                    for b in range(BLK):
                        pool.indirect_dma_start(rows[:, n, b, :], None, table,
                                                bass.IndirectOffsetOnAxis(ap=k.tile_i[:, b:b + 1], axis=0)).then_inc(pair_rows, 16)

            @block.vector
            def _(dv):
                dv.tensor_copy(ident[:, :], k.ident[:, :]).then_inc(split, 1)
                part = Chain(dv, split, 6)
                part.turn(0)
                part.left -= 1
                rest = ed[:, :, 0:H]
                for n in range(3):
                    part(dv.tensor_copy(ed_parts[:, n, :, :], rest))
                    if n < 2:
                        part(dv.tensor_tensor(ed_rest[:, n, :, :], rest, ed_parts[:, n, :, :], ALU.subtract))
                        rest = ed_rest[:, n, :, :]
                edge_hot(dv, 0, 0, k, t, s, s.hotT_psum)
                edge_loop(dv, lambda b, u, i, windows: edge_hot(dv, b + 1, u + 1, k, t, s, s.hotT_psum))
                if mixing:
                    mix.vector(dv)
                chain = Chain(dv, step, 20)
                chain.turn(0)
                dv.wait_ge(edges_in, 32)
                chain(dv.tensor_copy(seg[:, :], dst[:, :]))
                chain(dv.tensor_tensor(leave[:, 0:EJ - 1], seg[:, 0:EJ - 1], seg[:, 1:EJ], ALU.is_equal))
                chain(dv.tensor_scalar(leave[:, 0:EJ - 1], leave[:, 0:EJ - 1], 1.0, BIG, ALU.subtract, ALU.mult))
                chain(dv.memset(leave[:, EJ - 1:EJ], -BIG))
                chain(dv.tensor_copy(enter[:, 1:EJ], leave[:, 0:EJ - 1]))
                chain(dv.memset(enter[:, 0:1], -BIG))
                for end_of in range(2):
                    at = (EJ - 1) * end_of
                    chain(dv.tensor_scalar(other[:, end_of, :], seg[:, :], seg[:, at:at + 1], 1.0, ALU.is_equal, ALU.subtract))
                chain(dv.tensor_scalar(other[:, :, :], other[:, :, :], BIG, None, ALU.mult))
                for u in range(2):
                    dv.wait_ge(taken[u], 16 * NBG // 2)
                for h in range(H):
                    dv.tensor_tensor_scan(forth[:, :, h], enter[:, :], es[:, :, h], -BIG, ALU.add, ALU.max)
                    ins = dv.tensor_tensor_scan(backwards(back[:, :, h]), backwards(leave[:, :]), backwards(es[:, :, h]), -BIG,
                                                ALU.add, ALU.max)
                chain(ins)
                columns = [seg[:, 0:1], seg[:, EJ - 1:EJ]] + [back[:, 0, h:h + 1] for h in range(H)] + \
                    [forth[:, EJ - 1, h:h + 1] for h in range(H)]
                for n, column in enumerate(columns):
                    ins = dv.tensor_scalar(diag[:, n, :], k.ident[0:EP, :], column, None, ALU.mult)
                ins.then_inc(diag_ready, 1)
                dv.wait_ge(lines_psum, 1)
                chain(dv.tensor_tensor(forth[:, :, :], forth[:, :, :], back[:, :, :], ALU.max))
                chain(dv.tensor_copy(lines[:, :, :], pL[0:EP, :, :]))
                for end_of in range(2):
                    at = (EJ - 1) * end_of
                    ins = dv.tensor_scalar(barred[:, end_of, :, 0:EP], lines[:, 0:2, 0:EP], seg[:, at:at + 1], 1.0, ALU.is_equal, ALU.subtract)
                chain(ins)
                chain(dv.tensor_scalar(barred[:, :, :, 0:EP], barred[:, :, :, 0:EP], BIG, None, ALU.mult))
                for end_of in range(2):
                    ins = dv.tensor_tensor(parts[:, end_of, :, :, 0:EP], spread(barred[:, end_of, :, 0:EP], 2, H),
                                           lines[:, 2:NCOL, 0:EP].rearrange("p (w h) n -> p w h n", w=2), ALU.add)
                chain(ins)
                for end_of in range(2):
                    ins = dv.tensor_reduce(ends[:, end_of, :, :], parts[:, end_of, :, :, 0:EP], AX, ALU.max)
                chain(ins)
                chain(dv.tensor_tensor(end[:, :, :], ends[:, :, 0, :], ends[:, :, 1, :], ALU.max))
                for end_of in range(2):
                    chain(dv.tensor_tensor(back[:, :, :], spread(other[:, end_of, :], 2, H), spread(end[:, end_of, :], 1, EJ), ALU.add))
                    if end_of == 0:
                        chain(dv.tensor_tensor(forth[:, :, :], forth[:, :, :], back[:, :, :], ALU.max))
                dv.tensor_tensor(forth[:, :, :], forth[:, :, :], back[:, :, :], ALU.max).then_inc(most_ready, 1)
                assert chain.left == 0, chain.left
                for n in range(2 * H):
                    dv.wait_ge(turned, n + 1)
                    dv.tensor_copy(score[:, n // H, :, n % H].rearrange("p (b i s) -> p b s i", b=BLK, s=SUB),
                                   pR.rearrange("p (b s) n -> p b s n", b=BLK)[:, :, :, 0:PB]).then_inc(kept, 1)
                dv.wait_ge(kept, 2 * H)
                dv.wait_ge(look_kept, NB)
                final = Chain(dv, last, 2)
                final.turn(0)
                final(dv.tensor_tensor(score[:, :, :, :], score[:, :, :, :], spread(looked[:, :, :], 1, 2), ALU.add))
                final(dv.scalar_tensor_tensor(out=score[:, :, :, :], in0=score[:, :, :, :], scalar=0.01, in1=score[:, :, :, :],
                                              op0=ALU.mult, op1=ALU.max))
                dv.tensor_tensor(score[:, 0, :, :], score[:, 0, :, :], score[:, 1, :, :], ALU.subtract).then_inc(less, 1)

            @block.scalar
            def _(ac):
                edge_keep(ac, 0, 0, t, s)

                def slot(b, u, i, windows):
                    edge_keep(ac, b + 1, u + 1, t, s)
                    ac.wait_ge(s.looked_up, b + 1)
                    ac.copy(looked[:, bass.ds(b * BATCH, BATCH), :], look[u % 2][:, :, :]).then_inc(look_kept, 1)
                edge_loop(ac, slot)
                if mixing:
                    mix.scalar(ac)
                ac.wait_ge(less, 1)
                ac.activation(k.odds[:, :, 0:H], score[:, 0, :, :], ACT.Exp).then_inc(last, 1)

            @block.tensor
            def _(pe):
                pe.wait_ge(split, 6)
                edge_turn(pe, 0, 0, ident, t, s)

                def slot(b, u, i, windows):
                    edge_turn(pe, b + 1, u + 1, ident, t, s)
                    pe.wait_ge(s.hotT_ready, b + 1)
                    after(pe, look_kept, b - 1)
                    for m in range(BATCH):
                        for n in range(2, -1, -1):
                            ins = pe.matmul(look[u % 2][:, m, :], t.hotT[:, u % 2, m, :], ed_parts[:, n, bass.ds(windows[m // SUB], 1), :],
                                            start=n == 2, stop=n == 0)
                    ins.then_inc(s.looked_up, 1)
                edge_loop(pe, slot, k, 0)
                if mixing:
                    mix.tensor(pe)
                pe.wait_ge(diag_ready, 1)
                for n in range(NCOL):
                    ins = pe.matmul(pL[:, n, :], k.ones[0:EP, :], diag[:, n, :], start=True, stop=True)
                ins.then_inc(lines_psum, 1)
                pe.wait_ge(pair_rows, 32 * BLK)
                for n in range(2 * H):
                    after(pe, kept, n)
                    for b in range(BLK):
                        for m in range(SUB):
                            lanes = rows[:, n // H, b, m * P * H:(m + 1) * P * H].rearrange("p (n h) -> p n h", h=H)
                            ins = pe.transpose(pR[:, b * SUB + m, 0:PB], lanes[:, :, n % H], k.ident[0:PB, 0:PB])
                    ins.then_inc(turned, 1)


def backwards(ap):
    (partitions, lanes), (stride, n) = [list(x) for x in ap.ap]
    return bass.AP(tensor=ap.tensor, offset=ap.offset + (n - 1) * stride, ap=[[partitions, lanes], [-stride, n]])


def edge_sums(nc, k, H, table):
    W = C + H
    with ExitStack() as ctx:
        sb, ps, sem = scope(nc, ctx, f"sums{H}")
        t, s = Core(), Core()
        t.index = sb("index", [P, 2, DEEP * BATCH], I32)
        t.rows = sb("rows", [P, DEEP, BATCH, C])
        t.hot = sb("hot", [P, DEEP, BATCH, P])
        t.weighted = sb("weighted", [P, 2, BATCH, SW])
        t.p_sum = ps("p_sum", [P, 2 * BP, 512])
        s.fence, s.index_ready, s.hot_ready, s.weights_ready = sem("fence"), sem("index_ready"), sem("hot_ready"), sem("weights_ready")
        s.weighted_ready, s.summed, s.added = sem("weighted_ready"), sem("summed"), sem("added")
        s.rows_in = [sem(f"rows_in{u}") for u in range(DEEP)]

        with nc.Block() as block:
            @block.gpsimd
            def _(pool):
                edge_gather(pool, k, t, s, table, s.weighted_ready)

            @block.tensor
            def _(pe):
                def slot(b, u, i, windows):
                    pe.wait_ge(s.weights_ready, b + 1)
                    edge_sum(pe, b, u, t, s, W)
                edge_loop(pe, slot)

            @block.scalar
            def _(ac):
                def slot(b, u, i, windows):
                    after(ac, s.summed, b - 1)
                    ac.copy(t.weighted[:, u % 2, :, C:W], k.odds[:, bass.ds(b * BATCH, BATCH), 0:H]).then_inc(s.weights_ready, 1)
                edge_loop(ac, slot)

            @block.vector
            def _(dv):
                edge_hot(dv, 0, 0, k, t, s, s.summed)

                def slot(b, u, i, windows):
                    edge_hot(dv, b + 1, u + 1, k, t, s, s.summed)
                    dv.wait_ge(s.rows_in[u], (i + 1) * 16 * BATCH)
                    after(dv, s.summed, b - 1)
                    dv.tensor_tensor(t.weighted[:, u % 2, :, 0:C].rearrange("p m (h d) -> p m h d", h=H),
                                     t.rows[:, u, :, :].rearrange("p m (h d) -> p m h d", h=H),
                                     spread(k.odds[:, bass.ds(b * BATCH, BATCH), 0:H], 3, C // H), ALU.mult).then_inc(s.weighted_ready, 1)
                    if real(b, 1):
                        edge_add(dv, b - 1, u + 3, windows, k, t, s, W)
                edge_loop(dv, slot, k, -1)
                edge_add(dv, NB - 1, DEEP - 1, windows_of(dv, k, NB - 1), k, t, s, W)


def between_second(nc, k, a):
    ZW = C + 2
    with ExitStack() as ctx:
        sb, ps, sem = scope(nc, ctx, "between")
        w = sb("w", [P, KC, ZW])
        natural = sb("natural", [P, KC, C])
        vectors = sb("vectors", [P, KC, 2])
        den = sb("den", [P, GT, H1])
        mean = sb("mean", [P, GT, C])
        below = sb("below", [P, GT, C])
        grown = sb("grown", [P, GT, C])
        hidden = sb("hidden", [P, GT, C])
        hT = sb("hT", [P, GT, KC, P])
        outs = sb("outs", [P, 2, ZW])
        pT = [ps(f"pT{i}", [P, KC, P]) for i in range(2)]
        pM = [ps(f"pM{i}", [P, ZW]) for i in range(2)]
        loaded, folded, fold_kept, small = sem("loaded"), sem("folded"), sem("fold_kept"), sem("small")
        mean_ready, below_ready, grown_ready, above_ready = sem("mean_ready"), sem("below_ready"), sem("grown_ready"), sem("above_ready")
        hidden_ready, turned, kept, projected, z_ready = sem("hidden_ready"), sem("turned"), sem("kept"), sem("projected"), sem("z_ready")
        stored = [sem("stored0"), sem("stored1")]

        with nc.Block() as block:
            @block.sync
            def _(sp):
                for n in range(KC):
                    rows = slice(n * P, (n + 1) * P)
                    sp.dma_start(w[:, n, 0:C], a["w_z2"][rows, :]).then_inc(loaded, 16)
                    sp.dma_start(natural[:, n, :], a["w_natural2"][rows, :]).then_inc(loaded, 16)
                    sp.dma_start(vectors[:, n, :], a["vectors2"][rows, :], allow_slow_non_contiguous=True).then_inc(loaded, 16)

                def group(g):
                    for j in range(GT):
                        n, u = g * GT + j, j % 2
                        sp.wait_ge(z_ready, n + 1)
                        rows = bass.ds(n * P, P)
                        sp.dma_start(k.z_table[rows, :], outs[:, u, 0:C]).then_inc(stored[u], 16)
                        sp.dma_start(k.es_table2[rows, :], outs[:, u, C:C + 1]).then_inc(stored[u], 16)
                loop(sp, NG, group)
                for u in range(2):
                    sp.wait_ge(stored[u], 32 * USES[u] * NG)

            @block.vector
            def _(dv):
                dv.wait_ge(folded, 1)
                dv.tensor_copy(w[:, :, C:ZW], pT[0][:, :, 0:2]).then_inc(fold_kept, 1)

                def begin(g):
                    sums = k.sums[:, bass.ds(g * GT, GT), :]
                    dv.tensor_scalar(den[:, :, :], sums[:, :, C:C + H1], 1e-30, None, ALU.max).then_inc(small, 1)
                    dv.wait_ge(small, 2 * g + 1)
                    dv.reciprocal(den[:, :, :], den[:, :, :]).then_inc(small, 1)
                    dv.wait_ge(small, 2 * g + 2)
                    dv.tensor_tensor(mean[:, :, :].rearrange("p t (h d) -> p t h d", h=H1),
                                     sums[:, :, 0:C].rearrange("p t (h d) -> p t h d", h=H1),
                                     spread(den[:, :, :], 3, D1), ALU.mult).then_inc(mean_ready, 1)
                    dv.wait_ge(mean_ready, g + 1)
                    dv.tensor_scalar(below[:, :, :], mean[:, :, :], 0.0, None, ALU.min).then_inc(below_ready, 1)
                    dv.tensor_scalar(mean[:, :, :], mean[:, :, :], 0.0, None, ALU.max).then_inc(above_ready, 1)

                def finish(g):
                    dv.wait_ge(above_ready, g + 1)
                    dv.wait_ge(grown_ready, g + 1)
                    after(dv, turned, GT * g)
                    dv.scalar_tensor_tensor(out=hidden[:, :, :], in0=grown[:, :, :], scalar=-1.0, in1=mean[:, :, :],
                                            op0=ALU.add, op1=ALU.add).then_inc(hidden_ready, 1)

                def group(g, last=False):
                    for j in range(GT):
                        n, u = g * GT + j, j % 2
                        dv.wait_ge(projected, n + 1)
                        after(dv, stored[u], 32 * uses(g, j))
                        dv.tensor_copy(k.ed[:, bass.ds(n, 1), 0:1], pM[u][:, C + 1:ZW].unsqueeze(1))
                        dv.tensor_copy(outs[:, u, :], pM[u][:, :]).then_inc(z_ready, 1)
                        if j == 0 and not last:
                            dv.wait_ge(hidden_ready, g + 1)
                            begin(g + 1)
                        if j == 3 and not last:
                            finish(g + 1)
                begin(0)
                finish(0)
                loop(dv, NG - 1, group)
                group(NG - 1, True)

            @block.scalar
            def _(ac):
                ac.wait_ge(fold_kept, 1)

                def grow(g):
                    ac.wait_ge(below_ready, g + 1)
                    after(ac, hidden_ready, g)
                    ac.activation(grown[:, :, :], below[:, :, :], ACT.Exp).then_inc(grown_ready, 1)

                def group(g, last=False):
                    for j in range(GT):
                        n, u = g * GT + j, j % 2
                        ac.wait_ge(turned, n + 1)
                        after(ac, projected, n - GT + 1)
                        ac.copy(hT[:, j, :, :], pT[u][:, :, :]).then_inc(kept, 1)
                    if not last:
                        grow(g + 1)
                grow(0)
                loop(ac, NG - 1, group)
                group(NG - 1, True)

            @block.tensor
            def _(pe):
                pe.wait_ge(loaded, 96)
                for m in range(KC):
                    for c in range(KC):
                        ins = pe.matmul(pT[0][:, m, 0:2], natural[:, c, m * P:(m + 1) * P], vectors[:, c, :],
                                        start=c == 0, stop=c == KC - 1)
                ins.then_inc(folded, 1)
                pe.wait_ge(fold_kept, 1)

                def group(g):
                    pe.wait_ge(hidden_ready, g + 1)
                    for j in range(GT):
                        n, u = g * GT + j, j % 2
                        after(pe, kept, n - BEHIND[j] + 1)
                        for c in range(KC):
                            ins = pe.transpose(pT[u][:, c, :], hidden[:, j, c * P:(c + 1) * P], k.ident[:, :])
                        ins.then_inc(turned, 1)
                    for j in range(GT):
                        n, u = g * GT + j, j % 2
                        pe.wait_ge(kept, n + 1)
                        after(pe, z_ready, n - BEHIND[j] + 1)
                        for c in range(KC):
                            ins = pe.matmul(pM[u][:, :], hT[:, j, c, :], w[:, c, :], start=c == 0, stop=c == KC - 1)
                        ins.then_inc(projected, 1)
                loop(pe, NG, group)


def end_second(nc, k):
    with ExitStack() as ctx:
        sb, ps, sem = scope(nc, ctx, "end_second")
        den = sb("den", [P, NT, 1])
        step = sem("step")
        with nc.Block() as block:
            @block.vector
            def _(dv):
                chain = Chain(dv, step, 4)
                chain.turn(0)
                chain(dv.tensor_scalar(den[:, :, :], k.sums[:, :, C:C + 1], 1e-30, None, ALU.max))
                chain(dv.reciprocal(den[:, :, :], den[:, :, :]))
                chain(dv.tensor_tensor(k.sums[:, :, 0:C], k.sums[:, :, 0:C], spread(den[:, :, 0], 2, C), ALU.mult))
                chain(dv.tensor_tensor(k.x[:, :, :], k.x[:, :, :], k.sums[:, :, 0:C], ALU.add))


NS = 2 * NT + NE
NSX = NS + 2


def route(nc, k, a):
    with ExitStack() as ctx:
        sb, ps, sem = scope(nc, ctx, "route")
        t, s = norm_tensors(sb, sem)
        t2, s2 = norm_tensors(sb, sem, "_again")
        wr = sb("wr", [P, KC, NE])
        br = sb("br", [P, NE])
        gain, shift = sb("gain", [P, KC]), sb("shift", [P, KC])
        zeros = sb("zeros", [P, C])
        hT = sb("hT", [P, KC, GN])
        all_rows = sb("all_rows", [P, NT, C])
        logits = sb("logits", [P, NT, NE])
        found = sb("found", [P, NT, NE])
        one = [sb(f"one{n}", [P, NT, NE]) for n in range(2)]
        best = sb("best", [P, 2, NT])
        where = sb("where", [P, NT])
        less = sb("less", [P, NT])
        odds = sb("odds", [P, NT])
        total = sb("total", [P, NT])
        place = sb("place", [P, NE])
        before = sb("before", [P, P])
        taken = sb("taken", [P, NT, NE])
        within = sb("within", [P, NT, NE])
        tile_sum = sb("tile_sum", [P, NT, NE])
        upto = sb("upto", [P, NT, NE])
        spare = sb("spare", [P, NE], I32)
        tiles = sb("tiles", [P, NE])
        start = sb("start", [P, NE])
        slot_f = sb("slot_f", [P, 2, NT])
        slotno = sb("slotno", [1, NSX])
        begun = sb("begun", [1, NSX, NE])
        expert_f = sb("expert_f", [1, NSX])
        pT = [ps(f"pT{i}", [P, KC, P]) for i in range(2)]
        pS = ps("pS", [P, GT * NE])
        pW = [ps(f"pW{i}", [P, NT * NE]) for i in range(2)]
        loaded, zeroed, blank, consts = sem("loaded"), sem("zeroed"), sem("blank"), sem("consts")
        turned, kept, multiplied, added, rows_kept = sem("turned"), sem("kept"), sem("multiplied"), sem("added"), sem("rows_kept")
        small, less_ready, odds_ready, taken_ready, counted = sem("small"), sem("less_ready"), sem("odds_ready"), sem("taken_ready"), sem("counted")
        slots_ready, scattered = sem("slots_ready"), sem("scattered")

        with nc.Block() as block:
            @block.sync
            def _(sp):
                sp.dma_start(wr[:, :, :], a["w_r2"].rearrange("(c p) n -> p c n", p=P)).then_inc(loaded, 16)
                sp.dma_start(br[:, :], a["b_r2"].partition_broadcast(P)).then_inc(loaded, 16)
                sp.dma_start(gain[:, :], a["gamma"]).then_inc(loaded, 16)
                sp.dma_start(shift[:, :], a["beta"]).then_inc(loaded, 16)
                for e in range(NE):
                    sp.dma_start(k.w1[:, e * KC:(e + 1) * KC, :], a["w_hidden2"][e].rearrange("(c p) n -> p c n", p=P)).then_inc(k.weights_in, 16)
                    sp.dma_start(k.w2[:, e * 2 * KC:(e + 1) * 2 * KC, :], a["w_out2"][e].rearrange("(c p) n -> p c n", p=P)).then_inc(k.weights_in, 16)
                    sp.dma_start(k.b1[:, e, :], a["b_h2"][e:e + 1, :].partition_broadcast(P)).then_inc(k.weights_in, 16)
                    sp.dma_start(k.b2[:, e, :], a["b_o2"][e:e + 1, :].partition_broadcast(P)).then_inc(k.weights_in, 16)
                sp.wait_ge(zeroed, 1)

                def clear(i):
                    sp.dma_start(k.slots[bass.ds(i * P, P), :], zeros[:, :]).then_inc(blank, 16)
                loop(sp, NSX, clear)
                sp.wait_ge(blank, 16 * NSX)

            @block.gpsimd
            def _(pool):
                pool.memset(zeros[:, :], 0.0).then_inc(zeroed, 1)
                pool.iota(place[:, :], [[1, NE]], base=0, channel_multiplier=0,
                          allow_small_or_imprecise_dtypes=True).then_inc(consts, 1)
                pool.iota(slotno[:, :], [[1, NSX]], base=0, channel_multiplier=0,
                          allow_small_or_imprecise_dtypes=True).then_inc(consts, 1)
                pool.affine_select(out=before[:, :], in_=k.ones[:, :], compare_op=ALU.is_gt, fill=0.0, base=0,
                                   pattern=[[1, P]], channel_multiplier=-1).then_inc(consts, 1)

                def group(g):
                    deviations(pool, g, k, s, t)
                    deviations(pool, g, k, s2, t2)
                loop(pool, NG, group)
                pool.wait_ge(blank, 16 * NSX)
                pool.wait_ge(slots_ready, 1)
                pool.wait_ge(rows_kept, NG)
                for i in range(NT):
                    for n in range(2):
                        at = n * NT + i
                        pool.indirect_dma_start(k.slots, bass.IndirectOffsetOnAxis(ap=k.slot[:, at:at + 1], axis=0),
                                                all_rows[:, i, :], None).then_inc(scattered, 16)
                pool.wait_ge(scattered, 32 * NT)

            @block.vector
            def _(dv):
                dv.wait_ge(loaded, 64)
                dv.wait_ge(consts, 3)

                def add_bias(g):
                    dv.wait_ge(multiplied, g + 1)
                    dv.tensor_tensor(logits[:, bass.ds(g * GT, GT), :], pS.rearrange("p (t e) -> p t e", t=GT),
                                     spread(br[:, :], 1, GT), ALU.add).then_inc(added, 1)

                def group(g):
                    normalise(dv, g, lambda g, j: k.x[:, bass.ds(g * GT + j, 1), :], s, t)
                    if real(g, 1):
                        add_bias(g - 1)
                    after(dv, turned, GT * g)
                    after(dv, rows_kept, g)
                    dv.wait_ge(s.normed_ready, g * GT + GT)
                    normalise(dv, g, lambda g, j: t.normed[:, j, :], s2, t2)
                loop(dv, NG, group)
                add_bias(NG - 1)
                dv.wait_ge(added, NG)

                chain = Chain(dv, small, 35)
                chain.turn(0)
                places = spread(place[:, :], 1, NT)
                for n in range(2):
                    chain(dv.tensor_reduce(best[:, n, :], logits[:, :, :], AX, ALU.max))
                    chain(dv.tensor_tensor(found[:, :, :], logits[:, :, :], spread(best[:, n, :], 2, NE), ALU.is_lt))
                    chain(dv.tensor_scalar(found[:, :, :], found[:, :, :], float(NE), None, ALU.mult))
                    chain(dv.tensor_tensor(found[:, :, :], found[:, :, :], places, ALU.add))
                    chain(dv.tensor_reduce(where[:, :], found[:, :, :], AX, ALU.min))
                    chain(dv.tensor_tensor(one[n][:, :, :], places, spread(where[:, :], 2, NE), ALU.is_equal))
                    if n == 0:
                        chain(dv.scalar_tensor_tensor(out=logits[:, :, :], in0=one[0][:, :, :], scalar=-BIG, in1=logits[:, :, :],
                                                      op0=ALU.mult, op1=ALU.add))
                dv.tensor_tensor(less[:, :], best[:, 1, :], best[:, 0, :], ALU.subtract).then_inc(less_ready, 1)
                dv.tensor_tensor(taken[:, :, :], one[0][:, :, :], one[1][:, :, :], ALU.add).then_inc(taken_ready, 1)
                dv.wait_ge(odds_ready, 1)
                chain(dv.tensor_scalar(total[:, :], odds[:, :], 1.0, None, ALU.add))
                chain(dv.reciprocal(k.gates[:, 0, :], total[:, :]))
                chain(dv.tensor_tensor(k.gates[:, 1, :], odds[:, :], k.gates[:, 0, :], ALU.mult))
                dv.wait_ge(counted, 2)
                dv.tensor_copy(within[:, :, :], pW[0].rearrange("p (t e) -> p t e", t=NT))
                chain(dv.tensor_copy(tile_sum[:, :, :], pW[1].rearrange("p (t e) -> p t e", t=NT)))
                for e in range(NE):
                    ins = dv.tensor_tensor_scan(upto[:, :, e], k.ones[:, 0:NT], tile_sum[:, :, e], 0.0, ALU.mult, ALU.add)
                chain(ins)
                chain(dv.tensor_scalar(spare[:, :], upto[:, NT - 1, :], float(P - 1), None, ALU.add))
                chain(dv.tensor_scalar(spare[:, :], spare[:, :], 7, None, ALU.arith_shift_right))
                chain(dv.tensor_copy(tiles[:, :], spare[:, :]))
                chain(dv.tensor_tensor_scan(start[:, :], k.ones[:, 0:NE], tiles[:, :], 0.0, ALU.mult, ALU.add))
                chain(dv.tensor_tensor(start[:, :], start[:, :], tiles[:, :], ALU.subtract))
                chain(dv.tensor_tensor(begun[:, :, :], spread(slotno[:, :], 2, NE), spread(start[0:1, :], 1, NSX), ALU.is_ge))
                chain(dv.tensor_reduce(expert_f[:, :], begun[:, :, :], AX, ALU.add))
                chain(dv.tensor_scalar(k.expert[:, :], expert_f[:, :], -1.0, None, ALU.add))
                chain(dv.tensor_tensor(upto[:, :, :], upto[:, :, :], tile_sum[:, :, :], ALU.subtract))
                chain(dv.tensor_tensor(upto[:, :, :], upto[:, :, :], within[:, :, :], ALU.add))
                chain(dv.tensor_scalar(start[:, :], start[:, :], float(P), None, ALU.mult))
                chain(dv.tensor_tensor(upto[:, :, :], upto[:, :, :], spread(start[:, :], 1, NT), ALU.add))
                for n in range(2):
                    chain(dv.tensor_tensor(found[:, :, :], upto[:, :, :], one[n][:, :, :], ALU.mult))
                    chain(dv.tensor_reduce(slot_f[:, n, :], found[:, :, :], AX, ALU.add))
                chain(dv.tensor_copy(k.slot[:, :], slot_f.rearrange("p n t -> p (n t)")))
                dv.sem_inc(slots_ready, 1)
                assert chain.left == 0, chain.left

            @block.scalar
            def _(ac):
                ac.wait_ge(loaded, 64)

                def group(g):
                    for j in range(GT):
                        ac.wait_ge(turned, GT * g + j + 1)
                        after(ac, multiplied, g)
                        for c in range(KC):
                            ins = ac.activation(hT[:, c, j * P:(j + 1) * P], pT[j % 2][:, c, :], ACT.Identity,
                                                bias=shift[:, c:c + 1], scale=gain[:, c:c + 1])
                        ins.then_inc(kept, 1)
                    ac.copy(all_rows[:, bass.ds(g * GT, GT), :], t2.normed[:, :, :]).then_inc(rows_kept, 1)
                loop(ac, NG, group)
                ac.wait_ge(less_ready, 1)
                ac.activation(odds[:, :], less[:, :], ACT.Exp).then_inc(odds_ready, 1)

            @block.tensor
            def _(pe):
                pe.wait_ge(loaded, 64)

                def group(g):
                    for j in range(GT):
                        pe.wait_ge(s2.normed_ready, g * GT + j + 1)
                        after(pe, kept, GT * g + j - 1)
                        for c in range(KC):
                            ins = pe.transpose(pT[j % 2][:, c, :], t2.normed[:, j, c * P:(c + 1) * P], k.ident[:, :])
                        ins.then_inc(turned, 1)
                    pe.wait_ge(kept, GT * g + GT)
                    after(pe, added, g)
                    for j in range(GT):
                        for c in range(KC):
                            ins = pe.matmul(pS[:, j * NE:(j + 1) * NE], hT[:, c, j * P:(j + 1) * P], wr[:, c, :],
                                            start=c == 0, stop=c == KC - 1)
                    ins.then_inc(multiplied, 1)
                loop(pe, NG, group)
                pe.wait_ge(consts, 3)
                pe.wait_ge(taken_ready, 1)
                for n, ones in enumerate((before, k.ones)):
                    pe.matmul(pW[n][:, :], ones[:, :], taken.rearrange("p t e -> p (t e)"), start=True, stop=True).then_inc(counted, 1)


def slot_experts(nc, k, a):
    HID = 2 * C
    MC = HID // P
    with ExitStack() as ctx:
        sb, ps, sem = scope(nc, ctx, "slot_experts")
        w1, w2, b1, b2 = k.w1, k.w2, k.b1, k.b2
        gain, shift = sb("gain", [P, KC]), sb("shift", [P, KC])
        rows = sb("rows", [P, 2, C])
        xT = sb("xT", [P, 2, KC, P])
        biased = sb("biased", [P, 2, HID])
        hid = sb("hid", [P, 2, HID])
        hT = sb("hT", [P, 2, MC, P])
        y = sb("y", [P, 2, C])
        pT = ps("pT", [P, KC, P])
        pH = [ps(f"pH{u}", [P, HID]) for u in range(2)]
        pR = [ps(f"pR{u}", [P, MC, P]) for u in range(2)]
        pO = [ps(f"pO{u}", [P, C]) for u in range(2)]
        small_in, rows_in = sem("small_in"), [sem("rows_in0"), sem("rows_in1")]
        x_turned, x_ready, hidden_psum, biased_ready = sem("x_turned"), sem("x_ready"), sem("hidden_psum"), sem("biased_ready")
        hidden_ready, h_turned, hT_ready, projected, y_ready = sem("hidden_ready"), sem("h_turned"), sem("hT_ready"), sem("projected"), sem("y_ready")
        stored = [sem("stored0"), sem("stored1")]

        def expert_at(eng, i):
            return eng.value_load(k.expert[0:1, bass.ds(i, 1)], min_val=0, max_val=NE - 1)

        def slot_loop(eng, body):
            def steps(i):
                for u in range(2):
                    body(2 * i + u, u, i)
            loop(eng, NS // 2, steps)

        with nc.Block() as block:
            @block.sync
            def _(sp):
                sp.dma_start(gain[:, :], a["gamma"]).then_inc(small_in, 16)
                sp.dma_start(shift[:, :], a["beta"]).then_inc(small_in, 16)
                for u in range(2):
                    sp.dma_start(rows[:, u, :], k.slots[u * P:(u + 1) * P, :]).then_inc(rows_in[u], 16)

                def body(n, u, i):
                    sp.wait_ge(x_turned, n + 1)
                    sp.dma_start(rows[:, u, :], k.slots[bass.ds((n + 2) * P, P), :]).then_inc(rows_in[u], 16)
                    if real(n, 2):
                        sp.wait_ge(y_ready, n - 1)
                        sp.dma_start(k.results[bass.ds((n - 2) * P, P), :], y[:, u, :]).then_inc(stored[u], 16)
                slot_loop(sp, body)
                for n in (NS - 2, NS - 1):
                    sp.wait_ge(y_ready, n + 1)
                    sp.dma_start(k.results[n * P:(n + 1) * P, :], y[:, n % 2, :]).then_inc(stored[n % 2], 16)
                for u in range(2):
                    sp.wait_ge(stored[u], 16 * NS // 2)
                    sp.wait_ge(rows_in[u], 16 * (NS // 2 + 1))

            @block.tensor
            def _(pe):
                def turn(n, u, i):
                    pe.wait_ge(rows_in[u], 16 * (i + 1))
                    after(pe, x_ready, n)
                    for c in range(KC):
                        ins = pe.transpose(pT[:, c, :], rows[:, u, c * P:(c + 1) * P], k.ident[:, :])
                    ins.then_inc(x_turned, 1)

                def hidden(n, u):
                    e = expert_at(pe, n)
                    pe.wait_ge(x_ready, n + 1)
                    after(pe, biased_ready, n - 1)
                    for c in range(KC):
                        ins = pe.matmul(pH[u][:, :], xT[:, u, c, :], w1[:, bass.ds(e * KC + c, 1), :], start=c == 0, stop=c == KC - 1)
                    ins.then_inc(hidden_psum, 1)

                def turn_hidden(n, u):
                    pe.wait_ge(hidden_ready, n + 1)
                    after(pe, hT_ready, n - 1)
                    for m in range(MC):
                        ins = pe.transpose(pR[u][:, m, :], hid[:, u, m * P:(m + 1) * P], k.ident[:, :])
                    ins.then_inc(h_turned, 1)

                def product(n, u):
                    e = expert_at(pe, n)
                    pe.wait_ge(hT_ready, n + 1)
                    after(pe, y_ready, n - 1)
                    for m in range(MC):
                        ins = pe.matmul(pO[u][:, :], hT[:, u, m, :], w2[:, bass.ds(e * MC + m, 1), :], start=m == 0, stop=m == MC - 1)
                    ins.then_inc(projected, 1)

                turn(0, 0, 0)
                turn(1, 1, 0)
                pe.wait_ge(k.weights_in, 64 * NE)
                hidden(0, 0)

                def body(n, u, i):
                    turn(n + 2, u, i + 1)
                    hidden(n + 1, 1 - u)
                    turn_hidden(n, u)
                    if real(n, 1):
                        product(n - 1, 1 - u)
                slot_loop(pe, body)
                product(NS - 1, (NS - 1) % 2)

            @block.scalar
            def _(ac):
                def keep(n, u):
                    ac.wait_ge(x_turned, n + 1)
                    after(ac, hidden_psum, n - 1)
                    for c in range(KC):
                        ins = ac.activation(xT[:, u, c, :], pT[:, c, :], ACT.Identity, bias=shift[:, c:c + 1], scale=gain[:, c:c + 1])
                    ins.then_inc(x_ready, 1)

                ac.wait_ge(small_in, 32)
                keep(0, 0)
                keep(1, 1)

                def body(n, u, i):
                    ac.wait_ge(biased_ready, n + 1)
                    after(ac, h_turned, n - 1)
                    ac.activation(hid[:, u, :], biased[:, u, :], ACT.Gelu).then_inc(hidden_ready, 1)
                    keep(n + 2, u)
                slot_loop(ac, body)

            @block.vector
            def _(dv):
                dv.wait_ge(k.weights_in, 64 * NE)

                def add_first(n, u):
                    e = expert_at(dv, n)
                    dv.wait_ge(hidden_psum, n + 1)
                    after(dv, hidden_ready, n - 1)
                    dv.tensor_tensor(biased[:, u:u + 1, :], pH[u].unsqueeze(1), b1[:, bass.ds(e, 1), :], ALU.add).then_inc(biased_ready, 1)

                def add_second(n, u, i):
                    e = expert_at(dv, n)
                    dv.wait_ge(projected, n + 1)
                    after(dv, stored[u], 16 * i)
                    dv.tensor_tensor(y[:, u:u + 1, :], pO[u].unsqueeze(1), b2[:, bass.ds(e, 1), :], ALU.add).then_inc(y_ready, 1)

                add_first(0, 0)

                def body(n, u, i):
                    add_first(n + 1, 1 - u)
                    dv.wait_ge(h_turned, n + 1)
                    after(dv, projected, n - 1)
                    dv.tensor_copy(hT[:, u, :, :], pR[u][:, :, :]).then_inc(hT_ready, 1)
                    if real(n, 1):
                        add_second(n - 1, 1 - u, i if u else i - 1)
                slot_loop(dv, body)
                add_second(NS - 1, (NS - 1) % 2, NS // 2 - 1)


def combine(nc, k, out):
    DEPTH = 5
    with ExitStack() as ctx:
        sb, ps, sem = scope(nc, ctx, "combine")
        rows = sb("rows", [P, DEPTH, 2, C])
        rows_in = [sem(f"rows_in{u}") for u in range(DEPTH)]
        added, done = sem("added"), sem("done")
        with nc.Block() as block:
            @block.gpsimd
            def _(pool):
                for i in range(NT):
                    after(pool, added, 2 * (i - DEPTH + 1))
                    for n in range(2):
                        at = n * NT + i
                        pool.indirect_dma_start(rows[:, i % DEPTH, n, :], None, k.results,
                                                bass.IndirectOffsetOnAxis(ap=k.slot[:, at:at + 1], axis=0)).then_inc(rows_in[i % DEPTH], 16)

            @block.vector
            def _(dv):
                for i in range(NT):
                    dv.wait_ge(rows_in[i % DEPTH], 32 * (i // DEPTH + 1))
                    for n in range(2):
                        after(dv, added, 2 * i + n)
                        dv.scalar_tensor_tensor(out=k.x[:, i, :], in0=rows[:, i % DEPTH, n, :], scalar=k.gates[:, n, i:i + 1],
                                                in1=k.x[:, i, :], op0=ALU.mult, op1=ALU.add).then_inc(added, 1)

            @block.sync
            def _(sp):
                def part(lo, hi):
                    sp.wait_ge(added, 2 * hi)
                    sp.dma_start(out[lo * P:hi * P, :].rearrange("(t p) c -> p t c", p=P), k.x[:, lo:hi, :]).then_inc(done, 16)
                part(0, FULL // 2)
                part(FULL // 2, FULL)
                sp.wait_ge(added, 2 * NT)
                sp.dma_start(out[FULL * P:NODES, :], k.x[0:LAST, FULL, :]).then_inc(done, 16)
                sp.wait_ge(done, 48)


def program(nc, a, out):
    k = Core()
    k.nc = nc
    with ExitStack() as ctx:
        sb, ps, sem = scope(nc, ctx, "kept")
        k.x = sb("x", [P, NT, C])
        k.ident = sb("ident", [P, P])
        k.lane = sb("lane", [P, P])
        k.ones = sb("ones", [P, P])
        k.power = sb("power", [P, 64])
        k.share = sb("share", [P, NT])
        k.src_pad = nc.dram_tensor("src_pad", (EROWS, EW), I32).ap()
        k.dst_pad = nc.dram_tensor("dst_pad", (EROWS, EW), I32).ap()
        k.win_dram = nc.dram_tensor("win_dram", (BLK, PB), I32).ap()
        k.kv_table = nc.dram_tensor("kv_table", (ROWS, 2 * C), F32).ap()
        k.mix_qkv = nc.dram_tensor("mix_qkv", (ROWS, 3 * C), F32).ap()
        k.slots = nc.dram_tensor("slots", (NSX * P, C), F32).ap()
        k.results = nc.dram_tensor("results", (NS * P, C), F32).ap()
        k.z_table = nc.dram_tensor("z_table", (ROWS, C), F32).ap()
        k.es_table1 = nc.dram_tensor("es_table1", (ROWS, H1), F32).ap()
        k.es_table2 = nc.dram_tensor("es_table2", (ROWS, 1), F32).ap()
        k.scores1, k.most1 = [nc.dram_tensor(name, (EROWS, EW * H1), F32).ap() for name in ("scores1", "most1")]
        k.scores2, k.most2 = [nc.dram_tensor(name, (EROWS, EW), F32).ap() for name in ("scores2", "most2")]
        with ExitStack() as edges:
            sb, ps, sem = scope(nc, edges, "edges")
            k.xn = sb("xn", [P, NT, C])
            k.sums = sb("sums", [P, NT, SW])
            k.src = sb("src", [P, NPX * SUB], I32)
            k.rel = sb("rel", [P, NPX * SUB])
            k.win = sb("win", [1, NPX], I32)
            k.tile_i = sb("tile_i", [PB, BLK], I32)
            prepare(nc, k, a)
            with ExitStack() as first:
                sb, ps, sem = scope(nc, first, "first")
                k.node = sb("node", [P, NT, C])
                project_first(nc, k, a)
                attend_first(nc, k)
            with ExitStack() as mixing:
                sb, ps, sem = scope(nc, mixing, "mixing")
                k.mixed = sb("mixed", [P, FCH, SW])
                mix_keys(nc, k, a)
                mix_queries(nc, k, a)
            with ExitStack() as weights:
                sb, ps, sem = scope(nc, weights, "first_experts")
                k.w_hidden, k.w_deep, k.w_out = [sb(name, [P, NE, KC, C]) for name in ("w_hidden", "w_deep", "w_out")]
                k.expert_in = [sem(f"expert_in{e}") for e in range(NE)]
                layer_first(nc, k, a)
                experts(nc, k, a)
            sb, ps, sem = scope(nc, edges, "second")
            k.ed = sb("ed", [P, NT, H1])
            k.odds = sb("odds", [P, NP * SUB, H1])
            project_second(nc, k, a)
            edge_odds(nc, k, a, H1, k.es_table1, k.ed, k.scores1, k.most1, True)
            edge_sums(nc, k, H1, k.z_table)
            between_second(nc, k, a)
            edge_odds(nc, k, a, 1, k.es_table2, k.ed, k.scores2, k.most2, False)
            edge_sums(nc, k, 1, k.z_table)
            end_second(nc, k)
        with ExitStack() as ending:
            sb, ps, sem = scope(nc, ending, "ending")
            k.slot = sb("slot", [P, 2 * NT], I32)
            k.gates = sb("gates", [P, 2, NT])
            k.expert = sb("expert", [1, NSX], I32)
            k.w1 = sb("w1", [P, NE * KC, 2 * C])
            k.w2 = sb("w2", [P, NE * 2 * KC, C])
            k.b1 = sb("b1", [P, NE, 2 * C])
            k.b2 = sb("b2", [P, NE, C])
            k.weights_in = sem("weights_in")
            route(nc, k, a)
            slot_experts(nc, k, a)
            combine(nc, k, out)


def layout(v):
    c = np.ascontiguousarray

    def r(b):
        return c(np.reshape(b, (1, -1)))

    def columns(b):
        return c(np.reshape(b, (-1, P)).T)

    def by_expert(b):
        return c(np.reshape(b, (NE, -1, P)).transpose(2, 1, 0).reshape(P, -1))

    mix_w = v["L0_mix_Wqkv"].T
    mix_b = v["L0_mix_bqkv"]
    a1, a2 = v["L1_gnn_a1"], v["L1_gnn_a2"]
    vectors1 = np.zeros((C, 2 * H1), np.float32)
    for h in range(H1):
        vectors1[h * D1:(h + 1) * D1, h] = a1[h, :D1]
        vectors1[h * D1:(h + 1) * D1, H1 + h] = a1[h, D1:]
    w_z = np.reshape(v["L1_gnn_W1"], (C, C))
    w_qkv = v["L1_mix_w_qkv"]
    return {
        "x": c(v["x"]), "src": c(v["src"]), "dst": c(v["dst"]),
        "w_z1": c(w_z.T), "w_natural1": c(w_z), "vectors1": vectors1,
        "w_z2": c(v["L1_gnn_W2"].T), "w_natural2": c(v["L1_gnn_W2"]), "vectors2": c(np.stack([a2[:C], a2[C:]], axis=1)),
        "w_mixkv": c(w_qkv[:, HM * DM:]), "w_mixq": c(w_qkv[:, :HM * DM].T), "w_mixout": c(v["L1_mix_w_out"]),
        "b_mixout": r(v["L1_mix_b_out"]),
        "w_first": c(np.concatenate([v["L0_gnn_Wk"].T, v["L0_gnn_Wv"].T, v["L0_gnn_Wq"].T, mix_w[:, C:2 * C],
                                     mix_w[:, 2 * C:], mix_w[:, :C]], axis=1)),
        "b_first": r(np.concatenate([v["L0_gnn_bk"], v["L0_gnn_bv"], v["L0_gnn_bq"], mix_b[C:2 * C], mix_b[2 * C:],
                                     mix_b[:C]])),
        "w_mixproj": c(v["L0_mix_Wproj"].T), "b_mixproj": r(v["L0_mix_bproj"]), "temperature": r(v["L0_mix_temperature"]),
        "w_p": c(v["L0_gnn_Wp"].T), "b_p": r(v["L0_gnn_bp"]), "w_1": c(v["L0_gnn_W1"].T), "w_2": c(v["L0_gnn_W2"].T),
        "b_1": columns(v["L0_gnn_b1"]), "b_2": r(v["L0_gnn_b2"]), "ln_g": columns(v["L0_gnn_ln_g"]),
        "ln_b": columns(v["L0_gnn_ln_b"]),
        "w_r1": c(v["L0_ffn_Wr"]), "b_r1": r(v["L0_ffn_br"]), "b_o1": c(v["L0_ffn_bo"]), "w_hidden1": c(v["L0_ffn_W1"]),
        "w_deep": c(v["L0_ffn_W2"]), "w_out1": c(v["L0_ffn_Wo"]),
        "bn": c(np.stack([np.stack([by_expert(v["L0_ffn_" + name + str(n)]) for name in ("g", "be", "m", "v", "b")], axis=1)
                          for n in (1, 2)], axis=1)),
        "w_r2": c(v["L1_ffn_Wr"]), "b_r2": r(v["L1_ffn_br"]), "b_o2": c(v["L1_ffn_b2"]), "w_hidden2": c(v["L1_ffn_W1"]),
        "w_out2": c(v["L1_ffn_W2"]), "b_h2": c(v["L1_ffn_b1"]), "gamma": columns(v["L1_ffn_gamma"]),
        "beta": columns(v["L1_ffn_beta"]),
    }


def kernel(**inputs):
    import concourse.bacc as bacc
    from concourse.bass_utils import run_bass_kernel_spmd

    arrays = layout({name: np.asarray(value) for name, value in inputs.items()})
    nc = bacc.Bacc("TRN2", target_bir_lowering=False, num_devices=1)
    parts = {name: nc.dram_tensor(f"in_{name}_dram", a.shape, mybir.dt.from_np(a.dtype), kind="ExternalInput").ap()
             for name, a in arrays.items()}
    out = nc.dram_tensor("out_0_dram", (NODES, C), F32, kind="ExternalOutput").ap()
    program(nc, parts, out)
    ran = run_bass_kernel_spmd(nc, [{f"in_{name}_dram": a for name, a in arrays.items()}], core_ids=[0])
    return ran.results[0]["out_0_dram"]
```
